# Optimizing a Trainium2 kernel written in Bass

```python
import numpy as np
import jax
import jax.numpy as jnp

def _softmax(x, axis=-1):
    return jax.nn.softmax(x, axis=axis)

def _gelu(x):
    return jax.nn.gelu(x, approximate=True)

def _silu(x):
    return jax.nn.silu(x)

def _sigmoid(x):
    return jax.nn.sigmoid(x)

def _layernorm(x, axis=-1, eps=1e-05):
    m = jnp.mean(x, axis=axis, keepdims=True)
    v = jnp.var(x, axis=axis, keepdims=True)
    return (x - m) / jnp.sqrt(v + eps)

def _scatter_add(tgt, idx, src, axis=0):
    return tgt.at[idx].add(src)

def _segment_sum(src, seg, n):
    return jax.ops.segment_sum(src, seg, n)
kernel_name = 'mk_seq_postln_d2_jaxref_r8_8baa2c'

def setup_inputs(seed: int=0):
    np.random.seed(seed)
    _w = jnp.asarray

    def _L0_attn_setup():
        import jax, jax.numpy as jnp
        import numpy as np
        from jax import lax
        D_MODEL = 128
        D_STATE = 16
        D_CONV = 4
        EXPAND = 2
        D_INNER = EXPAND * D_MODEL
        DT_RANK = (D_MODEL + 15) // 16
        BATCH, LENGTH = (2, 128)
        DT_MIN, DT_MAX = (0.001, 0.1)

        def silu(v):
            return v * jax.nn.sigmoid(v)
        key = jax.random.key(seed)
        ks = jax.random.split(key, 8)
        s = lambda n: 1.0 / np.sqrt(n)
        x = jax.random.normal(ks[0], (BATCH, LENGTH, D_MODEL), jnp.float32)
        W_in = jax.random.normal(ks[1], (2 * D_INNER, D_MODEL), jnp.float32) * s(D_MODEL)
        W_conv = jax.random.normal(ks[2], (D_INNER, 1, D_CONV), jnp.float32) * s(D_CONV)
        W_xproj = jax.random.normal(ks[3], (DT_RANK + 2 * D_STATE, D_INNER), jnp.float32) * s(D_INNER)
        dt_init_std = DT_RANK ** (-0.5)
        W_dt = jax.random.uniform(ks[4], (D_INNER, DT_RANK), jnp.float32, minval=-dt_init_std, maxval=dt_init_std)
        dt = jnp.exp(jax.random.uniform(ks[5], (D_INNER,), jnp.float32) * (np.log(DT_MAX) - np.log(DT_MIN)) + np.log(DT_MIN))
        dt = jnp.maximum(dt, dt_init_std)
        b_dt = dt + jnp.log(-jnp.expm1(-dt))
        A_log = jnp.log(jnp.broadcast_to(jnp.arange(1, D_STATE + 1, dtype=jnp.float32), (D_INNER, D_STATE)))
        D = jnp.ones((D_INNER,), jnp.float32)
        W_out = jax.random.normal(ks[6], (D_MODEL, D_INNER), jnp.float32) * s(D_INNER)
        return dict(x=x, W_in=W_in, W_conv=W_conv, W_xproj=W_xproj, W_dt=W_dt, b_dt=b_dt, A_log=A_log, D=D, W_out=W_out)
    _L0_attn_in = _L0_attn_setup()

    def _L0_ffn_setup():
        import jax, jax.numpy as jnp
        import numpy as np
        DIM = 128
        DEPTH = 6
        HEADS = 16
        DIM_HEAD = 64
        WINDOW = 32
        INNER = HEADS * DIM_HEAD
        DIM_INNER = int(DIM * 4 * 2 / 3)
        QK_SCALE = 8.0

        def shift_tokens(t):
            a, s = jnp.split(t, 2, -1)
            s = jnp.pad(s, ((0, 0), (1, 0), (0, 0)))[:, :-1]
            return jnp.concatenate([a, s], -1)

        def l2norm(t):
            return t / jnp.maximum(jnp.linalg.norm(t, axis=-1, keepdims=True), 1e-12)

        def rotate_half(x):
            x1, x2 = jnp.split(x, 2, -1)
            return jnp.concatenate([-x2, x1], -1)

        def rotary_tables(n):
            half = jnp.arange(0, DIM_HEAD, 2, dtype=jnp.float32)
            inv_freq = 1.0 / 10000.0 ** (half / DIM_HEAD)
            t = jnp.arange(n, dtype=jnp.float32)
            freqs = t[:, None] * inv_freq[None, :]
            freqs = jnp.concatenate([freqs, freqs], -1)
            base_scale = (half + 0.4 * DIM_HEAD) / (1.4 * DIM_HEAD)
            power = (t - n // 2) / (WINDOW // 2)
            scale = base_scale[None, :] ** power[:, None]
            scale = jnp.concatenate([scale, scale], -1)
            return (freqs, scale)

        def local_attention(q, k, v):
            b, h, n, d = q.shape
            w = WINDOW
            nw = n // w
            bq = q.reshape(b, h, nw, w, d)
            bk = k.reshape(b, h, nw, w, d)
            bv = v.reshape(b, h, nw, w, d)

            def look(t):
                p = jnp.pad(t, ((0, 0), (0, 0), (1, 0), (0, 0), (0, 0)))
                return jnp.concatenate([p[:, :, :nw], p[:, :, 1:]], axis=3)
            bk2, bv2 = (look(bk), look(bv))
            seq = jnp.arange(n).reshape(nw, w)
            seq_p = jnp.pad(seq, ((1, 0), (0, 0)), constant_values=-1)
            jt = jnp.concatenate([seq_p[:nw], seq_p[1:]], axis=1)
            it = seq[:, :, None]
            jb = jt[:, None, :]
            mask = (it < jb) | (it > jb + w) | (jb == -1)
            sim = jnp.einsum('bhwie,bhwje->bhwij', bq, bk2) * QK_SCALE
            sim = jnp.where(mask, -jnp.finfo(sim.dtype).max, sim)
            attn = jax.nn.softmax(sim, -1)
            out = jnp.einsum('bhwij,bhwje->bhwie', attn, bv2)
            return out.reshape(b, h, n, d)

        def attn_layer(x, Wqkv, qs, ksc, Wo):
            b, n, _ = x.shape
            qkv = x @ Wqkv
            q, k, v = jnp.split(qkv, 3, -1)
            sh = lambda t: t.reshape(b, n, HEADS, DIM_HEAD).transpose(0, 2, 1, 3)
            q, k, v = (sh(q), sh(k), sh(v))
            q = l2norm(q) * qs
            k = l2norm(k) * ksc
            freqs, scale = rotary_tables(n)
            cos, sin = (jnp.cos(freqs), jnp.sin(freqs))
            q = q * cos * scale + rotate_half(q) * sin * scale
            inv = 1.0 / scale
            k = k * cos * inv + rotate_half(k) * sin * inv
            out = local_attention(q, k, v)
            out = out.transpose(0, 2, 1, 3).reshape(b, n, INNER)
            return out @ Wo

        def ffn_layer(x, g, bln, W1, b1, W2, b2):
            mu = x.mean(-1, keepdims=True)
            var = ((x - mu) ** 2).mean(-1, keepdims=True)
            xn = (x - mu) / jnp.sqrt(var + 1e-05) * g + bln
            hg = xn @ W1 + b1
            a, gate = jnp.split(hg, 2, -1)
            return a * jax.nn.gelu(gate, approximate=False) @ W2 + b2
        key = jax.random.key(seed)
        ks = jax.random.split(key, 8)
        B, N = (2, 256)
        init = lambda k, shape: jax.random.normal(k, shape, jnp.float32) * 0.02
        return {'x': jax.random.normal(ks[0], (B, N, DIM), jnp.float32), 'Wqkv': init(ks[1], (DEPTH, DIM, 3 * INNER)), 'q_scale': jnp.ones((DEPTH, DIM_HEAD), jnp.float32), 'k_scale': jnp.ones((DEPTH, DIM_HEAD), jnp.float32), 'Wo': init(ks[2], (DEPTH, INNER, DIM)), 'ln_g': jnp.ones((DEPTH, DIM), jnp.float32), 'ln_b': jnp.zeros((DEPTH, DIM), jnp.float32), 'W1': init(ks[3], (DEPTH, DIM, 2 * DIM_INNER)), 'b1': jnp.zeros((DEPTH, 2 * DIM_INNER), jnp.float32), 'W2': init(ks[4], (DEPTH, DIM_INNER, DIM)), 'b2': jnp.zeros((DEPTH, DIM), jnp.float32)}
    _L0_ffn_in = _L0_ffn_setup()

    def _L1_attn_setup():
        import jax, jax.numpy as jnp
        import numpy as np
        HID, INNER, CONV, L, DR = (128, 256, 4, 16, 64)
        B, S = (1, 256)

        def _combine(left, right):
            a1, b1 = left
            a2, b2 = right
            return (a1 * a2, a2 * b1 + b2)
        key = jax.random.key(seed)
        ks = jax.random.split(key, 8)

        def n(k, shape, scale=0.02):
            return jax.random.normal(k, shape, jnp.float32) * scale
        x = jax.random.normal(ks[0], (B, S, HID), jnp.float32)
        W_in = n(ks[1], (HID, 2 * INNER))
        conv_w = n(ks[2], (CONV, 1, INNER), 0.1)
        conv_b = n(ks[3], (INNER,), 0.01)
        W_x = n(ks[4], (INNER, DR + 2 * L))
        W_delta = n(ks[5], (DR, INNER), 0.05)
        b_delta = jnp.zeros((INNER,), jnp.float32)
        A_log = jnp.log(jnp.tile(jnp.arange(1, L + 1, dtype=jnp.float32), (INNER, 1)))
        D = jnp.ones((INNER,), jnp.float32)
        W_out = n(ks[6], (INNER, HID))
        return dict(x=x, W_in=W_in, conv_w=conv_w, conv_b=conv_b, W_x=W_x, W_delta=W_delta, b_delta=b_delta, A_log=A_log, D=D, W_out=W_out)
    _L1_attn_in = _L1_attn_setup()

    def _L1_ffn_setup():
        import jax, jax.numpy as jnp
        import numpy as np
        DIM = 128
        NUM_EXPERTS = 8
        TOP_K = 2
        HIDDEN = int(DIM * 1.5)
        key = jax.random.key(seed)
        k_x, k_r, k_w1, k_w2, k_w3 = jax.random.split(key, 5)
        B, T = (2, 512)
        s_in = 1.0 / np.sqrt(DIM)
        s_h = 1.0 / np.sqrt(HIDDEN)
        return {'x': jax.random.normal(k_x, (B, T, DIM), dtype=jnp.float32), 'Wr': jax.random.uniform(k_r, (DIM, NUM_EXPERTS), minval=-s_in, maxval=s_in, dtype=jnp.float32), 'W1': jax.random.uniform(k_w1, (NUM_EXPERTS, DIM, HIDDEN), minval=-s_in, maxval=s_in, dtype=jnp.float32), 'W2': jax.random.uniform(k_w2, (NUM_EXPERTS, HIDDEN, DIM), minval=-s_h, maxval=s_h, dtype=jnp.float32), 'W3': jax.random.uniform(k_w3, (NUM_EXPERTS, DIM, HIDDEN), minval=-s_in, maxval=s_in, dtype=jnp.float32)}
    _L1_ffn_in = _L1_ffn_setup()
    _d = {'L0_attn_x': _L0_attn_in['x'], 'L0_attn_W_in': _L0_attn_in['W_in'], 'L0_attn_W_conv': _L0_attn_in['W_conv'], 'L0_attn_W_xproj': _L0_attn_in['W_xproj'], 'L0_attn_W_dt': _L0_attn_in['W_dt'], 'L0_attn_b_dt': _L0_attn_in['b_dt'], 'L0_attn_A_log': _L0_attn_in['A_log'], 'L0_attn_D': _L0_attn_in['D'], 'L0_attn_W_out': _L0_attn_in['W_out'], 'L0_ffn_Wqkv': _L0_ffn_in['Wqkv'], 'L0_ffn_q_scale': _L0_ffn_in['q_scale'], 'L0_ffn_k_scale': _L0_ffn_in['k_scale'], 'L0_ffn_Wo': _L0_ffn_in['Wo'], 'L0_ffn_ln_g': _L0_ffn_in['ln_g'], 'L0_ffn_ln_b': _L0_ffn_in['ln_b'], 'L0_ffn_W1': _L0_ffn_in['W1'], 'L0_ffn_b1': _L0_ffn_in['b1'], 'L0_ffn_W2': _L0_ffn_in['W2'], 'L0_ffn_b2': _L0_ffn_in['b2'], 'L1_attn_W_in': _L1_attn_in['W_in'], 'L1_attn_conv_w': _L1_attn_in['conv_w'], 'L1_attn_conv_b': _L1_attn_in['conv_b'], 'L1_attn_W_x': _L1_attn_in['W_x'], 'L1_attn_W_delta': _L1_attn_in['W_delta'], 'L1_attn_b_delta': _L1_attn_in['b_delta'], 'L1_attn_A_log': _L1_attn_in['A_log'], 'L1_attn_D': _L1_attn_in['D'], 'L1_attn_W_out': _L1_attn_in['W_out'], 'L1_ffn_Wr': _L1_ffn_in['Wr'], 'L1_ffn_W1': _L1_ffn_in['W1'], 'L1_ffn_W2': _L1_ffn_in['W2'], 'L1_ffn_W3': _L1_ffn_in['W3']}
    _x0 = _d['L0_attn_x']
    _d['L0_attn_x'] = jax.random.normal(jax.random.fold_in(jax.random.key(seed), 1), (8, 512, 128), dtype=_x0.dtype)
    del _x0
    return _d

def reference(L0_attn_x, L0_attn_W_in, L0_attn_W_conv, L0_attn_W_xproj, L0_attn_W_dt, L0_attn_b_dt, L0_attn_A_log, L0_attn_D, L0_attn_W_out, L0_ffn_Wqkv, L0_ffn_q_scale, L0_ffn_k_scale, L0_ffn_Wo, L0_ffn_ln_g, L0_ffn_ln_b, L0_ffn_W1, L0_ffn_b1, L0_ffn_W2, L0_ffn_b2, L1_attn_W_in, L1_attn_conv_w, L1_attn_conv_b, L1_attn_W_x, L1_attn_W_delta, L1_attn_b_delta, L1_attn_A_log, L1_attn_D, L1_attn_W_out, L1_ffn_Wr, L1_ffn_W1, L1_ffn_W2, L1_ffn_W3):

    def _L0_attn_ref(x, W_in, W_conv, W_xproj, W_dt, b_dt, A_log, D, W_out):
        import jax, jax.numpy as jnp
        import numpy as np
        from jax import lax
        D_MODEL = 128
        D_STATE = 16
        D_CONV = 4
        EXPAND = 2
        D_INNER = EXPAND * D_MODEL
        DT_RANK = (D_MODEL + 15) // 16
        BATCH, LENGTH = (2, 128)
        DT_MIN, DT_MAX = (0.001, 0.1)

        def silu(v):
            return v * jax.nn.sigmoid(v)
        xz = x @ W_in.T
        xc, z = jnp.split(xz, 2, axis=-1)
        xc = lax.conv_general_dilated(xc.transpose(0, 2, 1), W_conv, window_strides=(1,), padding=[(D_CONV - 1, 0)], feature_group_count=D_INNER, dimension_numbers=('NCH', 'OIH', 'NCH')).transpose(0, 2, 1)
        xc = silu(xc)
        dbc = xc @ W_xproj.T
        dlt = dbc[..., :DT_RANK]
        Bm = dbc[..., DT_RANK:DT_RANK + D_STATE]
        Cm = dbc[..., DT_RANK + D_STATE:]
        delta = jax.nn.softplus(dlt @ W_dt.T + b_dt)
        A = -jnp.exp(A_log)
        deltaA = jnp.exp(delta[..., None] * A)
        deltaBx = delta[..., None] * Bm[:, :, None, :] * xc[..., None]

        def step(h, inp):
            dA, dBx, c = inp
            h = dA * h + dBx
            return (h, jnp.einsum('bdn,bn->bd', h, c))
        h0 = jnp.zeros((x.shape[0], D_INNER, D_STATE), xc.dtype)
        _, ys = lax.scan(step, h0, (deltaA.swapaxes(0, 1), deltaBx.swapaxes(0, 1), Cm.swapaxes(0, 1)))
        y = ys.swapaxes(0, 1) + xc * D
        y = y * silu(z)
        return y @ W_out.T

    def _L0_ffn_ref(x, Wqkv, q_scale, k_scale, Wo, ln_g, ln_b, W1, b1, W2, b2):
        import jax, jax.numpy as jnp
        import numpy as np
        DIM = 128
        DEPTH = 6
        HEADS = 16
        DIM_HEAD = 64
        WINDOW = 32
        INNER = HEADS * DIM_HEAD
        DIM_INNER = int(DIM * 4 * 2 / 3)
        QK_SCALE = 8.0

        def shift_tokens(t):
            a, s = jnp.split(t, 2, -1)
            s = jnp.pad(s, ((0, 0), (1, 0), (0, 0)))[:, :-1]
            return jnp.concatenate([a, s], -1)

        def l2norm(t):
            return t / jnp.maximum(jnp.linalg.norm(t, axis=-1, keepdims=True), 1e-12)

        def rotate_half(x):
            x1, x2 = jnp.split(x, 2, -1)
            return jnp.concatenate([-x2, x1], -1)

        def rotary_tables(n):
            half = jnp.arange(0, DIM_HEAD, 2, dtype=jnp.float32)
            inv_freq = 1.0 / 10000.0 ** (half / DIM_HEAD)
            t = jnp.arange(n, dtype=jnp.float32)
            freqs = t[:, None] * inv_freq[None, :]
            freqs = jnp.concatenate([freqs, freqs], -1)
            base_scale = (half + 0.4 * DIM_HEAD) / (1.4 * DIM_HEAD)
            power = (t - n // 2) / (WINDOW // 2)
            scale = base_scale[None, :] ** power[:, None]
            scale = jnp.concatenate([scale, scale], -1)
            return (freqs, scale)

        def local_attention(q, k, v):
            b, h, n, d = q.shape
            w = WINDOW
            nw = n // w
            bq = q.reshape(b, h, nw, w, d)
            bk = k.reshape(b, h, nw, w, d)
            bv = v.reshape(b, h, nw, w, d)

            def look(t):
                p = jnp.pad(t, ((0, 0), (0, 0), (1, 0), (0, 0), (0, 0)))
                return jnp.concatenate([p[:, :, :nw], p[:, :, 1:]], axis=3)
            bk2, bv2 = (look(bk), look(bv))
            seq = jnp.arange(n).reshape(nw, w)
            seq_p = jnp.pad(seq, ((1, 0), (0, 0)), constant_values=-1)
            jt = jnp.concatenate([seq_p[:nw], seq_p[1:]], axis=1)
            it = seq[:, :, None]
            jb = jt[:, None, :]
            mask = (it < jb) | (it > jb + w) | (jb == -1)
            sim = jnp.einsum('bhwie,bhwje->bhwij', bq, bk2) * QK_SCALE
            sim = jnp.where(mask, -jnp.finfo(sim.dtype).max, sim)
            attn = jax.nn.softmax(sim, -1)
            out = jnp.einsum('bhwij,bhwje->bhwie', attn, bv2)
            return out.reshape(b, h, n, d)

        def attn_layer(x, Wqkv, qs, ksc, Wo):
            b, n, _ = x.shape
            qkv = x @ Wqkv
            q, k, v = jnp.split(qkv, 3, -1)
            sh = lambda t: t.reshape(b, n, HEADS, DIM_HEAD).transpose(0, 2, 1, 3)
            q, k, v = (sh(q), sh(k), sh(v))
            q = l2norm(q) * qs
            k = l2norm(k) * ksc
            freqs, scale = rotary_tables(n)
            cos, sin = (jnp.cos(freqs), jnp.sin(freqs))
            q = q * cos * scale + rotate_half(q) * sin * scale
            inv = 1.0 / scale
            k = k * cos * inv + rotate_half(k) * sin * inv
            out = local_attention(q, k, v)
            out = out.transpose(0, 2, 1, 3).reshape(b, n, INNER)
            return out @ Wo

        def ffn_layer(x, g, bln, W1, b1, W2, b2):
            mu = x.mean(-1, keepdims=True)
            var = ((x - mu) ** 2).mean(-1, keepdims=True)
            xn = (x - mu) / jnp.sqrt(var + 1e-05) * g + bln
            hg = xn @ W1 + b1
            a, gate = jnp.split(hg, 2, -1)
            return a * jax.nn.gelu(gate, approximate=False) @ W2 + b2
        for i in range(DEPTH):
            x = attn_layer(shift_tokens(x), Wqkv[i], q_scale[i], k_scale[i], Wo[i]) + x
            x = ffn_layer(shift_tokens(x), ln_g[i], ln_b[i], W1[i], b1[i], W2[i], b2[i]) + x
        return x

    def _L1_attn_ref(x, W_in, conv_w, conv_b, W_x, W_delta, b_delta, A_log, D, W_out):
        import jax, jax.numpy as jnp
        import numpy as np
        HID, INNER, CONV, L, DR = (128, 256, 4, 16, 64)
        B, S = (1, 256)

        def _combine(left, right):
            a1, b1 = left
            a2, b2 = right
            return (a1 * a2, a2 * b1 + b2)
        b, s, _ = x.shape
        xz = x @ W_in
        xi, z = (xz[..., :INNER], xz[..., INNER:])
        xc = jax.lax.conv_general_dilated(xi, conv_w, window_strides=(1,), padding=[(CONV - 1, CONV - 1)], dimension_numbers=('NWC', 'WIO', 'NWC'), feature_group_count=INNER)
        xc = jax.nn.silu(xc[:, :s, :] + conv_b)
        A = -jnp.exp(A_log.astype(jnp.float32))
        Df = D.astype(jnp.float32)
        xp = xc @ W_x
        delta, Bm, Cm = (xp[..., :DR], xp[..., DR:DR + L], xp[..., DR + L:])
        delta = jax.nn.softplus(delta @ W_delta + b_delta)
        deltaA = jnp.exp(jnp.einsum('bsd,dl->bsdl', delta, A))
        deltaBx = jnp.einsum('bsd,bsl,bsd->bsdl', delta, Bm, xc)
        _, h = jax.lax.associative_scan(_combine, (deltaA, deltaBx), axis=1)
        y = jnp.einsum('bsdl,bsl->bsd', h, Cm) + xc * Df
        y = y * jax.nn.silu(z)
        return y @ W_out

    def _L1_ffn_ref(x, Wr, W1, W2, W3):
        import jax, jax.numpy as jnp
        import numpy as np
        DIM = 128
        NUM_EXPERTS = 8
        TOP_K = 2
        HIDDEN = int(DIM * 1.5)
        B, T, C = x.shape
        xf = x.reshape(-1, C)
        gate_logits = xf @ Wr
        w, idx = jax.lax.top_k(gate_logits, TOP_K)
        w = jax.nn.softmax(w, axis=-1)
        comb = jnp.sum(w[:, :, None] * jax.nn.one_hot(idx, NUM_EXPERTS, dtype=w.dtype), axis=1)
        h = jnp.einsum('nc,ech->neh', xf, W1)
        g = jnp.einsum('nc,ech->neh', xf, W3)
        y = jnp.einsum('neh,ehc->nec', jax.nn.silu(h) * g, W2)
        out = jnp.einsum('nec,ne->nc', y, comb)
        return out.reshape(B, T, C)
    x = L0_attn_x
    x = _layernorm(x + _L0_attn_ref(x, L0_attn_W_in, L0_attn_W_conv, L0_attn_W_xproj, L0_attn_W_dt, L0_attn_b_dt, L0_attn_A_log, L0_attn_D, L0_attn_W_out), axis=-1)
    x = _layernorm(x + _L0_ffn_ref(x, L0_ffn_Wqkv, L0_ffn_q_scale, L0_ffn_k_scale, L0_ffn_Wo, L0_ffn_ln_g, L0_ffn_ln_b, L0_ffn_W1, L0_ffn_b1, L0_ffn_W2, L0_ffn_b2), axis=-1)
    x = _layernorm(x + _L1_attn_ref(x, L1_attn_W_in, L1_attn_conv_w, L1_attn_conv_b, L1_attn_W_x, L1_attn_W_delta, L1_attn_b_delta, L1_attn_A_log, L1_attn_D, L1_attn_W_out), axis=-1)
    x = _layernorm(x + _L1_ffn_ref(x, L1_ffn_Wr, L1_ffn_W1, L1_ffn_W2, L1_ffn_W3), axis=-1)
    return x

_drawn_inputs = setup_inputs


def setup_inputs(seed=0):
    import zlib

    import numpy as np

    out = dict(_drawn_inputs(seed))
    spreads = {'L0_attn_b_dt': (-0.8577413558959961, 0.551),
     'L0_attn_D': (1.0, 0.2),
     'L0_ffn_q_scale': (1.0, 0.6),
     'L0_ffn_k_scale': (1.0, 0.6),
     'L0_ffn_ln_g': (1.0, 0.6),
     'L0_ffn_ln_b': (0.0, 0.8),
     'L0_ffn_b1': (0.0, 0.705),
     'L0_ffn_b2': (0.0, 0.1),
     'L1_attn_b_delta': (0.0, 0.8),
     'L1_attn_D': (1.0, 0.6)}
    factors = {'L0_ffn_W1': 3.302,
     'L0_ffn_W2': 3.236,
     'L1_attn_W_in': 8.0,
     'L1_attn_conv_w': 8.0,
     'L1_attn_conv_b': 8.0,
     'L1_attn_W_x': 8.0,
     'L1_attn_W_delta': 8.0,
     'L1_attn_A_log': 8.0,
     'L1_attn_W_out': 8.0}
    for name, (base, spread) in spreads.items():
        noise = np.random.default_rng([zlib.crc32(name.encode()), seed]).standard_normal(out[name].shape)
        drawn = base * np.exp(spread * noise) if base else spread * noise
        out[name] = jnp.asarray(drawn.astype(out[name].dtype))
    for name, factor in factors.items():
        out[name] = (out[name] * factor).astype(out[name].dtype)
    return out
```

```python
import math
from contextlib import ExitStack

import concourse.bass as bass
from concourse import mybir

F32 = mybir.dt.float32
BF16 = mybir.dt.bfloat16
U32 = mybir.dt.uint32
ALU = mybir.AluOpType
ACT = mybir.ActivationFunctionType
AX = mybir.AxisListType
EXP_LN_SET = "natural_log_exp_and_others"

P = 128
SEQS = 8
T = 512
EPS = 1e-5


class Counter:

    def __init__(self, ctx, nc, name, per):
        self.sem = ctx.enter_context(nc.semaphore(name))
        self.per = per

    def at(self, it, k):
        return it * self.per + k


class Memory:

    def __init__(self, ctx, nc, prefix):
        self.ctx, self.nc, self.prefix = ctx, nc, prefix

    def sb(self, name, shape, dt=F32):
        return self.ctx.enter_context(self.nc.sbuf_tensor(self.prefix + name, shape, dt))

    def bank(self, name):
        return self.ctx.enter_context(self.nc.psum_tensor(self.prefix + name, [P, 512], F32))

    def counter(self, name, per=1):
        return Counter(self.ctx, self.nc, self.prefix + name, per)


def state_space_phase(nc, prefix, signals, turn, xT, x_dram, const, w):
    NSTATE = 16
    HALVES = 2
    TAPS = 4
    R = w["w_dt"].shape[0]
    with ExitStack() as ctx:
        m = Memory(ctx, nc, prefix)
        w_in = m.sb("w_in", [P, 4 * P])
        pick = m.sb("pick", [2 * NSTATE, 2 * NSTATE, P])
        w_bc = m.sb("w_bc", [P, HALVES, 2 * NSTATE])
        w_dlt = m.sb("w_dlt", [P, HALVES, R])
        w_dt = m.sb("w_dt", [R, HALVES * P])
        w_out = m.sb("w_out", [P, HALVES, P])
        chan = m.sb("chan", [P, HALVES, TAPS + 3])
        a_log = m.sb("a_log", [P, HALVES, NSTATE])
        a_exp = m.sb("a_exp", [P, HALVES, NSTATE])
        decay = m.sb("decay", [P, HALVES, NSTATE])
        xpad = m.sb("xpad", [P, HALVES, TAPS - 1 + T])
        conv = m.sb("conv", [P, HALVES, T])
        ex = m.sb("ex", [P, HALVES, T])
        rx = m.sb("rx", [P, HALVES, T])
        xc = m.sb("xc", [P, HALVES, T])
        ez = m.sb("ez", [P, HALVES, T])
        rz = m.sb("rz", [P, HALVES, T])
        zs = m.sb("zs", [P, HALVES, T])
        bc = m.sb("bc", [2 * NSTATE, T])
        dlt = m.sb("dlt", [R, T])
        mag = m.sb("mag", [P, HALVES, T])
        em = m.sb("em", [P, HALVES, T])
        lg = m.sb("lg", [P, HALVES, T])
        onep = m.sb("onep", [P, HALVES, T])
        dm = m.sb("dm", [P, HALVES, T])
        pos = m.sb("pos", [P, HALVES, T])
        delta = m.sb("delta", [P, HALVES, T])
        u = m.sb("u", [P, HALVES, T])
        csb = m.sb("csb", [P, 2, T])
        dA = m.sb("dA", [P, 2, HALVES, T])
        dBx = m.sb("dBx", [P, 2, HALVES, T])
        h = m.sb("h", [P, 2, HALVES, T])
        hc = m.sb("hc", [P, 2, HALVES, T])
        y = m.sb("y", [P, HALVES, T])
        yz = m.sb("yz", [P, HALVES, T])
        res = m.sb("res", [P, T])
        cen = m.sb("cen", [P, T])
        sq = m.sb("sq", [P, T])
        lv = m.sb("lv", [P, T])
        rstd = m.sb("rstd", [P, T])
        bank = [m.bank(f"bank{i}") for i in range(8)]

        loaded = signals("loaded")
        x_loaded = signals("x_loaded")
        zero_pad = signals("zero_pad")
        a_ready = signals("a_ready")
        xz_ready = signals("xz_ready", 4)
        xpad_ready = signals("xpad_ready", 2)
        tap_done = signals("tap_done", TAPS * HALVES)
        ez_ready = signals("ez_ready", 2)
        rz_ready = signals("rz_ready", 4)
        zs_ready = signals("zs_ready", 2)
        ex_ready = signals("ex_ready", 2)
        rx_ready = signals("rx_ready", 4)
        xc_ready = signals("xc_ready", 2)
        bc_ps = signals("bc_ps")
        dlt_ps = signals("dlt_ps")
        bc_ready = signals("bc_ready")
        dlt_ready = signals("dlt_ready")
        dt_ready = signals("dt_ready", 2)
        mag_ready = signals("mag_ready", 2)
        em_ready = signals("em_ready", 2)
        lg_ready = signals("lg_ready", 2)
        dm_steps = signals("dm_steps", 5 * HALVES)
        pos_ready = signals("pos_ready", 2)
        rdm_ready = signals("rdm_ready", 2)
        delta_ready = signals("delta_ready", 2)
        u_ready = signals("u_ready", 2)
        b_ready = signals("b_ready", NSTATE)
        c_ready = signals("c_ready", NSTATE)
        c_copied = signals("c_copied", NSTATE)
        dA_ready = signals("dA_ready", NSTATE * HALVES)
        dBx_ready = signals("dBx_ready", NSTATE * HALVES)
        h_ready = signals("h_ready", NSTATE * HALVES)
        hc_ready = signals("hc_ready", NSTATE * HALVES)
        hc_used = signals("hc_used", NSTATE * HALVES)
        y_summed = signals("y_summed", 2)
        y_ready = signals("y_ready", 2)
        yz_ready = signals("yz_ready", 2)
        out_ps = signals("out_ps")
        res_ready = signals("res_ready")
        mean_ready = signals("mean_ready")
        cen_ready = signals("cen_ready")
        sq_ready = signals("sq_ready")
        var_ready = signals("var_ready")
        lv_ready = signals("lv_ready")
        rstd_ready = signals("rstd_ready")
        x_written = signals("x_written")

        block = ctx.enter_context(nc.Block())
        N_LOADS = 8

        def tokens(b):
            return bass.ds((b - turn * SEQS) * T if turn else b * T, T)

        @block.sync
        def _(sp):
            if x_dram is not None:
                sp.dma_start(xT[:, :], x_dram).then_inc(x_loaded.sem, 16)
            sp.dma_start(pick[:, :, :], w["pick"]).then_inc(loaded.sem, 16)
            sp.dma_start(w_in[:, :], w["w_in"]).then_inc(loaded.sem, 16)
            sp.dma_start(w_bc[:, :, :], w["w_bc"]).then_inc(loaded.sem, 16)
            sp.dma_start(w_dlt[:, :, :], w["w_dlt"]).then_inc(loaded.sem, 16)
            sp.dma_start(w_dt[:, :], w["w_dt"]).then_inc(loaded.sem, 16)
            sp.dma_start(w_out[:, :, :], w["w_out"]).then_inc(loaded.sem, 16)
            sp.dma_start(chan[:, :, :], w["chan"]).then_inc(loaded.sem, 16)
            sp.dma_start(a_log[:, :, :], w["a_log"]).then_inc(loaded.sem, 16)
            sp.wait_ge(loaded.sem, 16 * N_LOADS * (turn + 1))

        @block.tensor
        def _(pe):
            pe.wait_ge(loaded.sem, 16 * N_LOADS * (turn + 1))
            if x_dram is not None:
                pe.wait_ge(x_loaded.sem, 16)
            with pe.Fori(turn * SEQS, (turn + 1) * SEQS) as b:
                pe.wait_ge(x_written.sem, x_written.at(b, 1))
                for i in range(4):
                    pe.matmul(bank[i][:, :], w_in[:, i * P:(i + 1) * P], xT[:, tokens(b)],
                              start=True, stop=True).then_inc(xz_ready.sem, 1)
                pe.wait_ge(xc_ready.sem, xc_ready.at(b, 2))
                for c in range(HALVES):
                    mm = pe.matmul(bank[4][0:2 * NSTATE, :], w_bc[:, c, :], xc[:, c, :],
                                   start=(c == 0), stop=(c == 1))
                mm.then_inc(bc_ps.sem, 1)
                for c in range(HALVES):
                    mm = pe.matmul(bank[5][0:R, :], w_dlt[:, c, :], xc[:, c, :],
                                   start=(c == 0), stop=(c == 1))
                mm.then_inc(dlt_ps.sem, 1)
                pe.wait_ge(dlt_ready.sem, dlt_ready.at(b, 1))
                for c in range(HALVES):
                    pe.matmul(bank[6 + c][:, :], w_dt[:, c * P:(c + 1) * P], dlt[:, :],
                              start=True, stop=True).then_inc(dt_ready.sem, 1)
                pe.wait_ge(bc_ready.sem, bc_ready.at(b, 1))
                pe.wait_ge(xpad_ready.sem, xpad_ready.at(b, 2))
                pe.wait_ge(zs_ready.sem, zs_ready.at(b, 2))

                def accumulate(n):
                    for c in range(HALVES):
                        k = n * HALVES + c
                        pe.wait_ge(hc_ready.sem, hc_ready.at(b, k + 1))
                        mm = pe.matmul(bank[4 + c][:, :], const["ident"][:, :], hc[:, n % 2, c, :],
                                       start=(n == 0), stop=(n == NSTATE - 1))
                        mm.then_inc(hc_used.sem, 1)

                for n in range(NSTATE):
                    if n >= 2:
                        pe.wait_ge(dBx_ready.sem, dBx_ready.at(b, (n - 1) * HALVES))
                    pe.matmul(bank[n % 2][:, :], pick[:, n, :], bc[:, :],
                              start=True, stop=True).then_inc(b_ready.sem, 1)
                    if n >= 2:
                        pe.wait_ge(c_copied.sem, c_copied.at(b, n - 1))
                    pe.matmul(bank[2 + n % 2][:, :], pick[:, NSTATE + n, :], bc[:, :],
                              start=True, stop=True).then_inc(c_ready.sem, 1)
                    if n >= 1:
                        accumulate(n - 1)
                accumulate(NSTATE - 1)
                pe.wait_ge(yz_ready.sem, yz_ready.at(b, 2))
                for c in range(HALVES):
                    mm = pe.matmul(bank[6][:, :], w_out[:, c, :], yz[:, c, :],
                                   start=(c == 0), stop=(c == 1))
                mm.then_inc(out_ps.sem, 1)
                pe.wait_ge(res_ready.sem, res_ready.at(b, 1))
                pe.matmul(bank[7][:, :], const["mean"][:, :], res[:, :],
                          start=True, stop=True).then_inc(mean_ready.sem, 1)
                pe.wait_ge(sq_ready.sem, sq_ready.at(b, 1))
                pe.matmul(bank[6][:, :], const["mean"][:, :], sq[:, :],
                          start=True, stop=True).then_inc(var_ready.sem, 1)

        @block.scalar
        def _(act):
            act.preload_act_table_set(EXP_LN_SET)
            act.wait_ge(loaded.sem, 16 * N_LOADS * (turn + 1))
            act.activation(a_exp[:, :, :], a_log[:, :, :], ACT.Exp).then_inc(a_ready.sem, 1)
            act.wait_ge(a_ready.sem, 2 * turn + 2)
            act.wait_ge(zero_pad.sem, turn + 1)
            with act.Fori(turn * SEQS, (turn + 1) * SEQS) as b:
                act.preload_act_table_set(EXP_LN_SET)
                for c in range(HALVES):
                    act.wait_ge(xz_ready.sem, xz_ready.at(b, c + 1))
                    act.activation(xpad[:, c, TAPS - 1:], bank[c][:, :], ACT.Copy).then_inc(xpad_ready.sem, 1)
                for c in range(HALVES):
                    act.wait_ge(xz_ready.sem, xz_ready.at(b, 3 + c))
                    act.activation(ez[:, c, :], bank[2 + c][:, :], ACT.Exp, scale=-1.0).then_inc(ez_ready.sem, 1)
                for c in range(HALVES):
                    act.wait_ge(tap_done.sem, tap_done.at(b, HALVES * (TAPS - 1) + c + 1))
                    act.activation(ex[:, c, :], conv[:, c, :], ACT.Exp, scale=-1.0).then_inc(ex_ready.sem, 1)
                act.wait_ge(dlt_ps.sem, dlt_ps.at(b, 1))
                act.activation(dlt[:, :], bank[5][0:R, :], ACT.Copy).then_inc(dlt_ready.sem, 1)
                act.wait_ge(bc_ps.sem, bc_ps.at(b, 1))
                act.activation(bc[:, :], bank[4][0:2 * NSTATE, :], ACT.Copy).then_inc(bc_ready.sem, 1)
                for c in range(HALVES):
                    act.wait_ge(dt_ready.sem, dt_ready.at(b, c + 1))
                    act.activation(mag[:, c, :], bank[6 + c][:, :], ACT.Abs,
                                   bias=chan[:, c, TAPS + 1:TAPS + 2]).then_inc(mag_ready.sem, 1)
                for c in range(HALVES):
                    act.wait_ge(mag_ready.sem, mag_ready.at(b, c + 1))
                    act.activation(em[:, c, :], mag[:, c, :], ACT.Exp, scale=-1.0).then_inc(em_ready.sem, 1)
                for c in range(HALVES):
                    act.wait_ge(dm_steps.sem, dm_steps.at(b, c + 1))
                    act.activation(lg[:, c, :], onep[:, c, :], ACT.Ln).then_inc(lg_ready.sem, 1)
                act.wait_ge(delta_ready.sem, delta_ready.at(b, 2))
                for n in range(NSTATE):
                    act.wait_ge(c_ready.sem, c_ready.at(b, n + 1))
                    if n >= 2:
                        act.wait_ge(hc_ready.sem, hc_ready.at(b, (n - 1) * HALVES))
                    act.activation(csb[:, n % 2, :], bank[2 + n % 2][:, :], ACT.Copy).then_inc(c_copied.sem, 1)
                    for c in range(HALVES):
                        if n >= 2:
                            act.wait_ge(h_ready.sem, h_ready.at(b, (n - 2) * HALVES + c + 1))
                        act.activation(dA[:, n % 2, c, :], delta[:, c, :], ACT.Exp,
                                       scale=decay[:, c, n:n + 1]).then_inc(dA_ready.sem, 1)
                act.wait_ge(var_ready.sem, var_ready.at(b, 1))
                act.activation(lv[:, :], bank[6][:, :], ACT.Ln, bias=const["eps"][:, 0:1]).then_inc(lv_ready.sem, 1)
                act.wait_ge(lv_ready.sem, lv_ready.at(b, 1))
                act.activation(rstd[:, :], lv[:, :], ACT.Exp, scale=-0.5).then_inc(rstd_ready.sem, 1)

        @block.vector
        def _(ve):
            ve.memset(xpad[:, :, 0:TAPS - 1], 0.0).then_inc(zero_pad.sem, 1)
            ve.wait_ge(a_ready.sem, 2 * turn + 1)
            ve.tensor_scalar(decay[:, :, :], a_exp[:, :, :], -1.0, None, ALU.mult).then_inc(a_ready.sem, 1)
            if turn == 0:
                ve.sem_inc(x_written.sem, 1)
            with ve.Fori(turn * SEQS, (turn + 1) * SEQS) as b:
                for j in range(TAPS):
                    for c in range(HALVES):
                        src = xpad[:, c, j:j + T]
                        tap = chan[:, c, j:j + 1]
                        if j == 0:
                            ve.wait_ge(xpad_ready.sem, xpad_ready.at(b, c + 1))
                            ve.tensor_scalar(conv[:, c, :], src, tap, chan[:, c, TAPS:TAPS + 1],
                                             ALU.mult, ALU.add).then_inc(tap_done.sem, 1)
                        elif j < TAPS - 1:
                            ve.wait_ge(tap_done.sem, tap_done.at(b, HALVES * (j - 1) + c + 1))
                            ve.scalar_tensor_tensor(out=conv[:, c, :], in0=src, scalar=tap, in1=conv[:, c, :],
                                                    op0=ALU.mult, op1=ALU.add).then_inc(tap_done.sem, 1)
                for c in range(HALVES):
                    ve.wait_ge(tap_done.sem, tap_done.at(b, HALVES * (TAPS - 1)))
                    ve.scalar_tensor_tensor(out=conv[:, c, :], in0=xpad[:, c, TAPS - 1:TAPS - 1 + T],
                                            scalar=chan[:, c, TAPS - 1:TAPS], in1=conv[:, c, :],
                                            op0=ALU.mult, op1=ALU.add).then_inc(tap_done.sem, 1)
                for c in range(HALVES):
                    ve.wait_ge(ez_ready.sem, ez_ready.at(b, c + 1))
                    ve.tensor_scalar(ez[:, c, :], ez[:, c, :], 1.0, None, ALU.add).then_inc(rz_ready.sem, 1)
                for c in range(HALVES):
                    ve.wait_ge(rz_ready.sem, rz_ready.at(b, c + 1))
                    ve.reciprocal(rz[:, c, :], ez[:, c, :]).then_inc(rz_ready.sem, 1)
                for c in range(HALVES):
                    ve.wait_ge(rz_ready.sem, rz_ready.at(b, 3 + c))
                    ve.tensor_tensor(zs[:, c, :], bank[2 + c][:, :], rz[:, c, :], ALU.mult).then_inc(zs_ready.sem, 1)
                for c in range(HALVES):
                    ve.wait_ge(ex_ready.sem, ex_ready.at(b, c + 1))
                    ve.tensor_scalar(ex[:, c, :], ex[:, c, :], 1.0, None, ALU.add).then_inc(rx_ready.sem, 1)
                for c in range(HALVES):
                    ve.wait_ge(rx_ready.sem, rx_ready.at(b, c + 1))
                    ve.reciprocal(rx[:, c, :], ex[:, c, :]).then_inc(rx_ready.sem, 1)
                for c in range(HALVES):
                    ve.wait_ge(rx_ready.sem, rx_ready.at(b, 3 + c))
                    ve.tensor_tensor(xc[:, c, :], conv[:, c, :], rx[:, c, :], ALU.mult).then_inc(xc_ready.sem, 1)
                for c in range(HALVES):
                    ve.wait_ge(mag_ready.sem, mag_ready.at(b, c + 1))
                    ve.tensor_scalar(pos[:, c, :], bank[6 + c][:, :], chan[:, c, TAPS + 1:TAPS + 2], 0.0,
                                     ALU.add, ALU.max).then_inc(pos_ready.sem, 1)
                for c in range(HALVES):
                    ve.wait_ge(em_ready.sem, em_ready.at(b, c + 1))
                    ve.tensor_scalar(onep[:, c, :], em[:, c, :], 1.0, None, ALU.add).then_inc(dm_steps.sem, 1)
                for c in range(HALVES):
                    ve.wait_ge(dm_steps.sem, dm_steps.at(b, c + 1))
                    ve.tensor_scalar(dm[:, c, :], onep[:, c, :], 1.0, 1e-30,
                                     ALU.subtract, ALU.max).then_inc(dm_steps.sem, 1)
                for c in range(HALVES):
                    ve.wait_ge(dm_steps.sem, dm_steps.at(b, 3 + c))
                    ve.reciprocal(dm[:, c, :], dm[:, c, :]).then_inc(dm_steps.sem, 1)
                for c in range(HALVES):
                    ve.wait_ge(dm_steps.sem, dm_steps.at(b, 5 + c))
                    ve.wait_ge(lg_ready.sem, lg_ready.at(b, c + 1))
                    ve.scalar_tensor_tensor(out=dm[:, c, :], in0=lg[:, c, :], scalar=1e-30, in1=dm[:, c, :],
                                            op0=ALU.max, op1=ALU.mult).then_inc(dm_steps.sem, 1)
                for c in range(HALVES):
                    ve.wait_ge(dm_steps.sem, dm_steps.at(b, 7 + c))
                    ve.scalar_tensor_tensor(out=dm[:, c, :], in0=dm[:, c, :], scalar=1.0, in1=em[:, c, :],
                                            op0=ALU.min, op1=ALU.mult).then_inc(dm_steps.sem, 1)
                for c in range(HALVES):
                    ve.wait_ge(dm_steps.sem, dm_steps.at(b, 9 + c))
                    ve.wait_ge(pos_ready.sem, pos_ready.at(b, c + 1))
                    ve.tensor_tensor(delta[:, c, :], dm[:, c, :], pos[:, c, :], ALU.add).then_inc(delta_ready.sem, 1)
                for c in range(HALVES):
                    ve.wait_ge(delta_ready.sem, delta_ready.at(b, c + 1))
                    ve.wait_ge(xc_ready.sem, xc_ready.at(b, c + 1))
                    ve.tensor_tensor(u[:, c, :], delta[:, c, :], xc[:, c, :], ALU.mult).then_inc(u_ready.sem, 1)
                ve.wait_ge(u_ready.sem, u_ready.at(b, 2))
                for n in range(NSTATE):
                    ve.wait_ge(b_ready.sem, b_ready.at(b, n + 1))
                    for c in range(HALVES):
                        if n >= 2:
                            ve.wait_ge(h_ready.sem, h_ready.at(b, (n - 2) * HALVES + c + 1))
                        ve.tensor_tensor(dBx[:, n % 2, c, :], u[:, c, :], bank[n % 2][:, :],
                                         ALU.mult).then_inc(dBx_ready.sem, 1)
                    for c in range(HALVES):
                        k = n * HALVES + c
                        ve.wait_ge(dBx_ready.sem, dBx_ready.at(b, k + 1))
                        ve.wait_ge(dA_ready.sem, dA_ready.at(b, k + 1))
                        if n >= 2:
                            ve.wait_ge(hc_ready.sem, hc_ready.at(b, (n - 2) * HALVES + c + 1))
                        ve.tensor_tensor_scan(h[:, n % 2, c, :], dA[:, n % 2, c, :], dBx[:, n % 2, c, :], 0.0,
                                              ALU.mult, ALU.add).then_inc(h_ready.sem, 1)
                for c in range(HALVES):
                    ve.wait_ge(hc_used.sem, hc_used.at(b, NSTATE * HALVES))
                    ve.scalar_tensor_tensor(out=y[:, c, :], in0=xc[:, c, :], scalar=chan[:, c, TAPS + 2:TAPS + 3],
                                            in1=bank[4 + c][:, :], op0=ALU.mult, op1=ALU.add)\
                      .then_inc(y_ready.sem, 1)
                for c in range(HALVES):
                    ve.wait_ge(y_ready.sem, y_ready.at(b, c + 1))
                    ve.wait_ge(zs_ready.sem, zs_ready.at(b, c + 1))
                    ve.tensor_tensor(yz[:, c, :], y[:, c, :], zs[:, c, :], ALU.mult).then_inc(yz_ready.sem, 1)
                ve.wait_ge(out_ps.sem, out_ps.at(b, 1))
                ve.tensor_tensor(res[:, :], bank[6][:, :], xT[:, tokens(b)], ALU.add).then_inc(res_ready.sem, 1)
                ve.wait_ge(res_ready.sem, res_ready.at(b, 1))
                ve.wait_ge(mean_ready.sem, mean_ready.at(b, 1))
                ve.tensor_tensor(cen[:, :], res[:, :], bank[7][:, :], ALU.subtract).then_inc(cen_ready.sem, 1)
                ve.wait_ge(cen_ready.sem, cen_ready.at(b, 1))
                ve.tensor_tensor(sq[:, :], cen[:, :], cen[:, :], ALU.mult).then_inc(sq_ready.sem, 1)
                ve.wait_ge(rstd_ready.sem, rstd_ready.at(b, 1))
                ve.tensor_tensor(xT[:, tokens(b)], cen[:, :], rstd[:, :], ALU.mult).then_inc(x_written.sem, 1)

        @block.gpsimd
        def _(pool):
            with pool.Fori(turn * SEQS, (turn + 1) * SEQS) as b:
                for n in range(NSTATE):
                    pool.wait_ge(c_copied.sem, c_copied.at(b, n + 1))
                    for c in range(HALVES):
                        k = n * HALVES + c
                        pool.wait_ge(h_ready.sem, h_ready.at(b, k + 1))
                        if n >= 2:
                            pool.wait_ge(hc_used.sem, hc_used.at(b, (n - 2) * HALVES + c + 1))
                        pool.tensor_tensor(hc[:, n % 2, c, :], h[:, n % 2, c, :], csb[:, n % 2, :],
                                           ALU.mult).then_inc(hc_ready.sem, 1)


def local_attention_phase(nc, prefix, xT, x0T, const, w):
    DEPTH = 6
    PAIRS = 8
    HD = 64
    QB = 64
    KB = 96
    LOOK = KB - QB
    NB = T // QB
    HALF = NB // 2
    TILES = 2 * PAIRS
    INNER = PAIRS * P
    HID = w["w2"].shape[1]
    HT = 3
    HR = [HID, HID, 341 - 2 * HID]
    QK_SCALE = 8.0
    NORM_SHIFT = 2.0 ** 30
    with ExitStack() as ctx:
        m = Memory(ctx, nc, prefix)
        w_qkv = m.sb("w_qkv", [P, 3 * INNER])
        w_rot = m.sb("w_rot", [P, 2 * INNER])
        w_o = m.sb("w_o", [P, PAIRS, P])
        w_1 = m.sb("w_1", [P, 2 * 341])
        w_2 = m.sb("w_2", [HID, HT, P])
        chan = m.sb("chan", [P, 13])
        base = m.sb("base", [P, 4, T])
        table = m.sb("table", [P, 4, T])
        mask = m.sb("mask", [P, 2, HALF * KB])
        xs = m.sb("xs", [P, LOOK + T])
        vals = m.sb("vals", [KB, NB, INNER])
        sq = m.sb("sq", [P, 2, T])
        t1 = m.sb("t1", [P, 2, T])
        t2 = m.sb("t2", [P, 2, T])
        nrm = m.sb("nrm", [P, 2, T])
        lnn = m.sb("lnn", [P, 2, T])
        rn = m.sb("rn", [P, 2, T])
        qT = m.sb("qT", [P, 2, T])
        kT = m.sb("kT", [P, 2, LOOK + T])
        sc = m.sb("sc", [P, 2, HALF * KB])
        mx = m.sb("mx", [P, 2, HALF])
        pr = m.sb("pr", [P, 2, HALF * KB])
        den = m.sb("den", [P, 2, HALF])
        rden = m.sb("rden", [P, 2, HALF])
        pn = m.sb("pn", [P, 2, HALF * KB])
        pT = m.sb("pT", [KB, 2, HALF * P])
        oT = m.sb("oT", [P, PAIRS, T])
        fs = m.sb("fs", [P, T])
        cen = m.sb("cen", [P, T])
        csq = m.sb("csq", [P, T])
        lv = m.sb("lv", [P, T])
        rstd = m.sb("rstd", [P, T])
        xn = m.sb("xn", [P, T])
        hid = m.sb("hid", [HID, HT, T])
        bank = [m.bank(f"bank{i}") for i in range(8)]

        fixed_loaded = m.counter("fixed_loaded")
        zeroed = m.counter("zeroed")
        w_loaded = m.counter("w_loaded")
        rot_weights = m.counter("rot_weights", 4)
        tables_ready = m.counter("tables_ready", 4)
        shifted = m.counter("shifted", 2)
        v_ready = m.counter("v_ready", 2 * NB)
        v_copied = m.counter("v_copied", 2 * NB)
        rt_ready = m.counter("rt_ready", TILES)
        sq_ready = m.counter("sq_ready", TILES)
        t_ready = m.counter("t_ready", 2 * TILES)
        n_ready = m.counter("n_ready", TILES)
        guarded = m.counter("guarded", TILES)
        ln_ready = m.counter("ln_ready", TILES)
        rn_ready = m.counter("rn_ready", TILES)
        added = m.counter("added", TILES)
        rotated = m.counter("rotated", TILES)
        s_ready = m.counter("s_ready", TILES)
        masked = m.counter("masked", TILES)
        mx_ready = m.counter("mx_ready", TILES)
        sub_ready = m.counter("sub_ready", TILES)
        exp_ready = m.counter("exp_ready", TILES)
        den_ready = m.counter("den_ready", TILES)
        rden_ready = m.counter("rden_ready", TILES)
        p_ready = m.counter("p_ready", TILES)
        pt_ready = m.counter("pt_ready", TILES)
        pt_copied = m.counter("pt_copied", TILES)
        pv_done = m.counter("pv_done", TILES)
        o_copied = m.counter("o_copied", PAIRS)
        wo_done = m.counter("wo_done")
        x1_ready = m.counter("x1_ready")
        fs_ready = m.counter("fs_ready", 2)
        mean_ready = m.counter("mean_ready")
        cen_ready = m.counter("cen_ready")
        csq_ready = m.counter("csq_ready")
        var_ready = m.counter("var_ready")
        lv_ready = m.counter("lv_ready")
        rstd_ready = m.counter("rstd_ready")
        xh_ready = m.counter("xh_ready")
        xn_ready = m.counter("xn_ready")
        up_ready = m.counter("up_ready", 2 * HT)
        gate_ready = m.counter("gate_ready", HT)
        hid_ready = m.counter("hid_ready", HT)
        down_ready = m.counter("down_ready")
        x_done = m.counter("x_done")

        block = ctx.enter_context(nc.Block())
        N_FIXED, N_LAYER = 2, 5

        def tokens(b):
            return bass.ds(b * T, T)

        @block.sync
        def _(sp):
            sp.dma_start(base[:, :, :], w["tables"]).then_inc(fixed_loaded.sem, 16)
            sp.dma_start(mask[:, :, :], w["mask"]).then_inc(fixed_loaded.sem, 16)
            with sp.Fori(0, DEPTH) as l:
                sp.wait_ge(x_done.sem, l * SEQS + 1)
                sp.dma_start(w_qkv[:, :], w["w_qkv"][bass.ds(l, 1), :, :].rearrange("a p n -> p (a n)"))\
                  .then_inc(w_loaded.sem, 16)
                sp.dma_start(chan[:, :], w["chan"][bass.ds(l, 1), :, :].rearrange("a p n -> p (a n)"))\
                  .then_inc(w_loaded.sem, 16)
                sp.dma_start(w_o[:, :, :], w["w_o"][bass.ds(l, 1), :, :, :].rearrange("a p k n -> p (a k) n"))\
                  .then_inc(w_loaded.sem, 16)
                sp.dma_start(w_1[:, :], w["w1"][bass.ds(l, 1), :, :].rearrange("a p n -> p (a n)"))\
                  .then_inc(w_loaded.sem, 16)
                sp.dma_start(w_2[:, :, :], w["w2"][bass.ds(l, 1), :, :, :].rearrange("a p k n -> p (a k) n"))\
                  .then_inc(w_loaded.sem, 16)
            sp.wait_ge(w_loaded.sem, 16 * N_LAYER * DEPTH)

        @block.tensor
        def _(pe):
            def values(it):
                pe.wait_ge(shifted.sem, shifted.at(it, 2))
                for t in range(NB):
                    for f in range(2):
                        k = 2 * t + f
                        if k >= 4:
                            pe.wait_ge(v_copied.sem, v_copied.at(it, k - 3))
                        pe.matmul(bank[k % 4][0:KB, :], xs[:, t * QB:t * QB + KB],
                                  w_qkv[:, 2 * INNER + f * 512:2 * INNER + (f + 1) * 512],
                                  start=True, stop=True).then_inc(v_ready.sem, 1)

            def project(it, p, j):
                k = 2 * p + j
                if p == 0:
                    pe.wait_ge(v_copied.sem, v_copied.at(it, 2 * NB))
                else:
                    pe.wait_ge(t_ready.sem, t_ready.at(it, 2 * (k - 1)))
                col = j * INNER + p * P
                pe.matmul(bank[2 * j][:, :], w_qkv[:, col:col + P], xs[:, LOOK:], start=True, stop=True)
                pe.matmul(bank[2 * j + 1][:, :], w_rot[:, col:col + P], xs[:, LOOK:],
                          start=True, stop=True).then_inc(rt_ready.sem, 1)

            def norm(it, p, j):
                k = 2 * p + j
                pe.wait_ge(sq_ready.sem, sq_ready.at(it, k + 1))
                if k >= 1:
                    pe.wait_ge(guarded.sem, guarded.at(it, k))
                pe.matmul(bank[4][:, :], const["heads"][:, :], sq[:, j, :],
                          start=True, stop=True).then_inc(n_ready.sem, 1)

            def scores(it, p, f):
                g = 2 * p + f
                if f == 0:
                    pe.wait_ge(rotated.sem, rotated.at(it, 2 * p + 2))
                if g >= 1:
                    pe.wait_ge(masked.sem, masked.at(it, g))
                pe.nop(nofuse=True)
                for i in range(HALF):
                    t = HALF * f + i
                    for a in range(2):
                        r = slice(a * HD, (a + 1) * HD)
                        mm = pe.matmul(bank[5][r, i * KB:(i + 1) * KB], qT[r, p % 2, t * QB:(t + 1) * QB],
                                       kT[r, p % 2, t * QB:t * QB + KB], start=True, stop=True,
                                       skip_group_check=True)
                mm.then_inc(s_ready.sem, 1)

            def turn(it, p, f):
                g = 2 * p + f
                pe.wait_ge(p_ready.sem, p_ready.at(it, g + 1))
                if g >= 1:
                    pe.wait_ge(pt_copied.sem, pt_copied.at(it, g))
                for i in range(HALF):
                    mm = pe.transpose(bank[6][0:KB, i * P:(i + 1) * P], pn[:, f, i * KB:(i + 1) * KB],
                                      const["ident"][:, :])
                mm.then_inc(pt_ready.sem, 1)

            def mix(it, p, f):
                g = 2 * p + f
                pe.wait_ge(pt_copied.sem, pt_copied.at(it, g + 1))
                if f == 0 and p >= 1:
                    pe.wait_ge(o_copied.sem, o_copied.at(it, p))
                pe.nop(nofuse=True)
                for i in range(HALF):
                    t = HALF * f + i
                    for a in range(2):
                        mm = pe.matmul(bank[7][a * HD:(a + 1) * HD, t * QB:(t + 1) * QB],
                                       vals[:, t, (2 * p + a) * HD:(2 * p + a + 1) * HD],
                                       pT[:, f, i * P + a * QB:i * P + (a + 1) * QB],
                                       start=True, stop=True, skip_group_check=True)
                mm.then_inc(pv_done.sem, 1)

            def feed_forward(it):
                pe.wait_ge(o_copied.sem, o_copied.at(it, PAIRS))
                pe.wait_ge(guarded.sem, guarded.at(it, TILES))
                for p in range(PAIRS):
                    mm = pe.matmul(bank[4][:, :], w_o[:, p, :], oT[:, p, :], start=(p == 0), stop=(p == PAIRS - 1))
                mm.then_inc(wo_done.sem, 1)
                pe.wait_ge(fs_ready.sem, fs_ready.at(it, 2))
                pe.wait_ge(masked.sem, masked.at(it, TILES))
                pe.matmul(bank[5][:, :], const["mean"][:, :], fs[:, :], start=True, stop=True)\
                  .then_inc(mean_ready.sem, 1)
                pe.wait_ge(csq_ready.sem, csq_ready.at(it, 1))
                pe.matmul(bank[6][:, :], const["mean"][:, :], csq[:, :], start=True, stop=True)\
                  .then_inc(var_ready.sem, 1)
                pe.wait_ge(xn_ready.sem, xn_ready.at(it, 1))
                for i in range(2 * HT):
                    c = (i // HT) * 341 + (i % HT) * HID
                    pe.matmul(bank[i][0:HR[i % HT], :], w_1[:, c:c + HR[i % HT]], xn[:, :],
                              start=True, stop=True).then_inc(up_ready.sem, 1)
                for i in range(HT):
                    pe.wait_ge(hid_ready.sem, hid_ready.at(it, i + 1))
                    mm = pe.matmul(bank[7][:, :], w_2[0:HR[i], i, :], hid[0:HR[i], i, :],
                                   start=(i == 0), stop=(i == HT - 1))
                mm.then_inc(down_ready.sem, 1)

            with pe.Fori(0, DEPTH) as l:
                pe.wait_ge(w_loaded.sem, (l + 1) * (16 * N_LAYER))
                pe.wait_ge(rot_weights.sem, rot_weights.at(l, 4))
                pe.nop(nofuse=True)
                with pe.Fori(0, SEQS) as b:
                    it = l * SEQS + b
                    pe.wait_ge(x_done.sem, it + 1)
                    values(it)
                    for p in range(PAIRS + 2):
                        if p >= 2:
                            turn(it, p - 2, 0)
                        if p < PAIRS:
                            project(it, p, 0)
                        if p >= 2:
                            mix(it, p - 2, 0)
                            turn(it, p - 2, 1)
                        if p < PAIRS:
                            project(it, p, 1)
                        if p >= 2:
                            mix(it, p - 2, 1)
                        if 1 <= p <= PAIRS:
                            scores(it, p - 1, 0)
                        if p < PAIRS:
                            norm(it, p, 0)
                            norm(it, p, 1)
                        if 1 <= p <= PAIRS:
                            scores(it, p - 1, 1)
                    feed_forward(it)

        @block.scalar
        def _(act):
            def square(it, p, j):
                k = 2 * p + j
                act.wait_ge(rt_ready.sem, rt_ready.at(it, k + 1))
                if p >= 1:
                    act.wait_ge(n_ready.sem, n_ready.at(it, k - 1))
                act.activation(sq[:, j, :], bank[2 * j][:, :], ACT.Square).then_inc(sq_ready.sem, 1)

            def inverse_norm(it, p, j):
                k = 2 * p + j
                act.wait_ge(guarded.sem, guarded.at(it, k + 1))
                act.activation(lnn[:, j, :], nrm[:, j, :], ACT.Ln, scale=NORM_SHIFT).then_inc(ln_ready.sem, 1)
                act.wait_ge(ln_ready.sem, ln_ready.at(it, k + 1))
                if p >= 1:
                    act.wait_ge(rotated.sem, rotated.at(it, k - 1))
                act.activation(rn[:, j, :], lnn[:, j, :], ACT.Exp, scale=-0.5,
                               bias=const["unshift"][:, 0:1]).then_inc(rn_ready.sem, 1)

            def exponential(it, p, f):
                g = 2 * p + f
                act.wait_ge(sub_ready.sem, sub_ready.at(it, g + 1))
                if p >= 1:
                    act.wait_ge(p_ready.sem, p_ready.at(it, g - 1))
                act.activation(pr[:, f, :], sc[:, f, :], ACT.Exp, scale=QK_SCALE).then_inc(exp_ready.sem, 1)

            def copy_turned(it, p, f):
                g = 2 * p + f
                act.wait_ge(pt_ready.sem, pt_ready.at(it, g + 1))
                if p >= 1:
                    act.wait_ge(pv_done.sem, pv_done.at(it, g - 1))
                act.activation(pT[:, f, :], bank[6][0:KB, :], ACT.Copy).then_inc(pt_copied.sem, 1)

            act.wait_ge(zeroed.sem, 7)
            with act.Fori(0, DEPTH) as l:
                with act.Fori(0, SEQS) as b:
                    it = l * SEQS + b
                    act.preload_act_table_set(EXP_LN_SET)
                    for k in range(2 * NB):
                        act.wait_ge(v_ready.sem, v_ready.at(it, k + 1))
                        act.activation(vals[:, k // 2, (k % 2) * 512:(k % 2 + 1) * 512], bank[k % 4][0:KB, :],
                                       ACT.Copy).then_inc(v_copied.sem, 1)
                    for p in range(PAIRS + 2):
                        if p >= 2:
                            copy_turned(it, p - 2, 0)
                        if p < PAIRS:
                            square(it, p, 0)
                        if p >= 2:
                            copy_turned(it, p - 2, 1)
                        if p < PAIRS:
                            square(it, p, 1)
                        if p >= 2:
                            act.wait_ge(pv_done.sem, pv_done.at(it, 2 * (p - 2) + 2))
                            act.activation(oT[:, p - 2, :], bank[7][:, :], ACT.Copy).then_inc(o_copied.sem, 1)
                        if 1 <= p <= PAIRS:
                            exponential(it, p - 1, 0)
                        if p < PAIRS:
                            inverse_norm(it, p, 0)
                            inverse_norm(it, p, 1)
                        if 1 <= p <= PAIRS:
                            exponential(it, p - 1, 1)
                    act.wait_ge(cen_ready.sem, cen_ready.at(it, 1))
                    act.activation(csq[:, :], cen[:, :], ACT.Square).then_inc(csq_ready.sem, 1)
                    act.wait_ge(var_ready.sem, var_ready.at(it, 1))
                    act.activation(lv[:, :], bank[6][:, :], ACT.Ln, bias=const["eps"][:, 0:1]).then_inc(lv_ready.sem, 1)
                    act.wait_ge(lv_ready.sem, lv_ready.at(it, 1))
                    act.activation(rstd[:, :], lv[:, :], ACT.Exp, scale=-0.5).then_inc(rstd_ready.sem, 1)
                    for i in range(HT):
                        r = slice(0, HR[i])
                        act.wait_ge(up_ready.sem, up_ready.at(it, HT + i + 1))
                        act.activation(hid[r, i, :], bank[HT + i][r, :], ACT.Gelu,
                                       bias=chan[r, 10 + i:11 + i]).then_inc(gate_ready.sem, 1)

        @block.vector
        def _(ve):
            def rotate(it, p, j):
                k = 2 * p + j
                ve.wait_ge(sq_ready.sem, sq_ready.at(it, k + 1))
                if p >= 1:
                    ve.wait_ge(rotated.sem, rotated.at(it, k - 1))
                ve.tensor_tensor(t1[:, j, :], bank[2 * j][:, :], table[:, 2 * j, :], ALU.mult).then_inc(t_ready.sem, 1)
                ve.tensor_tensor(t2[:, j, :], bank[2 * j + 1][:, :], table[:, 2 * j + 1, :],
                                 ALU.mult).then_inc(t_ready.sem, 1)

            def guard(it, p, j):
                k = 2 * p + j
                ve.wait_ge(n_ready.sem, n_ready.at(it, k + 1))
                if p >= 1:
                    ve.wait_ge(ln_ready.sem, ln_ready.at(it, k - 1))
                ve.tensor_scalar(nrm[:, j, :], bank[4][:, :], 1e-24, None, ALU.max).then_inc(guarded.sem, 1)

            def center(it, p, f):
                g = 2 * p + f
                sc3 = sc[:, f, :].rearrange("p (i k) -> p i k", k=KB)
                ve.wait_ge(s_ready.sem, s_ready.at(it, g + 1))
                if p >= 1:
                    ve.wait_ge(exp_ready.sem, exp_ready.at(it, g - 1))
                ve.tensor_tensor(sc[:, f, :], bank[5][:, 0:HALF * KB], mask[:, f, :], ALU.add).then_inc(masked.sem, 1)
                ve.wait_ge(masked.sem, masked.at(it, g + 1))
                ve.tensor_reduce(mx[:, f, :], sc3, AX.X, ALU.max).then_inc(mx_ready.sem, 1)
                ve.wait_ge(mx_ready.sem, mx_ready.at(it, g + 1))
                ve.tensor_tensor(sc3, sc3, mx[:, f, :].unsqueeze(2).to_broadcast([P, HALF, KB]),
                                 ALU.subtract).then_inc(sub_ready.sem, 1)

            def denominator(it, p, f):
                g = 2 * p + f
                ve.wait_ge(exp_ready.sem, exp_ready.at(it, g + 1))
                ve.tensor_reduce(den[:, f, :], pr[:, f, :].rearrange("p (i k) -> p i k", k=KB), AX.X,
                                 ALU.add).then_inc(den_ready.sem, 1)
                ve.wait_ge(den_ready.sem, den_ready.at(it, g + 1))
                if p >= 1:
                    ve.wait_ge(p_ready.sem, p_ready.at(it, g - 1))
                ve.reciprocal(rden[:, f, :], den[:, f, :]).then_inc(rden_ready.sem, 1)

            ve.memset(xs[:, 0:LOOK], 0.0).then_inc(zeroed.sem, 1)
            ve.memset(xs[HD:P, LOOK:LOOK + 1], 0.0).then_inc(zeroed.sem, 1)
            ve.memset(fs[HD:P, 0:1], 0.0).then_inc(zeroed.sem, 1)
            ve.memset(kT[:, :, 0:LOOK], 0.0).then_inc(zeroed.sem, 1)
            ve.tensor_copy(x0T[:, :], xT[:, :]).then_inc(zeroed.sem, 1)
            ve.wait_ge(zeroed.sem, 5)
            ve.sem_inc(zeroed.sem, 2)
            ve.sem_inc(x_done.sem, 1)
            with ve.Fori(0, DEPTH) as l:
                ve.wait_ge(w_loaded.sem, (l + 1) * (16 * N_LAYER))
                ve.wait_ge(tables_ready.sem, tables_ready.at(l, 4))
                ve.nop(nofuse=True)
                with ve.Fori(0, SEQS) as b:
                    it = l * SEQS + b
                    ve.wait_ge(x_done.sem, it + 1)
                    ve.nop(nofuse=True)
                    ve.tensor_copy(xs[0:HD, LOOK:], xT[0:HD, tokens(b)]).then_inc(shifted.sem, 1)
                    ve.tensor_copy(xs[HD:P, LOOK + 1:], xT[HD:P, bass.ds(b * T, T - 1)]).then_inc(shifted.sem, 1)
                    for p in range(PAIRS + 1):
                        if p < PAIRS:
                            rotate(it, p, 0)
                            rotate(it, p, 1)
                        if 1 <= p:
                            center(it, p - 1, 0)
                        if p < PAIRS:
                            guard(it, p, 0)
                            guard(it, p, 1)
                        if 1 <= p:
                            center(it, p - 1, 1)
                            denominator(it, p - 1, 0)
                            denominator(it, p - 1, 1)
                    ve.wait_ge(wo_done.sem, wo_done.at(it, 1))
                    ve.tensor_tensor(xT[:, tokens(b)], bank[4][:, :], xT[:, tokens(b)], ALU.add).then_inc(x1_ready.sem, 1)
                    ve.wait_ge(x1_ready.sem, x1_ready.at(it, 1))
                    ve.nop(nofuse=True)
                    ve.tensor_copy(fs[0:HD, :], xT[0:HD, tokens(b)]).then_inc(fs_ready.sem, 1)
                    ve.tensor_copy(fs[HD:P, 1:], xT[HD:P, bass.ds(b * T, T - 1)]).then_inc(fs_ready.sem, 1)
                    ve.wait_ge(fs_ready.sem, fs_ready.at(it, 2))
                    ve.wait_ge(mean_ready.sem, mean_ready.at(it, 1))
                    ve.tensor_tensor(cen[:, :], fs[:, :], bank[5][:, :], ALU.subtract).then_inc(cen_ready.sem, 1)
                    ve.wait_ge(rstd_ready.sem, rstd_ready.at(it, 1))
                    ve.tensor_tensor(xn[:, :], cen[:, :], rstd[:, :], ALU.mult).then_inc(xh_ready.sem, 1)
                    ve.wait_ge(xh_ready.sem, xh_ready.at(it, 1))
                    ve.tensor_scalar(xn[:, :], xn[:, :], chan[:, 4:5], chan[:, 5:6], ALU.mult, ALU.add)\
                      .then_inc(xn_ready.sem, 1)
                    for i in range(HT):
                        r = slice(0, HR[i])
                        ve.wait_ge(gate_ready.sem, gate_ready.at(it, i + 1))
                        ve.scalar_tensor_tensor(out=hid[r, i, :], in0=bank[i][r, :], scalar=chan[r, 7 + i:8 + i],
                                                in1=hid[r, i, :], op0=ALU.add, op1=ALU.mult)\
                          .then_inc(hid_ready.sem, 1)
                    ve.wait_ge(down_ready.sem, down_ready.at(it, 1))
                    ve.scalar_tensor_tensor(out=xT[:, tokens(b)], in0=bank[7][:, :], scalar=chan[:, 6:7],
                                            in1=xT[:, tokens(b)], op0=ALU.add, op1=ALU.add).then_inc(x_done.sem, 1)

        @block.gpsimd
        def _(pool):
            def join(it, p, j):
                k = 2 * p + j
                pool.wait_ge(t_ready.sem, t_ready.at(it, 2 * k + 2))
                pool.tensor_tensor(t1[:, j, :], t1[:, j, :], t2[:, j, :], ALU.add).then_inc(added.sem, 1)

            def normalise(it, p, j):
                k = 2 * p + j
                pool.wait_ge(rn_ready.sem, rn_ready.at(it, k + 1))
                pool.wait_ge(added.sem, added.at(it, k + 1))
                if p >= 2:
                    pool.wait_ge(s_ready.sem, s_ready.at(it, 2 * (p - 2) + 2))
                dst = kT[:, p % 2, LOOK:] if j else qT[:, p % 2, :]
                pool.tensor_tensor(dst, t1[:, j, :], rn[:, j, :], ALU.mult).then_inc(rotated.sem, 1)

            def probabilities(it, p, f):
                g = 2 * p + f
                pool.wait_ge(rden_ready.sem, rden_ready.at(it, g + 1))
                if p >= 1:
                    pool.wait_ge(pt_ready.sem, pt_ready.at(it, g - 1))
                pool.tensor_tensor(pn[:, f, :].rearrange("p (i k) -> p i k", k=KB),
                                   pr[:, f, :].rearrange("p (i k) -> p i k", k=KB),
                                   rden[:, f, :].unsqueeze(2).to_broadcast([P, HALF, KB]),
                                   ALU.mult).then_inc(p_ready.sem, 1)

            pool.wait_ge(zeroed.sem, 7)
            pool.wait_ge(fixed_loaded.sem, 16 * N_FIXED)
            with pool.Fori(0, DEPTH) as l:
                pool.wait_ge(w_loaded.sem, (l + 1) * (16 * N_LAYER))
                pool.nop(nofuse=True)
                src = w_qkv[:, 0:2 * INNER].rearrange("p (h s c) -> p h s c", s=2, c=HD // 2)
                dst = w_rot[:, :].rearrange("p (h s c) -> p h s c", s=2, c=HD // 2)
                for s in range(2):
                    for j in range(2):
                        h = slice(j * PAIRS * 2, (j + 1) * PAIRS * 2)
                        pool.tensor_copy(dst[:, h, s, :], src[:, h, 1 - s, :]).then_inc(rot_weights.sem, 1)
                for i in range(4):
                    pool.tensor_scalar(table[:, i, :], base[:, i, :], chan[:, i:i + 1], None,
                                       ALU.mult).then_inc(tables_ready.sem, 1)
                with pool.Fori(0, SEQS) as b:
                    it = l * SEQS + b
                    for p in range(PAIRS + 1):
                        if p < PAIRS:
                            join(it, p, 0)
                            join(it, p, 1)
                            normalise(it, p, 0)
                            normalise(it, p, 1)
                        if 1 <= p:
                            probabilities(it, p - 1, 0)
                            probabilities(it, p - 1, 1)


def layer_norm_phase(nc, prefix, xT, x0T, const):
    with ExitStack() as ctx:
        m = Memory(ctx, nc, prefix)
        res = m.sb("res", [P, T])
        cen = m.sb("cen", [P, T])
        sq = m.sb("sq", [P, T])
        lv = m.sb("lv", [P, T])
        rstd = m.sb("rstd", [P, T])
        bank = [m.bank(f"bank{i}") for i in range(2)]
        res_ready, mean_ready, cen_ready = m.counter("res_ready"), m.counter("mean_ready"), m.counter("cen_ready")
        sq_ready, var_ready, lv_ready = m.counter("sq_ready"), m.counter("var_ready"), m.counter("lv_ready")
        rstd_ready, x_written = m.counter("rstd_ready"), m.counter("x_written")
        block = ctx.enter_context(nc.Block())

        @block.tensor
        def _(pe):
            with pe.Fori(0, SEQS) as b:
                pe.wait_ge(res_ready.sem, b + 1)
                pe.matmul(bank[0][:, :], const["mean"][:, :], res[:, :], start=True, stop=True).then_inc(mean_ready.sem, 1)
                pe.wait_ge(sq_ready.sem, b + 1)
                pe.matmul(bank[1][:, :], const["mean"][:, :], sq[:, :], start=True, stop=True).then_inc(var_ready.sem, 1)

        @block.scalar
        def _(act):
            with act.Fori(0, SEQS) as b:
                act.preload_act_table_set(EXP_LN_SET)
                act.wait_ge(cen_ready.sem, b + 1)
                act.activation(sq[:, :], cen[:, :], ACT.Square).then_inc(sq_ready.sem, 1)
                act.wait_ge(var_ready.sem, b + 1)
                act.activation(lv[:, :], bank[1][:, :], ACT.Ln, bias=const["eps"][:, 0:1]).then_inc(lv_ready.sem, 1)
                act.wait_ge(lv_ready.sem, b + 1)
                act.activation(rstd[:, :], lv[:, :], ACT.Exp, scale=-0.5).then_inc(rstd_ready.sem, 1)

        @block.vector
        def _(ve):
            with ve.Fori(0, SEQS) as b:
                x = xT[:, bass.ds(b * T, T)]
                ve.tensor_tensor(res[:, :], x, x0T[:, bass.ds(b * T, T)], ALU.add).then_inc(res_ready.sem, 1)
                ve.wait_ge(res_ready.sem, b + 1)
                ve.wait_ge(mean_ready.sem, b + 1)
                ve.tensor_tensor(cen[:, :], res[:, :], bank[0][:, :], ALU.subtract).then_inc(cen_ready.sem, 1)
                ve.wait_ge(cen_ready.sem, b + 1)
                ve.wait_ge(rstd_ready.sem, b + 1)
                ve.tensor_tensor(x, cen[:, :], rstd[:, :], ALU.mult).then_inc(x_written.sem, 1)



def expert_phase(nc, prefix, xT, const, w, out):
    EXPERTS = 8
    ET = 12
    TB = T // P
    with ExitStack() as ctx:
        m = Memory(ctx, nc, prefix)
        wr = m.sb("wr", [P, EXPERTS])
        w1 = m.sb("w1", [P, ET * P])
        w3 = m.sb("w3", [P, ET * P])
        w2 = m.sb("w2", [P, ET, P])
        owner = m.sb("owner", [72, ET, P], BF16)
        part = m.sb("part", [P, 2])
        iota = m.sb("iota", [P, EXPERTS])
        xm = m.sb("xm", [P, T])
        logit = m.sb("logit", [P, TB, EXPERTS])
        top = m.sb("top", [P, TB, 8])
        topi = m.sb("topi", [P, TB, 8], U32)
        topf = m.sb("topf", [P, TB, 8])
        gap = m.sb("gap", [P, TB])
        eg = m.sb("eg", [P, TB])
        sg = m.sb("sg", [P, TB])
        wt = m.sb("wt", [P, 2, TB])
        first = m.sb("first", [P, TB, EXPERTS])
        second = m.sb("second", [P, TB, EXPERTS])
        comb3 = m.sb("comb3", [P, TB, 96])
        part_a = m.sb("part_a", [72, T], BF16)
        rest_a = m.sb("rest_a", [72, T])
        part_b = m.sb("part_b", [72, T], BF16)
        combT = m.sb("combT", [72, T], BF16)
        act_h = m.sb("act_h", [P, 2, T])
        prod = m.sb("prod", [P, 2, T])
        hid = m.sb("hid", [P, 2, T])
        res = m.sb("res", [P, T])
        cen = m.sb("cen", [P, T])
        sq = m.sb("sq", [P, T])
        lv = m.sb("lv", [P, T])
        rstd = m.sb("rstd", [P, T])
        fin = m.sb("fin", [P, T])
        bank = [m.bank(f"bank{i}") for i in range(8)]

        loaded = m.counter("loaded")
        comb_zeroed = m.counter("comb_zeroed")
        xm_ready = m.counter("xm_ready")
        logits_ready = m.counter("logits_ready")
        logit_copied = m.counter("logit_copied")
        top_ready = m.counter("top_ready", TB)
        topi_ready = m.counter("topi_ready", TB)
        gap_ready = m.counter("gap_ready", 2)
        eg_ready = m.counter("eg_ready")
        wt_steps = m.counter("wt_steps", 3)
        chosen = m.counter("chosen", 2 * TB)
        comb_ready = m.counter("comb_ready", 3)
        comb_turned = m.counter("comb_turned")
        split_steps = m.counter("split_steps", 4)
        h_ready = m.counter("h_ready", ET)
        g_ready = m.counter("g_ready", ET)
        cb_ready = m.counter("cb_ready", ET)
        silu_ready = m.counter("silu_ready", ET)
        prod_ready = m.counter("prod_ready", ET)
        hid_ready = m.counter("hid_ready", ET)
        hid_used = m.counter("hid_used", ET)
        res_ready = m.counter("res_ready")
        mean_ready = m.counter("mean_ready")
        cen_ready = m.counter("cen_ready")
        sq_ready = m.counter("sq_ready")
        var_ready = m.counter("var_ready")
        lv_ready = m.counter("lv_ready")
        rstd_ready = m.counter("rstd_ready")
        fin_ready = m.counter("fin_ready")
        stored = m.counter("stored")

        block = ctx.enter_context(nc.Block())
        N_LOADS = 7

        @block.sync
        def _(sp):
            for dst, name in ((wr, "wr"), (w1, "w1"), (w3, "w3"), (part, "part"), (iota, "iota")):
                sp.dma_start(dst[:, :], w[name]).then_inc(loaded.sem, 16)
            for dst, name in ((w2, "w2"), (owner, "owner")):
                sp.dma_start(dst[:, :, :], w[name]).then_inc(loaded.sem, 16)
            with sp.Fori(0, SEQS) as b:
                sp.wait_ge(fin_ready.sem, b + 1)
                sp.dma_start(out[:, bass.ds(b * T, T)], fin[:, :]).then_inc(stored.sem, 16)
            sp.wait_ge(loaded.sem, 16 * N_LOADS)
            sp.wait_ge(stored.sem, 16 * SEQS + 1)

        @block.tensor
        def _(pe):
            pe.wait_ge(loaded.sem, 16 * N_LOADS)
            with pe.Fori(0, SEQS) as b:
                pe.wait_ge(xm_ready.sem, b + 1)
                for t in range(TB):
                    mm = pe.matmul(bank[7][:, t * EXPERTS:(t + 1) * EXPERTS], xm[:, t * P:(t + 1) * P], wr[:, :],
                                   start=True, stop=True, skip_group_check=True)
                mm.then_inc(logits_ready.sem, 1)
                pe.wait_ge(comb_ready.sem, comb_ready.at(b, 3))
                for t in range(TB):
                    mm = pe.transpose(bank[7][0:96, t * P:(t + 1) * P], comb3[:, t, :], const["ident"][:, :])
                mm.then_inc(comb_turned.sem, 1)
                pe.wait_ge(split_steps.sem, split_steps.at(b, 4))

                def down(j):
                    pe.wait_ge(hid_ready.sem, hid_ready.at(b, j + 1))
                    pe.matmul(bank[6][:, :], w2[:, j, :], hid[:, j % 2, :],
                              start=(j == 0), stop=(j == ET - 1)).then_inc(hid_used.sem, 1)

                for j in range(ET):
                    if j >= 2:
                        pe.wait_ge(hid_ready.sem, hid_ready.at(b, j - 1))
                    pe.matmul(bank[j % 2][:, :], w1[:, j * P:(j + 1) * P], xm[:, :],
                              start=True, stop=True).then_inc(h_ready.sem, 1)
                    pe.matmul(bank[2 + j % 2][:, :], w3[:, j * P:(j + 1) * P], xm[:, :],
                              start=True, stop=True).then_inc(g_ready.sem, 1)
                    pe.matmul(bank[4 + j % 2][:, :], owner[:, j, :], combT[:, :],
                              start=True, stop=True).then_inc(cb_ready.sem, 1)
                    if j >= 1:
                        down(j - 1)
                down(ET - 1)
                pe.wait_ge(res_ready.sem, b + 1)
                pe.matmul(bank[0][:, :], const["mean"][:, :], res[:, :], start=True, stop=True).then_inc(mean_ready.sem, 1)
                pe.wait_ge(sq_ready.sem, b + 1)
                pe.matmul(bank[1][:, :], const["mean"][:, :], sq[:, :], start=True, stop=True).then_inc(var_ready.sem, 1)

        @block.scalar
        def _(act):
            with act.Fori(0, SEQS) as b:
                act.preload_act_table_set(EXP_LN_SET)
                act.wait_ge(gap_ready.sem, gap_ready.at(b, 1))
                act.activation(eg[:, :], gap[:, :], ACT.Exp).then_inc(eg_ready.sem, 1)
                act.wait_ge(comb_turned.sem, b + 1)
                act.activation(part_a[:, :], bank[7][0:72, :], ACT.Copy).then_inc(split_steps.sem, 1)
                for j in range(ET):
                    act.wait_ge(h_ready.sem, h_ready.at(b, j + 1))
                    if j >= 2:
                        act.wait_ge(prod_ready.sem, prod_ready.at(b, j - 1))
                    act.activation(act_h[:, j % 2, :], bank[j % 2][:, :], ACT.Silu).then_inc(silu_ready.sem, 1)
                act.preload_act_table_set(EXP_LN_SET)
                act.wait_ge(cen_ready.sem, b + 1)
                act.activation(sq[:, :], cen[:, :], ACT.Square).then_inc(sq_ready.sem, 1)
                act.wait_ge(var_ready.sem, b + 1)
                act.activation(lv[:, :], bank[1][:, :], ACT.Ln, bias=const["eps"][:, 0:1]).then_inc(lv_ready.sem, 1)
                act.wait_ge(lv_ready.sem, b + 1)
                act.activation(rstd[:, :], lv[:, :], ACT.Exp, scale=-0.5).then_inc(rstd_ready.sem, 1)

        @block.vector
        def _(ve):
            ve.memset(comb3[:, :, :], 0.0).then_inc(comb_zeroed.sem, 1)
            ve.wait_ge(loaded.sem, 16 * N_LOADS)
            ve.wait_ge(comb_zeroed.sem, 1)
            ve.sem_inc(stored.sem, 1)
            with ve.Fori(0, SEQS) as b:
                ve.tensor_copy(xm[:, :], xT[:, bass.ds(b * T, T)]).then_inc(xm_ready.sem, 1)
                ve.wait_ge(logits_ready.sem, b + 1)
                ve.tensor_copy(logit[:, :, :], bank[7][:, 0:TB * EXPERTS].rearrange("p (t e) -> p t e", e=EXPERTS))\
                  .then_inc(logit_copied.sem, 1)
                ve.wait_ge(logit_copied.sem, b + 1)
                ve.nop(nofuse=True)
                for t in range(TB):
                    ve.max(top[:, t, :], logit[:, t, :]).then_inc(top_ready.sem, 1)
                ve.wait_ge(top_ready.sem, top_ready.at(b, TB))
                ve.nop(nofuse=True)
                for t in range(TB):
                    ve.max_index(topi[:, t, :], top[:, t, :], logit[:, t, :]).then_inc(topi_ready.sem, 1)
                ve.tensor_tensor(gap[:, :], top[:, :, 1], top[:, :, 0], ALU.subtract).then_inc(gap_ready.sem, 1)
                ve.wait_ge(topi_ready.sem, topi_ready.at(b, TB))
                ve.tensor_copy(topf[:, :, :], topi[:, :, :]).then_inc(gap_ready.sem, 1)
                ve.wait_ge(eg_ready.sem, b + 1)
                ve.tensor_scalar(sg[:, :], eg[:, :], 1.0, None, ALU.add).then_inc(wt_steps.sem, 1)
                ve.wait_ge(wt_steps.sem, wt_steps.at(b, 1))
                ve.reciprocal(wt[:, 0, :], sg[:, :]).then_inc(wt_steps.sem, 1)
                ve.wait_ge(wt_steps.sem, wt_steps.at(b, 2))
                ve.tensor_tensor(wt[:, 1, :], wt[:, 0, :], eg[:, :], ALU.mult).then_inc(wt_steps.sem, 1)
                ve.wait_ge(wt_steps.sem, wt_steps.at(b, 3))
                ve.wait_ge(gap_ready.sem, gap_ready.at(b, 2))
                for k, dst in enumerate((first, second)):
                    for t in range(TB):
                        ve.tensor_scalar(dst[:, t, :], iota[:, :], topf[:, t, k:k + 1], wt[:, k, t:t + 1],
                                         ALU.is_equal, ALU.mult).then_inc(chosen.sem, 1)
                ve.wait_ge(chosen.sem, chosen.at(b, 2 * TB))
                for r in range(3):
                    ve.tensor_tensor(comb3[:, :, 32 * r:32 * r + EXPERTS], first[:, :, :], second[:, :, :],
                                     ALU.add).then_inc(comb_ready.sem, 1)
                ve.wait_ge(split_steps.sem, split_steps.at(b, 1))
                ve.scalar_tensor_tensor(out=rest_a[:, :], in0=part_a[:, :], scalar=part[0:72, 0:1],
                                        in1=bank[7][0:72, :], op0=ALU.mult, op1=ALU.add).then_inc(split_steps.sem, 1)
                ve.wait_ge(split_steps.sem, split_steps.at(b, 2))
                ve.tensor_copy(part_b[:, :], rest_a[:, :]).then_inc(split_steps.sem, 1)
                ve.wait_ge(split_steps.sem, split_steps.at(b, 3))
                ve.scalar_tensor_tensor(out=combT[:, :], in0=part_b[:, :], scalar=part[0:72, 1:2],
                                        in1=rest_a[:, :], op0=ALU.mult, op1=ALU.add).then_inc(split_steps.sem, 1)
                for j in range(ET):
                    ve.wait_ge(silu_ready.sem, silu_ready.at(b, j + 1))
                    ve.wait_ge(g_ready.sem, g_ready.at(b, j + 1))
                    ve.tensor_tensor(prod[:, j % 2, :], act_h[:, j % 2, :], bank[2 + j % 2][:, :],
                                     ALU.mult).then_inc(prod_ready.sem, 1)
                    ve.wait_ge(prod_ready.sem, prod_ready.at(b, j + 1))
                    ve.wait_ge(cb_ready.sem, cb_ready.at(b, j + 1))
                    if j >= 2:
                        ve.wait_ge(hid_used.sem, hid_used.at(b, j - 1))
                    ve.tensor_tensor(hid[:, j % 2, :], prod[:, j % 2, :], bank[4 + j % 2][:, :],
                                     ALU.mult).then_inc(hid_ready.sem, 1)
                ve.wait_ge(hid_used.sem, hid_used.at(b, ET))
                ve.tensor_tensor(res[:, :], bank[6][:, :], xm[:, :], ALU.add).then_inc(res_ready.sem, 1)
                ve.wait_ge(mean_ready.sem, b + 1)
                ve.wait_ge(res_ready.sem, b + 1)
                ve.tensor_tensor(cen[:, :], res[:, :], bank[0][:, :], ALU.subtract).then_inc(cen_ready.sem, 1)
                ve.wait_ge(rstd_ready.sem, b + 1)
                ve.wait_ge(stored.sem, b * 16 + 1)
                ve.tensor_tensor(fin[:, :], cen[:, :], rstd[:, :], ALU.mult).then_inc(fin_ready.sem, 1)



def build_program(nc, d, out):
    with ExitStack() as ctx:
        def sb(name, shape):
            return ctx.enter_context(nc.sbuf_tensor(name, shape, F32))

        xT = sb("xT", [P, SEQS * T])
        x0T = sb("x0T", [P, SEQS * T])
        const = {"ident": sb("ident", [P, P]), "mean": sb("mean", [P, P]),
                 "heads": sb("heads", [P, P]),
                 "one": sb("one", [P, 1]), "eps": sb("eps", [P, 1]), "unshift": sb("unshift", [P, 1])}
        with ExitStack() as c2:
            const_loaded = c2.enter_context(nc.semaphore("const_loaded"))
            const_set = c2.enter_context(nc.semaphore("const_set"))
            block = c2.enter_context(nc.Block())

            @block.sync
            def _(sp):
                sp.dma_start(const["ident"][:, :], d["c_ident"]).then_inc(const_loaded, 16)
                sp.dma_start(const["heads"][:, :], d["c_heads"]).then_inc(const_loaded, 16)
                sp.wait_ge(const_loaded, 32)
                sp.wait_ge(const_set, 4)

            @block.vector
            def _(ve):
                ve.memset(const["mean"][:, :], 1.0 / P).then_inc(const_set, 1)
                ve.memset(const["one"][:, :], 1.0).then_inc(const_set, 1)
                ve.memset(const["eps"][:, :], EPS).then_inc(const_set, 1)
                ve.memset(const["unshift"][:, :], 15 * math.log(2.0)).then_inc(const_set, 1)

        def ssm_weights(k):
            return {"pick": d["c_pick"],
                    **{n: d[f"{k}_{n}"] for n in ("w_in", "w_bc", "w_dlt", "w_dt", "w_out", "chan", "a_log")}}

        held = {}

        def signals(name, per=1):
            if name not in held:
                held[name] = Counter(ctx, nc, "ssm_" + name, per)
            return held[name]

        state_space_phase(nc, "s0_", signals, 0, xT, d["x"], const, ssm_weights("s0"))
        local_attention_phase(nc, "at_", xT, x0T, const,
                              {n: d["at_" + n] for n in ("w_qkv", "w_o", "w1", "w2", "chan", "tables", "mask")})
        layer_norm_phase(nc, "ln_", xT, x0T, const)
        state_space_phase(nc, "s1_", signals, 1, xT, None, const, ssm_weights("s1"))
        expert_phase(nc, "ex_", xT, const,
                     {n: d["ex_" + n] for n in ("wr", "w1", "w3", "w2", "owner", "part", "iota")}, out)


def kernel(**inputs):
    import numpy as np
    import concourse.bacc as _bacc
    from concourse.bass_utils import run_bass_kernel_spmd as _run

    i = {k: np.asarray(v) for k, v in inputs.items()}
    f = np.float32
    arrays = {"x": i["L0_attn_x"].transpose(2, 0, 1).reshape(P, SEQS * T)}
    pick = np.zeros((32, 32, P), f)
    pick[np.arange(32), np.arange(32), :] = 1
    arrays["c_ident"], arrays["c_pick"] = np.eye(P, dtype=f), pick

    def halves(a):
        return a.reshape(2, P, -1).transpose(1, 0, 2)

    def ssm(k, w_in, w_x, rank, w_dt, taps, conv_b, b_dt, skip, a_log, w_out):
        arrays[k + "w_in"] = w_in
        arrays[k + "w_bc"], arrays[k + "w_dlt"] = halves(w_x[:, rank:]), halves(w_x[:, :rank])
        arrays[k + "w_dt"], arrays[k + "w_out"] = w_dt, halves(w_out)
        arrays[k + "chan"] = np.concatenate([halves(taps), halves(conv_b), halves(b_dt), halves(skip)], 2)
        arrays[k + "a_log"] = halves(a_log)

    ssm("s0_", i["L0_attn_W_in"].T, i["L0_attn_W_xproj"].T, 8, i["L0_attn_W_dt"].T, i["L0_attn_W_conv"][:, 0, :],
        np.zeros(256, f), i["L0_attn_b_dt"], i["L0_attn_D"], i["L0_attn_A_log"], i["L0_attn_W_out"].T)
    ssm("s1_", i["L1_attn_W_in"], i["L1_attn_W_x"], 64, i["L1_attn_W_delta"], i["L1_attn_conv_w"][:, 0, :].T,
        i["L1_attn_conv_b"], i["L1_attn_b_delta"], i["L1_attn_D"], i["L1_attn_A_log"], i["L1_attn_W_out"])

    half = np.arange(0, 64, 2, dtype=f)
    t = np.arange(T, dtype=f)
    freqs = t[:, None] * (1.0 / 10000.0 ** (half / 64)).astype(f)[None, :]
    scale = (((half + 0.4 * 64) / (1.4 * 64)).astype(f)[None, :] ** ((t - T // 2) / 16)[:, None]).astype(f)
    cos, sin = np.cos(freqs), np.sin(freqs)

    def both_heads(a, sign):
        return np.concatenate([sign * a, a, sign * a, a], 1).T.astype(f)

    arrays["at_tables"] = np.stack([both_heads(cos * scale, 1), both_heads(sin * scale, -1),
                                    both_heads(cos / scale, 1), both_heads(sin / scale, -1)], 1)
    qi, kc = np.arange(P)[:, None] % 64, np.arange(96)[None, :]
    band = np.where((kc >= qi) & (kc <= qi + 32), f(0), f(-1e30))
    first = np.where(kc >= 32, band, f(-1e30))
    arrays["at_mask"] = np.concatenate([first] + [band] * 7, 1).reshape(P, 2, 4 * 96).astype(f)
    arrays["c_heads"] = np.kron(np.eye(2, dtype=f), np.ones((64, 64), f))
    arrays["at_w_qkv"] = i["L0_ffn_Wqkv"]
    arrays["at_w_o"] = i["L0_ffn_Wo"].reshape(6, 8, P, P).transpose(0, 2, 1, 3)
    arrays["at_w1"] = i["L0_ffn_W1"]
    hid = 114

    def hidden(a):
        a = np.concatenate([a, a[:, :1]], 1)
        return a.reshape(6, 3, hid, -1).transpose(0, 2, 1, 3)

    def per_channel(a):
        return np.stack([np.tile(a, 2), np.tile(np.roll(a, 32, 1), 2)], 2)

    arrays["at_w2"] = hidden(i["L0_ffn_W2"])
    b1 = i["L0_ffn_b1"][:, :, None]
    b1 = np.concatenate([hidden(b1[:, :341])[..., 0], hidden(b1[:, 341:])[..., 0]], 2)
    b1 = np.concatenate([b1, b1[:, :P - hid]], 1)
    arrays["at_chan"] = np.concatenate(
        [per_channel(i["L0_ffn_q_scale"]), per_channel(i["L0_ffn_k_scale"]),
         np.stack([i["L0_ffn_ln_g"], i["L0_ffn_ln_b"], i["L0_ffn_b2"]], 2), b1], 2)

    import ml_dtypes
    arrays["ex_wr"] = i["L1_ffn_Wr"]
    arrays["ex_w1"] = i["L1_ffn_W1"].transpose(1, 0, 2).reshape(P, -1)
    arrays["ex_w3"] = i["L1_ffn_W3"].transpose(1, 0, 2).reshape(P, -1)
    arrays["ex_w2"] = i["L1_ffn_W2"].reshape(12, P, P).transpose(1, 0, 2)
    owner = np.zeros((72, 12 * P), ml_dtypes.bfloat16)
    for r in range(3):
        for e in range(8):
            owner[32 * r + e, 192 * e:192 * (e + 1)] = 1
    arrays["ex_owner"] = owner.reshape(72, 12, P)
    rows = np.arange(P)
    arrays["ex_part"] = np.stack([np.where(rows >= 32, f(-1), f(0)), np.where(rows >= 64, f(-1), f(0))], 1)
    arrays["ex_iota"] = np.tile(np.arange(8, dtype=f), (P, 1))

    nc = _bacc.Bacc("TRN2", target_bir_lowering=False, num_devices=1)
    arrays = {k: np.ascontiguousarray(v) for k, v in arrays.items()}
    d = {k: nc.dram_tensor("in_" + k, v.shape, mybir.dt.from_np(v.dtype), kind="ExternalInput").ap()
         for k, v in arrays.items()}
    out = nc.dram_tensor("out", (P, SEQS * T), F32, kind="ExternalOutput").ap()
    build_program(nc, d, out)
    r = _run(nc, [{"in_" + k: v for k, v in arrays.items()}], core_ids=[0])
    return np.ascontiguousarray(r.results[0]["out"].reshape(P, SEQS, T).transpose(1, 2, 0))
```

```python
import math
from contextlib import ExitStack

import concourse.bass as bass
from concourse import mybir

F32 = mybir.dt.float32
BF16 = mybir.dt.bfloat16
U32 = mybir.dt.uint32
ALU = mybir.AluOpType
ACT = mybir.ActivationFunctionType
AX = mybir.AxisListType
EXP_LN_SET = "natural_log_exp_and_others"
GELU_SET = "gelu_and_others"

P = 128
SEQS = 8
T = 512
EPS = 1e-5


class Counter:

    def __init__(self, ctx, nc, name, per):
        self.sem = ctx.enter_context(nc.semaphore(name))
        self.per = per

    def at(self, it, k):
        return it * self.per + k


class Memory:

    def __init__(self, ctx, nc, prefix):
        self.ctx, self.nc, self.prefix = ctx, nc, prefix

    def sb(self, name, shape, dt=F32):
        return self.ctx.enter_context(self.nc.sbuf_tensor(self.prefix + name, shape, dt))

    def bank(self, name):
        return self.ctx.enter_context(self.nc.psum_tensor(self.prefix + name, [P, 512], F32))

    def counter(self, name, per=1):
        return Counter(self.ctx, self.nc, self.prefix + name, per)


def state_space_phase(nc, prefix, signals, turn, xT, x_dram, const, w):
    NSTATE = 16
    HALVES = 2
    TAPS = 4
    R = w["w_dt"].shape[0]
    with ExitStack() as ctx:
        m = Memory(ctx, nc, prefix)
        w_in = m.sb("w_in", [P, 4 * P])
        pick = m.sb("pick", [2 * NSTATE, 2 * NSTATE, P])
        w_bc = m.sb("w_bc", [P, HALVES, 2 * NSTATE])
        w_dlt = m.sb("w_dlt", [P, HALVES, R])
        w_dt = m.sb("w_dt", [R, HALVES * P])
        w_out = m.sb("w_out", [P, HALVES, P])
        chan = m.sb("chan", [P, HALVES, TAPS + 3])
        a_log = m.sb("a_log", [P, HALVES, NSTATE])
        a_exp = m.sb("a_exp", [P, HALVES, NSTATE])
        decay = m.sb("decay", [P, HALVES, NSTATE])
        xpad = m.sb("xpad", [P, HALVES, TAPS - 1 + T])
        conv = m.sb("conv", [P, HALVES, T])
        ex = m.sb("ex", [P, HALVES, T])
        rx = m.sb("rx", [P, HALVES, T])
        xc = m.sb("xc", [P, HALVES, T])
        ez = m.sb("ez", [P, HALVES, T])
        rz = m.sb("rz", [P, HALVES, T])
        zs = m.sb("zs", [P, HALVES, T])
        bc = m.sb("bc", [2 * NSTATE, T])
        dlt = m.sb("dlt", [R, T])
        mag = m.sb("mag", [P, HALVES, T])
        em = m.sb("em", [P, HALVES, T])
        lg = m.sb("lg", [P, HALVES, T])
        onep = m.sb("onep", [P, HALVES, T])
        dm = m.sb("dm", [P, HALVES, T])
        pos = m.sb("pos", [P, HALVES, T])
        delta = m.sb("delta", [P, HALVES, T])
        u = m.sb("u", [P, HALVES, T])
        csb = m.sb("csb", [P, 2, T])
        dA = m.sb("dA", [P, 2, HALVES, T])
        dBx = m.sb("dBx", [P, 2, HALVES, T])
        h = m.sb("h", [P, 2, HALVES, T])
        hc = m.sb("hc", [P, 2, HALVES, T])
        y = m.sb("y", [P, HALVES, T])
        yz = m.sb("yz", [P, HALVES, T])
        res = m.sb("res", [P, T])
        cen = m.sb("cen", [P, T])
        sq = m.sb("sq", [P, T])
        lv = m.sb("lv", [P, T])
        rstd = m.sb("rstd", [P, T])
        bank = [m.bank(f"bank{i}") for i in range(8)]

        loaded = signals("loaded")
        x_loaded = signals("x_loaded")
        zero_pad = signals("zero_pad")
        a_ready = signals("a_ready")
        xz_ready = signals("xz_ready", 4)
        xpad_ready = signals("xpad_ready", 2)
        tap_done = signals("tap_done", TAPS * HALVES)
        ez_ready = signals("ez_ready", 2)
        rz_ready = signals("rz_ready", 4)
        zs_ready = signals("zs_ready", 2)
        ex_ready = signals("ex_ready", 2)
        rx_ready = signals("rx_ready", 4)
        xc_ready = signals("xc_ready", 2)
        bc_ps = signals("bc_ps")
        dlt_ps = signals("dlt_ps")
        bc_ready = signals("bc_ready")
        dlt_ready = signals("dlt_ready")
        dt_ready = signals("dt_ready", 2)
        mag_ready = signals("mag_ready", 2)
        em_ready = signals("em_ready", 2)
        lg_ready = signals("lg_ready", 2)
        dm_steps = signals("dm_steps", 5 * HALVES)
        pos_ready = signals("pos_ready", 2)
        rdm_ready = signals("rdm_ready", 2)
        delta_ready = signals("delta_ready", 2)
        u_ready = signals("u_ready", 2)
        b_ready = signals("b_ready", NSTATE)
        c_ready = signals("c_ready", NSTATE)
        c_copied = signals("c_copied", NSTATE)
        dA_ready = signals("dA_ready", NSTATE * HALVES)
        dBx_ready = signals("dBx_ready", NSTATE * HALVES)
        h_ready = signals("h_ready", NSTATE * HALVES)
        hc_ready = signals("hc_ready", NSTATE * HALVES)
        hc_used = signals("hc_used", NSTATE * HALVES)
        y_summed = signals("y_summed", 2)
        y_ready = signals("y_ready", 2)
        yz_ready = signals("yz_ready", 2)
        out_ps = signals("out_ps")
        res_ready = signals("res_ready")
        mean_ready = signals("mean_ready")
        cen_ready = signals("cen_ready")
        sq_ready = signals("sq_ready")
        var_ready = signals("var_ready")
        lv_ready = signals("lv_ready")
        rstd_ready = signals("rstd_ready")
        x_written = signals("x_written")

        block = ctx.enter_context(nc.Block())
        N_LOADS = 8

        def tokens(b):
            return bass.ds((b - turn * SEQS) * T if turn else b * T, T)

        @block.sync
        def _(sp):
            if x_dram is not None:
                sp.dma_start(xT[:, :], x_dram).then_inc(x_loaded.sem, 16)
            sp.dma_start(pick[:, :, :], w["pick"]).then_inc(loaded.sem, 16)
            sp.dma_start(w_in[:, :], w["w_in"]).then_inc(loaded.sem, 16)
            sp.dma_start(w_bc[:, :, :], w["w_bc"]).then_inc(loaded.sem, 16)
            sp.dma_start(w_dlt[:, :, :], w["w_dlt"]).then_inc(loaded.sem, 16)
            sp.dma_start(w_dt[:, :], w["w_dt"]).then_inc(loaded.sem, 16)
            sp.dma_start(w_out[:, :, :], w["w_out"]).then_inc(loaded.sem, 16)
            sp.dma_start(chan[:, :, :], w["chan"]).then_inc(loaded.sem, 16)
            sp.dma_start(a_log[:, :, :], w["a_log"]).then_inc(loaded.sem, 16)
            sp.wait_ge(loaded.sem, 16 * N_LOADS * (turn + 1))

        @block.tensor
        def _(pe):
            pe.wait_ge(loaded.sem, 16 * N_LOADS * (turn + 1))
            if x_dram is not None:
                pe.wait_ge(x_loaded.sem, 16)
            with pe.Fori(turn * SEQS, (turn + 1) * SEQS) as b:
                pe.wait_ge(x_written.sem, x_written.at(b, 1))
                for i in range(4):
                    pe.matmul(bank[i][:, :], w_in[:, i * P:(i + 1) * P], xT[:, tokens(b)],
                              start=True, stop=True).then_inc(xz_ready.sem, 1)
                pe.wait_ge(xc_ready.sem, xc_ready.at(b, 2))
                for c in range(HALVES):
                    mm = pe.matmul(bank[4][0:2 * NSTATE, :], w_bc[:, c, :], xc[:, c, :],
                                   start=(c == 0), stop=(c == 1))
                mm.then_inc(bc_ps.sem, 1)
                for c in range(HALVES):
                    mm = pe.matmul(bank[5][0:R, :], w_dlt[:, c, :], xc[:, c, :],
                                   start=(c == 0), stop=(c == 1))
                mm.then_inc(dlt_ps.sem, 1)
                pe.wait_ge(dlt_ready.sem, dlt_ready.at(b, 1))
                for c in range(HALVES):
                    pe.matmul(bank[6 + c][:, :], w_dt[:, c * P:(c + 1) * P], dlt[:, :],
                              start=True, stop=True).then_inc(dt_ready.sem, 1)
                pe.wait_ge(bc_ready.sem, bc_ready.at(b, 1))
                pe.wait_ge(xpad_ready.sem, xpad_ready.at(b, 2))
                pe.wait_ge(zs_ready.sem, zs_ready.at(b, 2))

                def accumulate(n):
                    for c in range(HALVES):
                        k = n * HALVES + c
                        pe.wait_ge(hc_ready.sem, hc_ready.at(b, k + 1))
                        mm = pe.matmul(bank[4 + c][:, :], const["ident"][:, :], hc[:, n % 2, c, :],
                                       start=(n == 0), stop=(n == NSTATE - 1))
                        mm.then_inc(hc_used.sem, 1)

                for n in range(NSTATE):
                    if n >= 2:
                        pe.wait_ge(dBx_ready.sem, dBx_ready.at(b, (n - 1) * HALVES))
                    pe.matmul(bank[n % 2][:, :], pick[:, n, :], bc[:, :],
                              start=True, stop=True).then_inc(b_ready.sem, 1)
                    if n >= 2:
                        pe.wait_ge(c_copied.sem, c_copied.at(b, n - 1))
                    pe.matmul(bank[2 + n % 2][:, :], pick[:, NSTATE + n, :], bc[:, :],
                              start=True, stop=True).then_inc(c_ready.sem, 1)
                    if n >= 1:
                        accumulate(n - 1)
                accumulate(NSTATE - 1)
                pe.wait_ge(yz_ready.sem, yz_ready.at(b, 2))
                for c in range(HALVES):
                    mm = pe.matmul(bank[6][:, :], w_out[:, c, :], yz[:, c, :],
                                   start=(c == 0), stop=(c == 1))
                mm.then_inc(out_ps.sem, 1)
                pe.wait_ge(res_ready.sem, res_ready.at(b, 1))
                pe.matmul(bank[7][:, :], const["mean"][:, :], res[:, :],
                          start=True, stop=True).then_inc(mean_ready.sem, 1)
                pe.wait_ge(sq_ready.sem, sq_ready.at(b, 1))
                pe.matmul(bank[6][:, :], const["mean"][:, :], sq[:, :],
                          start=True, stop=True).then_inc(var_ready.sem, 1)

        @block.scalar
        def _(act):
            act.preload_act_table_set(EXP_LN_SET)
            act.wait_ge(loaded.sem, 16 * N_LOADS * (turn + 1))
            act.activation(a_exp[:, :, :], a_log[:, :, :], ACT.Exp).then_inc(a_ready.sem, 1)
            act.wait_ge(a_ready.sem, 2 * turn + 2)
            act.wait_ge(zero_pad.sem, turn + 1)
            with act.Fori(turn * SEQS, (turn + 1) * SEQS) as b:
                act.preload_act_table_set(EXP_LN_SET)
                for c in range(HALVES):
                    act.wait_ge(xz_ready.sem, xz_ready.at(b, c + 1))
                    act.activation(xpad[:, c, TAPS - 1:], bank[c][:, :], ACT.Copy).then_inc(xpad_ready.sem, 1)
                for c in range(HALVES):
                    act.wait_ge(xz_ready.sem, xz_ready.at(b, 3 + c))
                    act.activation(ez[:, c, :], bank[2 + c][:, :], ACT.Exp, scale=-1.0).then_inc(ez_ready.sem, 1)
                for c in range(HALVES):
                    act.wait_ge(tap_done.sem, tap_done.at(b, HALVES * (TAPS - 1) + c + 1))
                    act.activation(ex[:, c, :], conv[:, c, :], ACT.Exp, scale=-1.0).then_inc(ex_ready.sem, 1)
                act.wait_ge(dlt_ps.sem, dlt_ps.at(b, 1))
                act.activation(dlt[:, :], bank[5][0:R, :], ACT.Copy).then_inc(dlt_ready.sem, 1)
                act.wait_ge(bc_ps.sem, bc_ps.at(b, 1))
                act.activation(bc[:, :], bank[4][0:2 * NSTATE, :], ACT.Copy).then_inc(bc_ready.sem, 1)
                for c in range(HALVES):
                    act.wait_ge(dt_ready.sem, dt_ready.at(b, c + 1))
                    act.activation(mag[:, c, :], bank[6 + c][:, :], ACT.Abs,
                                   bias=chan[:, c, TAPS + 1:TAPS + 2]).then_inc(mag_ready.sem, 1)
                for c in range(HALVES):
                    act.wait_ge(mag_ready.sem, mag_ready.at(b, c + 1))
                    act.activation(em[:, c, :], mag[:, c, :], ACT.Exp, scale=-1.0).then_inc(em_ready.sem, 1)
                for c in range(HALVES):
                    act.wait_ge(dm_steps.sem, dm_steps.at(b, c + 1))
                    act.activation(lg[:, c, :], onep[:, c, :], ACT.Ln).then_inc(lg_ready.sem, 1)
                act.wait_ge(delta_ready.sem, delta_ready.at(b, 2))
                for n in range(NSTATE):
                    act.wait_ge(c_ready.sem, c_ready.at(b, n + 1))
                    if n >= 2:
                        act.wait_ge(hc_ready.sem, hc_ready.at(b, (n - 1) * HALVES))
                    act.activation(csb[:, n % 2, :], bank[2 + n % 2][:, :], ACT.Copy).then_inc(c_copied.sem, 1)
                    for c in range(HALVES):
                        if n >= 2:
                            act.wait_ge(h_ready.sem, h_ready.at(b, (n - 2) * HALVES + c + 1))
                        act.activation(dA[:, n % 2, c, :], delta[:, c, :], ACT.Exp,
                                       scale=decay[:, c, n:n + 1]).then_inc(dA_ready.sem, 1)
                act.wait_ge(var_ready.sem, var_ready.at(b, 1))
                act.activation(lv[:, :], bank[6][:, :], ACT.Ln, bias=const["eps"][:, 0:1]).then_inc(lv_ready.sem, 1)
                act.wait_ge(lv_ready.sem, lv_ready.at(b, 1))
                act.activation(rstd[:, :], lv[:, :], ACT.Exp, scale=-0.5).then_inc(rstd_ready.sem, 1)

        @block.vector
        def _(ve):
            ve.memset(xpad[:, :, 0:TAPS - 1], 0.0).then_inc(zero_pad.sem, 1)
            ve.wait_ge(a_ready.sem, 2 * turn + 1)
            ve.tensor_scalar(decay[:, :, :], a_exp[:, :, :], -1.0, None, ALU.mult).then_inc(a_ready.sem, 1)
            if turn == 0:
                ve.sem_inc(x_written.sem, 1)
            with ve.Fori(turn * SEQS, (turn + 1) * SEQS) as b:
                for j in range(TAPS):
                    for c in range(HALVES):
                        src = xpad[:, c, j:j + T]
                        tap = chan[:, c, j:j + 1]
                        if j == 0:
                            ve.wait_ge(xpad_ready.sem, xpad_ready.at(b, c + 1))
                            ve.tensor_scalar(conv[:, c, :], src, tap, chan[:, c, TAPS:TAPS + 1],
                                             ALU.mult, ALU.add).then_inc(tap_done.sem, 1)
                        elif j < TAPS - 1:
                            ve.wait_ge(tap_done.sem, tap_done.at(b, HALVES * (j - 1) + c + 1))
                            ve.scalar_tensor_tensor(out=conv[:, c, :], in0=src, scalar=tap, in1=conv[:, c, :],
                                                    op0=ALU.mult, op1=ALU.add).then_inc(tap_done.sem, 1)
                for c in range(HALVES):
                    ve.wait_ge(tap_done.sem, tap_done.at(b, HALVES * (TAPS - 1)))
                    ve.scalar_tensor_tensor(out=conv[:, c, :], in0=xpad[:, c, TAPS - 1:TAPS - 1 + T],
                                            scalar=chan[:, c, TAPS - 1:TAPS], in1=conv[:, c, :],
                                            op0=ALU.mult, op1=ALU.add).then_inc(tap_done.sem, 1)
                for c in range(HALVES):
                    ve.wait_ge(ez_ready.sem, ez_ready.at(b, c + 1))
                    ve.tensor_scalar(ez[:, c, :], ez[:, c, :], 1.0, None, ALU.add).then_inc(rz_ready.sem, 1)
                for c in range(HALVES):
                    ve.wait_ge(rz_ready.sem, rz_ready.at(b, c + 1))
                    ve.reciprocal(rz[:, c, :], ez[:, c, :]).then_inc(rz_ready.sem, 1)
                for c in range(HALVES):
                    ve.wait_ge(rz_ready.sem, rz_ready.at(b, 3 + c))
                    ve.tensor_tensor(zs[:, c, :], bank[2 + c][:, :], rz[:, c, :], ALU.mult).then_inc(zs_ready.sem, 1)
                for c in range(HALVES):
                    ve.wait_ge(ex_ready.sem, ex_ready.at(b, c + 1))
                    ve.tensor_scalar(ex[:, c, :], ex[:, c, :], 1.0, None, ALU.add).then_inc(rx_ready.sem, 1)
                for c in range(HALVES):
                    ve.wait_ge(rx_ready.sem, rx_ready.at(b, c + 1))
                    ve.reciprocal(rx[:, c, :], ex[:, c, :]).then_inc(rx_ready.sem, 1)
                for c in range(HALVES):
                    ve.wait_ge(rx_ready.sem, rx_ready.at(b, 3 + c))
                    ve.tensor_tensor(xc[:, c, :], conv[:, c, :], rx[:, c, :], ALU.mult).then_inc(xc_ready.sem, 1)
                for c in range(HALVES):
                    ve.wait_ge(mag_ready.sem, mag_ready.at(b, c + 1))
                    ve.tensor_scalar(pos[:, c, :], bank[6 + c][:, :], chan[:, c, TAPS + 1:TAPS + 2], 0.0,
                                     ALU.add, ALU.max).then_inc(pos_ready.sem, 1)
                for c in range(HALVES):
                    ve.wait_ge(em_ready.sem, em_ready.at(b, c + 1))
                    ve.tensor_scalar(onep[:, c, :], em[:, c, :], 1.0, None, ALU.add).then_inc(dm_steps.sem, 1)
                for c in range(HALVES):
                    ve.wait_ge(dm_steps.sem, dm_steps.at(b, c + 1))
                    ve.tensor_scalar(dm[:, c, :], onep[:, c, :], 1.0, 1e-30,
                                     ALU.subtract, ALU.max).then_inc(dm_steps.sem, 1)
                for c in range(HALVES):
                    ve.wait_ge(dm_steps.sem, dm_steps.at(b, 3 + c))
                    ve.reciprocal(dm[:, c, :], dm[:, c, :]).then_inc(dm_steps.sem, 1)
                for c in range(HALVES):
                    ve.wait_ge(dm_steps.sem, dm_steps.at(b, 5 + c))
                    ve.wait_ge(lg_ready.sem, lg_ready.at(b, c + 1))
                    ve.scalar_tensor_tensor(out=dm[:, c, :], in0=lg[:, c, :], scalar=1e-30, in1=dm[:, c, :],
                                            op0=ALU.max, op1=ALU.mult).then_inc(dm_steps.sem, 1)
                for c in range(HALVES):
                    ve.wait_ge(dm_steps.sem, dm_steps.at(b, 7 + c))
                    ve.scalar_tensor_tensor(out=dm[:, c, :], in0=dm[:, c, :], scalar=1.0, in1=em[:, c, :],
                                            op0=ALU.min, op1=ALU.mult).then_inc(dm_steps.sem, 1)
                for c in range(HALVES):
                    ve.wait_ge(dm_steps.sem, dm_steps.at(b, 9 + c))
                    ve.wait_ge(pos_ready.sem, pos_ready.at(b, c + 1))
                    ve.tensor_tensor(delta[:, c, :], dm[:, c, :], pos[:, c, :], ALU.add).then_inc(delta_ready.sem, 1)
                for c in range(HALVES):
                    ve.wait_ge(delta_ready.sem, delta_ready.at(b, c + 1))
                    ve.wait_ge(xc_ready.sem, xc_ready.at(b, c + 1))
                    ve.tensor_tensor(u[:, c, :], delta[:, c, :], xc[:, c, :], ALU.mult).then_inc(u_ready.sem, 1)
                ve.wait_ge(u_ready.sem, u_ready.at(b, 2))
                for n in range(NSTATE):
                    ve.wait_ge(b_ready.sem, b_ready.at(b, n + 1))
                    for c in range(HALVES):
                        if n >= 2:
                            ve.wait_ge(h_ready.sem, h_ready.at(b, (n - 2) * HALVES + c + 1))
                        ve.tensor_tensor(dBx[:, n % 2, c, :], u[:, c, :], bank[n % 2][:, :],
                                         ALU.mult).then_inc(dBx_ready.sem, 1)
                    for c in range(HALVES):
                        k = n * HALVES + c
                        ve.wait_ge(dBx_ready.sem, dBx_ready.at(b, k + 1))
                        ve.wait_ge(dA_ready.sem, dA_ready.at(b, k + 1))
                        if n >= 2:
                            ve.wait_ge(hc_ready.sem, hc_ready.at(b, (n - 2) * HALVES + c + 1))
                        ve.tensor_tensor_scan(h[:, n % 2, c, :], dA[:, n % 2, c, :], dBx[:, n % 2, c, :], 0.0,
                                              ALU.mult, ALU.add).then_inc(h_ready.sem, 1)
                for c in range(HALVES):
                    ve.wait_ge(hc_used.sem, hc_used.at(b, NSTATE * HALVES))
                    ve.scalar_tensor_tensor(out=y[:, c, :], in0=xc[:, c, :], scalar=chan[:, c, TAPS + 2:TAPS + 3],
                                            in1=bank[4 + c][:, :], op0=ALU.mult, op1=ALU.add)\
                      .then_inc(y_ready.sem, 1)
                for c in range(HALVES):
                    ve.wait_ge(y_ready.sem, y_ready.at(b, c + 1))
                    ve.wait_ge(zs_ready.sem, zs_ready.at(b, c + 1))
                    ve.tensor_tensor(yz[:, c, :], y[:, c, :], zs[:, c, :], ALU.mult).then_inc(yz_ready.sem, 1)
                ve.wait_ge(out_ps.sem, out_ps.at(b, 1))
                ve.tensor_tensor(res[:, :], bank[6][:, :], xT[:, tokens(b)], ALU.add).then_inc(res_ready.sem, 1)
                ve.wait_ge(res_ready.sem, res_ready.at(b, 1))
                ve.wait_ge(mean_ready.sem, mean_ready.at(b, 1))
                ve.tensor_tensor(cen[:, :], res[:, :], bank[7][:, :], ALU.subtract).then_inc(cen_ready.sem, 1)
                ve.wait_ge(cen_ready.sem, cen_ready.at(b, 1))
                ve.tensor_tensor(sq[:, :], cen[:, :], cen[:, :], ALU.mult).then_inc(sq_ready.sem, 1)
                ve.wait_ge(rstd_ready.sem, rstd_ready.at(b, 1))
                ve.tensor_tensor(xT[:, tokens(b)], cen[:, :], rstd[:, :], ALU.mult).then_inc(x_written.sem, 1)

        @block.gpsimd
        def _(pool):
            with pool.Fori(turn * SEQS, (turn + 1) * SEQS) as b:
                for n in range(NSTATE):
                    pool.wait_ge(c_copied.sem, c_copied.at(b, n + 1))
                    for c in range(HALVES):
                        k = n * HALVES + c
                        pool.wait_ge(h_ready.sem, h_ready.at(b, k + 1))
                        if n >= 2:
                            pool.wait_ge(hc_used.sem, hc_used.at(b, (n - 2) * HALVES + c + 1))
                        pool.tensor_tensor(hc[:, n % 2, c, :], h[:, n % 2, c, :], csb[:, n % 2, :],
                                           ALU.mult).then_inc(hc_ready.sem, 1)


def local_attention_phase(nc, prefix, xT, x0T, const, w):
    DEPTH = 6
    PAIRS = 8
    HD = 64
    QB = 64
    KB = 96
    LOOK = KB - QB
    NB = T // QB
    HALF = NB // 2
    TILES = 2 * PAIRS
    INNER = PAIRS * P
    HID = w["w2"].shape[1]
    HT = 3
    HR = [HID, HID, 341 - 2 * HID]
    QK_SCALE = 8.0
    NORM_SHIFT = 2.0 ** 30
    with ExitStack() as ctx:
        m = Memory(ctx, nc, prefix)
        w_qkv = m.sb("w_qkv", [P, 3 * INNER])
        w_rot = m.sb("w_rot", [P, 2 * INNER])
        w_o = m.sb("w_o", [P, PAIRS, P])
        w_1 = m.sb("w_1", [P, 2 * 341])
        w_2 = m.sb("w_2", [HID, HT, P])
        chan_a = m.sb("chan_a", [P, 4])
        chan = m.sb("chan", [P, 9])
        flag = m.sb("flag", [P, 1])
        base = m.sb("base", [P, 4, T])
        table = m.sb("table", [P, 4, T])
        mask = m.sb("mask", [P, 2, HALF * KB])
        xs = m.sb("xs", [P, LOOK + T])
        vals = m.sb("vals", [KB, NB, INNER])
        sq = m.sb("sq", [P, 2, T])
        t1 = m.sb("t1", [P, 2, T])
        t2 = m.sb("t2", [P, 2, T])
        nrm = m.sb("nrm", [P, 2, T])
        lnn = m.sb("lnn", [P, 2, T])
        rn = m.sb("rn", [P, 2, T])
        qT = m.sb("qT", [P, 2, T])
        kT = m.sb("kT", [P, 2, LOOK + T])
        sc = m.sb("sc", [P, 2, HALF * KB])
        mx = m.sb("mx", [P, 2, HALF])
        pr = m.sb("pr", [P, 2, HALF * KB])
        den = m.sb("den", [P, 2, HALF])
        rden = m.sb("rden", [P, 2, HALF])
        pn = m.sb("pn", [P, 2, HALF * KB])
        pT = m.sb("pT", [KB, 2, HALF * P])
        oT = m.sb("oT", [P, PAIRS, T])
        fs = m.sb("fs", [P, T])
        cen = m.sb("cen", [P, T])
        csq = m.sb("csq", [P, T])
        lv = m.sb("lv", [P, T])
        rstd = m.sb("rstd", [P, T])
        xn = m.sb("xn", [P, T])
        hid = m.sb("hid", [HID, HT, T])
        bank = [m.bank(f"bank{i}") for i in range(8)]

        fixed_loaded = m.counter("fixed_loaded")
        zeroed = m.counter("zeroed")
        qkv_loaded = m.counter("qkv_loaded")
        qkv_free = m.counter("qkv_free")
        ffn_loaded = m.counter("ffn_loaded")
        rot_weights = m.counter("rot_weights", 4)
        tables_ready = m.counter("tables_ready", 4)
        shifted = m.counter("shifted", 2)
        v_ready = m.counter("v_ready", 2 * NB)
        v_copied = m.counter("v_copied", 2 * NB)
        rt_ready = m.counter("rt_ready", TILES)
        sq_ready = m.counter("sq_ready", TILES)
        t_ready = m.counter("t_ready", 2 * TILES)
        n_ready = m.counter("n_ready", TILES)
        guarded = m.counter("guarded", TILES)
        ln_ready = m.counter("ln_ready", TILES)
        rn_ready = m.counter("rn_ready", TILES)
        added = m.counter("added", TILES)
        rotated = m.counter("rotated", TILES)
        s_ready = m.counter("s_ready", TILES)
        masked = m.counter("masked", TILES)
        mx_ready = m.counter("mx_ready", TILES)
        sub_ready = m.counter("sub_ready", TILES)
        exp_ready = m.counter("exp_ready", TILES)
        den_ready = m.counter("den_ready", TILES)
        rden_ready = m.counter("rden_ready", TILES)
        p_ready = m.counter("p_ready", TILES)
        pt_ready = m.counter("pt_ready", TILES)
        pt_copied = m.counter("pt_copied", TILES)
        pv_done = m.counter("pv_done", TILES)
        o_copied = m.counter("o_copied", PAIRS)
        wo_done = m.counter("wo_done")
        x1_ready = m.counter("x1_ready")
        fs_ready = m.counter("fs_ready", 2)
        mean_ready = m.counter("mean_ready")
        cen_ready = m.counter("cen_ready")
        csq_ready = m.counter("csq_ready")
        var_ready = m.counter("var_ready")
        lv_ready = m.counter("lv_ready")
        rstd_ready = m.counter("rstd_ready")
        xh_ready = m.counter("xh_ready")
        xn_ready = m.counter("xn_ready")
        gate_up_ready = m.counter("gate_up_ready", HT)
        up_ready = m.counter("up_ready", HT)
        gate_ready = m.counter("gate_ready", HT)
        hid_ready = m.counter("hid_ready", HT)
        down_ready = m.counter("down_ready")
        x_done = m.counter("x_done")

        block = ctx.enter_context(nc.Block())
        N_FIXED, N_QKV, N_FFN = 2, 2, 4
        LEAD = SEQS
        V_STEPS = {0: (0, 0), 1: (0, 4), 3: (1, 0), 4: (1, 4)}

        def tokens(b):
            return bass.ds(b * T, T)

        @block.sync
        def _(sp):
            sp.dma_start(base[:, :, :], w["tables"]).then_inc(fixed_loaded.sem, 16)
            sp.dma_start(mask[:, :, :], w["mask"]).then_inc(fixed_loaded.sem, 16)
            with sp.Fori(0, DEPTH) as l:
                sp.wait_ge(qkv_free.sem, l + 1)
                sp.dma_start(w_qkv[:, :], w["w_qkv"][bass.ds(l, 1), :, :].rearrange("a p n -> p (a n)"))\
                  .then_inc(qkv_loaded.sem, 16)
                sp.dma_start(chan_a[:, :], w["chan_a"][bass.ds(l, 1), :, :].rearrange("a p n -> p (a n)"))\
                  .then_inc(qkv_loaded.sem, 16)
                sp.wait_ge(x_done.sem, l * SEQS + LEAD)
                sp.dma_start(w_o[:, :, :], w["w_o"][bass.ds(l, 1), :, :, :].rearrange("a p k n -> p (a k) n"))\
                  .then_inc(ffn_loaded.sem, 16)
                sp.dma_start(w_1[:, :], w["w1"][bass.ds(l, 1), :, :].rearrange("a p n -> p (a n)"))\
                  .then_inc(ffn_loaded.sem, 16)
                sp.dma_start(w_2[:, :, :], w["w2"][bass.ds(l, 1), :, :, :].rearrange("a p k n -> p (a k) n"))\
                  .then_inc(ffn_loaded.sem, 16)
                sp.dma_start(chan[:, :], w["chan"][bass.ds(l, 1), :, :].rearrange("a p n -> p (a n)"))\
                  .then_inc(ffn_loaded.sem, 16)
            sp.wait_ge(qkv_loaded.sem, 16 * N_QKV * DEPTH)
            sp.wait_ge(ffn_loaded.sem, 16 * N_FFN * DEPTH)

        @block.tensor
        def _(pe):
            def values(it, p):
                f, t0 = V_STEPS[p]
                for i in range(4):
                    k = 4 * sorted(V_STEPS).index(p) + i
                    mm = pe.matmul(bank[i][0:KB, :], xs[:, (t0 + i) * QB:(t0 + i) * QB + KB],
                                   w_qkv[:, 2 * INNER + f * 512:2 * INNER + (f + 1) * 512],
                                   start=True, stop=True)
                    mm.then_inc(v_ready.sem, 1)

            def project(it, p, j, first):
                k = 2 * p + j
                if p in V_STEPS:
                    pe.wait_ge(v_copied.sem, v_copied.at(it, 4 * sorted(V_STEPS).index(p) + 2 * (j + 1)))
                elif not first or p >= 1:
                    pe.wait_ge(t_ready.sem, t_ready.at(it, 2 * (k - 1)))
                col = j * INNER + p * P
                pe.matmul(bank[2 * j][:, :], w_qkv[:, col:col + P], xs[:, LOOK:], start=True, stop=True)
                pe.matmul(bank[2 * j + 1][:, :], w_rot[:, col:col + P], xs[:, LOOK:],
                          start=True, stop=True).then_inc(rt_ready.sem, 1)

            def norm(it, p, j, first):
                k = 2 * p + j
                pe.wait_ge(sq_ready.sem, sq_ready.at(it, k + 1))
                if not first or k >= 1:
                    pe.wait_ge(guarded.sem, guarded.at(it, k))
                pe.matmul(bank[4][:, :], const["heads"][:, :], sq[:, j, :],
                          start=True, stop=True).then_inc(n_ready.sem, 1)

            def scores(it, p, f, first):
                g = 2 * p + f
                if f == 0:
                    pe.wait_ge(rotated.sem, rotated.at(it, 2 * p + 2))
                if not first or g >= 1:
                    pe.wait_ge(masked.sem, masked.at(it, g))
                pe.nop(nofuse=True)
                for i in range(HALF):
                    t = HALF * f + i
                    for a in range(2):
                        r = slice(a * HD, (a + 1) * HD)
                        mm = pe.matmul(bank[5][r, i * KB:(i + 1) * KB], qT[r, p % 2, t * QB:(t + 1) * QB],
                                       kT[r, p % 2, t * QB:t * QB + KB], start=True, stop=True,
                                       skip_group_check=True)
                mm.then_inc(s_ready.sem, 1)

            def turn(it, p, f, first):
                g = 2 * p + f
                pe.wait_ge(p_ready.sem, p_ready.at(it, g + 1))
                if not first or g >= 1:
                    pe.wait_ge(pt_copied.sem, pt_copied.at(it, g))
                for i in range(HALF):
                    mm = pe.transpose(bank[6][0:KB, i * P:(i + 1) * P], pn[:, f, i * KB:(i + 1) * KB],
                                      const["ident"][:, :])
                mm.then_inc(pt_ready.sem, 1)

            def mix(it, p, f, first):
                g = 2 * p + f
                if f == 0 and p in (0, 4):
                    pe.wait_ge(v_copied.sem, v_copied.at(it, 8 + 8 * (p // 4)))
                pe.wait_ge(pt_copied.sem, pt_copied.at(it, g + 1))
                if f == 0 and (not first or p >= 1):
                    pe.wait_ge(o_copied.sem, o_copied.at(it, p))
                pe.nop(nofuse=True)
                for i in range(HALF):
                    t = HALF * f + i
                    for a in range(2):
                        mm = pe.matmul(bank[7][a * HD:(a + 1) * HD, t * QB:(t + 1) * QB],
                                       vals[:, t, ((2 * p + a) * HD) % INNER:((2 * p + a) * HD) % INNER + HD],
                                       pT[:, f, i * P + a * QB:i * P + (a + 1) * QB],
                                       start=True, stop=True, skip_group_check=True)
                mm.then_inc(pv_done.sem, 1)

            def attention_out(it, ft, loads):
                pe.wait_ge(ffn_loaded.sem, loads)
                pe.wait_ge(o_copied.sem, o_copied.at(ft, PAIRS))
                pe.wait_ge(guarded.sem, guarded.at(it, 4) if it is not ft else guarded.at(ft, TILES))
                for p in range(PAIRS):
                    mm = pe.matmul(bank[4][:, :], w_o[:, p, :], oT[:, p, :], start=(p == 0), stop=(p == PAIRS - 1))
                mm.then_inc(wo_done.sem, 1)

            def mean(ft):
                pe.wait_ge(fs_ready.sem, fs_ready.at(ft, 2))
                pe.matmul(bank[4][:, :], const["mean"][:, :], fs[:, :], start=True, stop=True)\
                  .then_inc(mean_ready.sem, 1)

            def variance(ft):
                pe.wait_ge(csq_ready.sem, csq_ready.at(ft, 1))
                pe.matmul(bank[4][:, :], const["mean"][:, :], csq[:, :], start=True, stop=True)\
                  .then_inc(var_ready.sem, 1)

            def gate_up(ft, i):
                pe.wait_ge(xn_ready.sem, xn_ready.at(ft, 1))
                if i >= 1:
                    pe.wait_ge(gate_ready.sem, gate_ready.at(ft, i))
                c = 341 + i * HID
                pe.matmul(bank[4][0:HR[i], :], w_1[:, c:c + HR[i]], xn[:, :],
                          start=True, stop=True).then_inc(gate_up_ready.sem, 1)

            def linear_up(ft, i):
                if i == 0:
                    pe.wait_ge(gate_ready.sem, gate_ready.at(ft, HT))
                else:
                    pe.wait_ge(hid_ready.sem, hid_ready.at(ft, i))
                c = i * HID
                pe.matmul(bank[4][0:HR[i], :], w_1[:, c:c + HR[i]], xn[:, :],
                          start=True, stop=True).then_inc(up_ready.sem, 1)

            def down(ft):
                pe.wait_ge(hid_ready.sem, hid_ready.at(ft, HT))
                for i in range(HT):
                    mm = pe.matmul(bank[4][:, :], w_2[0:HR[i], i, :], hid[0:HR[i], i, :],
                                   start=(i == 0), stop=(i == HT - 1))
                mm.then_inc(down_ready.sem, 1)

            def body(it, first, loads):
                ft = it - 1
                for p in range(PAIRS):
                    if not first:
                        if p == 2:
                            attention_out(it, ft, loads)
                        if p >= 3:
                            pe.wait_ge(guarded.sem, guarded.at(it, 2 * p))
                    if p in V_STEPS:
                        if not first or p > 0:
                            pe.wait_ge(t_ready.sem, t_ready.at(it, 4 * p))
                        if p == 0:
                            pe.wait_ge(shifted.sem, shifted.at(it, 2))
                        values(it, p)
                    project(it, p, 0, first)
                    if not first:
                        if p == 3:
                            mean(ft)
                        if p == 4:
                            variance(ft)
                        if p == 5:
                            gate_up(ft, 0)
                        if p == 6:
                            linear_up(ft, 0)
                    if not first or p >= 2:
                        turn(it, p - 2, 0, first)
                    project(it, p, 1, first)
                    if not first:
                        if p == 5:
                            gate_up(ft, 1)
                        if p == 6:
                            linear_up(ft, 1)
                        if p == 7:
                            down(ft)
                    if not first or p >= 2:
                        mix(it, p - 2, 0, first)
                        turn(it, p - 2, 1, first)
                    if not first:
                        if p == 5:
                            gate_up(ft, 2)
                        if p == 6:
                            linear_up(ft, 2)
                    if not first or p >= 1:
                        scores(it, p - 1, 0, first)
                    if not first:
                        if p == 2:
                            pe.wait_ge(x1_ready.sem, x1_ready.at(ft, 1))
                        if p == 3:
                            pe.wait_ge(cen_ready.sem, cen_ready.at(ft, 1))
                        if p == 4:
                            pe.wait_ge(lv_ready.sem, lv_ready.at(ft, 1))
                        if p == 5:
                            pe.wait_ge(gate_ready.sem, gate_ready.at(ft, HT))
                        if p == 6:
                            pe.wait_ge(hid_ready.sem, hid_ready.at(ft, HT))
                        if p == 7:
                            pe.wait_ge(x_done.sem, ft + LEAD + 1)
                    norm(it, p, 0, first)
                    if not first or p >= 2:
                        mix(it, p - 2, 1, first)
                    norm(it, p, 1, first)
                    if not first or p >= 1:
                        scores(it, p - 1, 1, first)

            def rest(it, loads):
                ft = it - 1
                turn(it, -2, 0, False)
                mix(it, -2, 0, False)
                turn(it, -2, 1, False)
                mix(it, -2, 1, False)
                scores(it, -1, 0, False)
                scores(it, -1, 1, False)
                turn(it, -1, 0, False)
                mix(it, -1, 0, False)
                turn(it, -1, 1, False)
                mix(it, -1, 1, False)
                attention_out(ft, ft, loads)
                mean(ft)
                variance(ft)
                for i in range(HT):
                    gate_up(ft, i)
                for i in range(HT):
                    linear_up(ft, i)
                down(ft)

            with pe.Fori(0, DEPTH) as l:
                pe.wait_ge(x_done.sem, l * SEQS + LEAD)
                pe.wait_ge(qkv_loaded.sem, (l + 1) * (16 * N_QKV))
                pe.wait_ge(rot_weights.sem, rot_weights.at(l, 4))
                loads = (l + 1) * (16 * N_FFN)
                body(l * SEQS, True, loads)
                pe.nop(nofuse=True)
                with pe.Fori(1, SEQS) as b:
                    body(l * SEQS + b, False, loads)
                rest((l + 1) * SEQS, loads)

        @block.scalar
        def _(act):
            def square(it, p, j, first):
                k = 2 * p + j
                act.wait_ge(rt_ready.sem, rt_ready.at(it, k + 1))
                if not first or p >= 1:
                    act.wait_ge(n_ready.sem, n_ready.at(it, k - 1))
                act.activation(sq[:, j, :], bank[2 * j][:, :], ACT.Square).then_inc(sq_ready.sem, 1)

            def inverse_norm(it, p, j, first):
                k = 2 * p + j
                act.wait_ge(guarded.sem, guarded.at(it, k + 1))
                act.activation(lnn[:, j, :], nrm[:, j, :], ACT.Ln, scale=NORM_SHIFT).then_inc(ln_ready.sem, 1)
                act.wait_ge(ln_ready.sem, ln_ready.at(it, k + 1))
                if not first or p >= 1:
                    act.wait_ge(rotated.sem, rotated.at(it, k - 1))
                act.activation(rn[:, j, :], lnn[:, j, :], ACT.Exp, scale=-0.5,
                               bias=const["unshift"][:, 0:1]).then_inc(rn_ready.sem, 1)

            def exponential(it, p, f, first):
                g = 2 * p + f
                act.wait_ge(sub_ready.sem, sub_ready.at(it, g + 1))
                if not first or p >= 1:
                    act.wait_ge(p_ready.sem, p_ready.at(it, g - 1))
                act.activation(pr[:, f, :], sc[:, f, :], ACT.Exp, scale=QK_SCALE).then_inc(exp_ready.sem, 1)

            def copy_turned(it, p, f, first):
                g = 2 * p + f
                act.wait_ge(pt_ready.sem, pt_ready.at(it, g + 1))
                if not first or p >= 1:
                    act.wait_ge(pv_done.sem, pv_done.at(it, g - 1))
                act.activation(pT[:, f, :], bank[6][0:KB, :], ACT.Copy).then_inc(pt_copied.sem, 1)

            def copy_mixed(it, p, first):
                act.wait_ge(pv_done.sem, pv_done.at(it, 2 * p + 2))
                if p == 0 and not first:
                    act.wait_ge(wo_done.sem, wo_done.at(it, 0))
                act.activation(oT[:, p % PAIRS, :], bank[7][:, :], ACT.Copy).then_inc(o_copied.sem, 1)

            def copy_values(it, p):
                f, t0 = V_STEPS[p]
                for i in range(4):
                    act.wait_ge(v_ready.sem, v_ready.at(it, 4 * sorted(V_STEPS).index(p) + i + 1))
                    act.activation(vals[:, t0 + i, f * 512:(f + 1) * 512], bank[i][0:KB, :],
                                   ACT.Copy).then_inc(v_copied.sem, 1)

            def center_square(ft):
                act.wait_ge(cen_ready.sem, cen_ready.at(ft, 1))
                act.activation(csq[:, :], cen[:, :], ACT.Square).then_inc(csq_ready.sem, 1)

            def inverse_deviation(ft):
                act.wait_ge(var_ready.sem, var_ready.at(ft, 1))
                act.activation(lv[:, :], bank[4][:, :], ACT.Ln, bias=const["eps"][:, 0:1]).then_inc(lv_ready.sem, 1)
                act.wait_ge(lv_ready.sem, lv_ready.at(ft, 1))
                act.activation(rstd[:, :], lv[:, :], ACT.Exp, scale=-0.5).then_inc(rstd_ready.sem, 1)

            def gelu(ft, i):
                r = slice(0, HR[i])
                act.wait_ge(gate_up_ready.sem, gate_up_ready.at(ft, i + 1))
                act.activation(hid[r, i, :], bank[4][r, :], ACT.Gelu,
                               bias=chan[r, 6 + i:7 + i]).then_inc(gate_ready.sem, 1)

            def body(it, first):
                ft = it - 1
                act.preload_act_table_set(EXP_LN_SET)
                for p in range(PAIRS):
                    if p == 5 and not first:
                        act.preload_act_table_set(GELU_SET)
                    if p in V_STEPS:
                        copy_values(it, p)
                    square(it, p, 0, first)
                    if p == 5 and not first:
                        gelu(ft, 0)
                    if not first or p >= 2:
                        copy_turned(it, p - 2, 0, first)
                    square(it, p, 1, first)
                    if p == 5 and not first:
                        gelu(ft, 1)
                    if not first or p >= 2:
                        copy_turned(it, p - 2, 1, first)
                    if not first:
                        if p == 4:
                            inverse_deviation(ft)
                        if p == 5:
                            gelu(ft, 2)
                            act.preload_act_table_set(EXP_LN_SET)
                    if not first or p >= 1:
                        exponential(it, p - 1, 0, first)
                    inverse_norm(it, p, 0, first)
                    if not first or p >= 2:
                        copy_mixed(it, p - 2, first)
                    inverse_norm(it, p, 1, first)
                    if not first or p >= 1:
                        exponential(it, p - 1, 1, first)
                    if p == 3 and not first:
                        center_square(ft)

            def rest(it):
                ft = it - 1
                act.preload_act_table_set(EXP_LN_SET)
                copy_turned(it, -2, 0, False)
                copy_turned(it, -2, 1, False)
                copy_mixed(it, -2, False)
                exponential(it, -1, 0, False)
                exponential(it, -1, 1, False)
                copy_turned(it, -1, 0, False)
                copy_turned(it, -1, 1, False)
                copy_mixed(it, -1, False)
                center_square(ft)
                inverse_deviation(ft)
                act.preload_act_table_set(GELU_SET)
                for i in range(HT):
                    gelu(ft, i)

            act.wait_ge(zeroed.sem, 5)
            with act.Fori(0, DEPTH) as l:
                act.wait_ge(x_done.sem, l * SEQS + LEAD)
                act.nop(nofuse=True)
                body(l * SEQS, True)
                act.wait_ge(ffn_loaded.sem, (l + 1) * (16 * N_FFN))
                act.nop(nofuse=True)
                with act.Fori(1, SEQS) as b:
                    body(l * SEQS + b, False)
                rest((l + 1) * SEQS)

        @block.vector
        def _(ve):
            def rotate(it, p, j, first):
                k = 2 * p + j
                ve.wait_ge(rt_ready.sem, rt_ready.at(it, k + 1))
                if not first or p >= 1:
                    ve.wait_ge(rotated.sem, rotated.at(it, k - 1))
                ve.tensor_tensor(t2[:, j, :], bank[2 * j + 1][:, :], table[:, 2 * j + 1, :],
                                 ALU.mult).then_inc(t_ready.sem, 1)
                ve.wait_ge(sq_ready.sem, sq_ready.at(it, k + 1))
                ve.tensor_tensor(t1[:, j, :], bank[2 * j][:, :], table[:, 2 * j, :], ALU.mult).then_inc(t_ready.sem, 1)

            def guard(it, p, j, first):
                k = 2 * p + j
                ve.wait_ge(n_ready.sem, n_ready.at(it, k + 1))
                if not first or p >= 1:
                    ve.wait_ge(ln_ready.sem, ln_ready.at(it, k - 1))
                ve.tensor_scalar(nrm[:, j, :], bank[4][:, :], 1e-24, None, ALU.max).then_inc(guarded.sem, 1)

            def center(it, p, f, first):
                g = 2 * p + f
                sc3 = sc[:, f, :].rearrange("p (i k) -> p i k", k=KB)
                ve.wait_ge(s_ready.sem, s_ready.at(it, g + 1))
                if not first or p >= 1:
                    ve.wait_ge(exp_ready.sem, exp_ready.at(it, g - 1))
                ve.tensor_tensor(sc[:, f, :], bank[5][:, 0:HALF * KB], mask[:, f, :], ALU.add).then_inc(masked.sem, 1)
                ve.wait_ge(masked.sem, masked.at(it, g + 1))
                ve.tensor_reduce(mx[:, f, :], sc3, AX.X, ALU.max).then_inc(mx_ready.sem, 1)
                ve.wait_ge(mx_ready.sem, mx_ready.at(it, g + 1))
                ve.tensor_tensor(sc3, sc3, mx[:, f, :].unsqueeze(2).to_broadcast([P, HALF, KB]),
                                 ALU.subtract).then_inc(sub_ready.sem, 1)

            def denominator(it, p, f, first):
                g = 2 * p + f
                ve.wait_ge(exp_ready.sem, exp_ready.at(it, g + 1))
                ve.tensor_reduce(den[:, f, :], pr[:, f, :].rearrange("p (i k) -> p i k", k=KB), AX.X,
                                 ALU.add).then_inc(den_ready.sem, 1)
                ve.wait_ge(den_ready.sem, den_ready.at(it, g + 1))
                if not first or p >= 1:
                    ve.wait_ge(p_ready.sem, p_ready.at(it, g - 1))
                ve.reciprocal(rden[:, f, :], den[:, f, :]).then_inc(rden_ready.sem, 1)

            def residual(ft, b):
                ve.wait_ge(wo_done.sem, wo_done.at(ft, 1))
                ve.tensor_tensor(xT[:, tokens(b)], bank[4][:, :], xT[:, tokens(b)], ALU.add).then_inc(x1_ready.sem, 1)
                ve.wait_ge(x1_ready.sem, x1_ready.at(ft, 1))
                ve.nop(nofuse=True)
                ve.tensor_copy(fs[0:HD, :], xT[0:HD, tokens(b)]).then_inc(fs_ready.sem, 1)
                ve.tensor_copy(fs[HD:P, 1:], xT[HD:P, bass.ds(b * T, T - 1)]).then_inc(fs_ready.sem, 1)

            def subtract_mean(ft):
                ve.wait_ge(fs_ready.sem, fs_ready.at(ft, 2))
                ve.wait_ge(mean_ready.sem, mean_ready.at(ft, 1))
                ve.tensor_tensor(cen[:, :], fs[:, :], bank[4][:, :], ALU.subtract).then_inc(cen_ready.sem, 1)

            def scale_normed(ft):
                ve.wait_ge(rstd_ready.sem, rstd_ready.at(ft, 1))
                ve.tensor_tensor(xn[:, :], cen[:, :], rstd[:, :], ALU.mult).then_inc(xh_ready.sem, 1)
                ve.wait_ge(xh_ready.sem, xh_ready.at(ft, 1))
                ve.tensor_scalar(xn[:, :], xn[:, :], chan[:, 0:1], chan[:, 1:2], ALU.mult, ALU.add)\
                  .then_inc(xn_ready.sem, 1)

            def gated(ft, i):
                r = slice(0, HR[i])
                ve.wait_ge(gate_ready.sem, gate_ready.at(ft, i + 1))
                ve.wait_ge(up_ready.sem, up_ready.at(ft, i + 1))
                ve.scalar_tensor_tensor(out=hid[r, i, :], in0=bank[4][r, :], scalar=chan[r, 3 + i:4 + i],
                                        in1=hid[r, i, :], op0=ALU.add, op1=ALU.mult)\
                  .then_inc(hid_ready.sem, 1)

            def finish(ft, b):
                ve.wait_ge(down_ready.sem, down_ready.at(ft, 1))
                ve.scalar_tensor_tensor(out=xT[:, tokens(b)], in0=bank[4][:, :], scalar=chan[:, 2:3],
                                        in1=xT[:, tokens(b)], op0=ALU.add, op1=ALU.add).then_inc(x_done.sem, 1)

            def shift(b):
                ve.tensor_copy(xs[0:HD, LOOK:], xT[0:HD, tokens(b)]).then_inc(shifted.sem, 1)
                ve.tensor_copy(xs[HD:P, LOOK + 1:], xT[HD:P, bass.ds(b * T, T - 1)]).then_inc(shifted.sem, 1)

            def body(it, b, first):
                ft = it - 1
                for p in range(PAIRS):
                    rotate(it, p, 0, first)
                    if p == 6 and not first:
                        gated(ft, 0)
                    rotate(it, p, 1, first)
                    if not first:
                        if p == 2:
                            residual(ft, b - 1)
                        if p == 3:
                            subtract_mean(ft)
                        if p == 6:
                            gated(ft, 1)
                            gated(ft, 2)
                        if p == 7:
                            finish(ft, b - 1)
                    if p == 7:
                        ve.wait_ge(x_done.sem, it + 2)
                        ve.wait_ge(rt_ready.sem, rt_ready.at(it, TILES))
                        ve.nop(nofuse=True)
                        shift(1 if first else (b + 1) % SEQS)
                    if not first or p >= 1:
                        center(it, p - 1, 0, first)
                    guard(it, p, 0, first)
                    if not first or p >= 1:
                        denominator(it, p - 1, 0, first)
                    guard(it, p, 1, first)
                    if not first or p >= 1:
                        center(it, p - 1, 1, first)
                        denominator(it, p - 1, 1, first)
                    if p == 4 and not first:
                        scale_normed(ft)

            def rest(it):
                ft = it - 1
                center(it, -1, 0, False)
                ve.memset(flag[:, :], 0.0).then_inc(qkv_free.sem, 1)
                center(it, -1, 1, False)
                denominator(it, -1, 0, False)
                denominator(it, -1, 1, False)
                residual(ft, SEQS - 1)
                subtract_mean(ft)
                scale_normed(ft)
                for i in range(HT):
                    gated(ft, i)
                finish(ft, SEQS - 1)

            ve.memset(flag[:, :], 0.0).then_inc(qkv_free.sem, 1)
            ve.memset(xs[:, 0:LOOK], 0.0).then_inc(zeroed.sem, 1)
            ve.memset(xs[HD:P, LOOK:LOOK + 1], 0.0).then_inc(zeroed.sem, 1)
            ve.memset(fs[HD:P, 0:1], 0.0).then_inc(zeroed.sem, 1)
            ve.memset(kT[:, :, 0:LOOK], 0.0).then_inc(zeroed.sem, 1)
            ve.tensor_copy(x0T[:, :], xT[:, :]).then_inc(zeroed.sem, 1)
            ve.wait_ge(zeroed.sem, 5)
            ve.sem_inc(x_done.sem, LEAD)
            shift(0)
            with ve.Fori(0, DEPTH) as l:
                ve.wait_ge(x_done.sem, l * SEQS + LEAD)
                ve.wait_ge(tables_ready.sem, tables_ready.at(l, 4))
                ve.nop(nofuse=True)
                body(l * SEQS, 0, True)
                ve.wait_ge(ffn_loaded.sem, (l + 1) * (16 * N_FFN))
                ve.nop(nofuse=True)
                with ve.Fori(1, SEQS) as b:
                    body(l * SEQS + b, b, False)
                rest((l + 1) * SEQS)

        @block.gpsimd
        def _(pool):
            def join(it, p, j):
                k = 2 * p + j
                pool.wait_ge(t_ready.sem, t_ready.at(it, 2 * k + 2))
                pool.tensor_tensor(t1[:, j, :], t1[:, j, :], t2[:, j, :], ALU.add).then_inc(added.sem, 1)

            def normalise(it, p, j, first):
                k = 2 * p + j
                pool.wait_ge(rn_ready.sem, rn_ready.at(it, k + 1))
                pool.wait_ge(added.sem, added.at(it, k + 1))
                if not first or p >= 2:
                    pool.wait_ge(s_ready.sem, s_ready.at(it, 2 * (p - 2) + 2))
                dst = kT[:, p % 2, LOOK:] if j else qT[:, p % 2, :]
                pool.tensor_tensor(dst, t1[:, j, :], rn[:, j, :], ALU.mult).then_inc(rotated.sem, 1)

            def probabilities(it, p, f, first):
                g = 2 * p + f
                pool.wait_ge(rden_ready.sem, rden_ready.at(it, g + 1))
                if not first or p >= 1:
                    pool.wait_ge(pt_ready.sem, pt_ready.at(it, g - 1))
                pool.tensor_tensor(pn[:, f, :].rearrange("p (i k) -> p i k", k=KB),
                                   pr[:, f, :].rearrange("p (i k) -> p i k", k=KB),
                                   rden[:, f, :].unsqueeze(2).to_broadcast([P, HALF, KB]),
                                   ALU.mult).then_inc(p_ready.sem, 1)

            def body(it, first):
                for p in range(PAIRS):
                    join(it, p, 0)
                    join(it, p, 1)
                    if not first or p >= 1:
                        probabilities(it, p - 1, 0, first)
                    normalise(it, p, 0, first)
                    normalise(it, p, 1, first)
                    if not first or p >= 1:
                        probabilities(it, p - 1, 1, first)

            pool.wait_ge(zeroed.sem, 5)
            pool.wait_ge(fixed_loaded.sem, 16 * N_FIXED)
            with pool.Fori(0, DEPTH) as l:
                pool.wait_ge(qkv_free.sem, l + 1)
                pool.wait_ge(qkv_loaded.sem, (l + 1) * (16 * N_QKV))
                pool.nop(nofuse=True)
                src = w_qkv[:, 0:2 * INNER].rearrange("p (h s c) -> p h s c", s=2, c=HD // 2)
                dst = w_rot[:, :].rearrange("p (h s c) -> p h s c", s=2, c=HD // 2)
                for s in range(2):
                    for j in range(2):
                        h = slice(j * PAIRS * 2, (j + 1) * PAIRS * 2)
                        pool.tensor_copy(dst[:, h, s, :], src[:, h, 1 - s, :]).then_inc(rot_weights.sem, 1)
                for i in range(4):
                    pool.tensor_scalar(table[:, i, :], base[:, i, :], chan_a[:, i:i + 1], None,
                                       ALU.mult).then_inc(tables_ready.sem, 1)
                body(l * SEQS, True)
                pool.nop(nofuse=True)
                with pool.Fori(1, SEQS) as b:
                    body(l * SEQS + b, False)
                probabilities((l + 1) * SEQS, -1, 0, False)
                probabilities((l + 1) * SEQS, -1, 1, False)


def layer_norm_phase(nc, prefix, xT, x0T, const):
    with ExitStack() as ctx:
        m = Memory(ctx, nc, prefix)
        res = m.sb("res", [P, T])
        cen = m.sb("cen", [P, T])
        sq = m.sb("sq", [P, T])
        lv = m.sb("lv", [P, T])
        rstd = m.sb("rstd", [P, T])
        bank = [m.bank(f"bank{i}") for i in range(2)]
        res_ready, mean_ready, cen_ready = m.counter("res_ready"), m.counter("mean_ready"), m.counter("cen_ready")
        sq_ready, var_ready, lv_ready = m.counter("sq_ready"), m.counter("var_ready"), m.counter("lv_ready")
        rstd_ready, x_written = m.counter("rstd_ready"), m.counter("x_written")
        block = ctx.enter_context(nc.Block())

        @block.tensor
        def _(pe):
            with pe.Fori(0, SEQS) as b:
                pe.wait_ge(res_ready.sem, b + 1)
                pe.matmul(bank[0][:, :], const["mean"][:, :], res[:, :], start=True, stop=True).then_inc(mean_ready.sem, 1)
                pe.wait_ge(sq_ready.sem, b + 1)
                pe.matmul(bank[1][:, :], const["mean"][:, :], sq[:, :], start=True, stop=True).then_inc(var_ready.sem, 1)

        @block.scalar
        def _(act):
            with act.Fori(0, SEQS) as b:
                act.preload_act_table_set(EXP_LN_SET)
                act.wait_ge(cen_ready.sem, b + 1)
                act.activation(sq[:, :], cen[:, :], ACT.Square).then_inc(sq_ready.sem, 1)
                act.wait_ge(var_ready.sem, b + 1)
                act.activation(lv[:, :], bank[1][:, :], ACT.Ln, bias=const["eps"][:, 0:1]).then_inc(lv_ready.sem, 1)
                act.wait_ge(lv_ready.sem, b + 1)
                act.activation(rstd[:, :], lv[:, :], ACT.Exp, scale=-0.5).then_inc(rstd_ready.sem, 1)

        @block.vector
        def _(ve):
            with ve.Fori(0, SEQS) as b:
                x = xT[:, bass.ds(b * T, T)]
                ve.tensor_tensor(res[:, :], x, x0T[:, bass.ds(b * T, T)], ALU.add).then_inc(res_ready.sem, 1)
                ve.wait_ge(res_ready.sem, b + 1)
                ve.wait_ge(mean_ready.sem, b + 1)
                ve.tensor_tensor(cen[:, :], res[:, :], bank[0][:, :], ALU.subtract).then_inc(cen_ready.sem, 1)
                ve.wait_ge(cen_ready.sem, b + 1)
                ve.wait_ge(rstd_ready.sem, b + 1)
                ve.tensor_tensor(x, cen[:, :], rstd[:, :], ALU.mult).then_inc(x_written.sem, 1)



def expert_phase(nc, prefix, xT, const, w, out):
    EXPERTS = 8
    ET = 12
    TB = T // P
    with ExitStack() as ctx:
        m = Memory(ctx, nc, prefix)
        wr = m.sb("wr", [P, EXPERTS])
        w1 = m.sb("w1", [P, ET * P])
        w3 = m.sb("w3", [P, ET * P])
        w2 = m.sb("w2", [P, ET, P])
        owner = m.sb("owner", [72, ET, P], BF16)
        part = m.sb("part", [P, 2])
        iota = m.sb("iota", [P, EXPERTS])
        xm = m.sb("xm", [P, T])
        logit = m.sb("logit", [P, TB, EXPERTS])
        top = m.sb("top", [P, TB, 8])
        topi = m.sb("topi", [P, TB, 8], U32)
        topf = m.sb("topf", [P, TB, 8])
        gap = m.sb("gap", [P, TB])
        eg = m.sb("eg", [P, TB])
        sg = m.sb("sg", [P, TB])
        wt = m.sb("wt", [P, 2, TB])
        first = m.sb("first", [P, TB, EXPERTS])
        second = m.sb("second", [P, TB, EXPERTS])
        comb3 = m.sb("comb3", [P, TB, 96])
        part_a = m.sb("part_a", [72, T], BF16)
        rest_a = m.sb("rest_a", [72, T])
        part_b = m.sb("part_b", [72, T], BF16)
        combT = m.sb("combT", [72, T], BF16)
        act_h = m.sb("act_h", [P, 2, T])
        prod = m.sb("prod", [P, 2, T])
        hid = m.sb("hid", [P, 2, T])
        res = m.sb("res", [P, T])
        cen = m.sb("cen", [P, T])
        sq = m.sb("sq", [P, T])
        lv = m.sb("lv", [P, T])
        rstd = m.sb("rstd", [P, T])
        fin = m.sb("fin", [P, T])
        bank = [m.bank(f"bank{i}") for i in range(8)]

        loaded = m.counter("loaded")
        comb_zeroed = m.counter("comb_zeroed")
        xm_ready = m.counter("xm_ready")
        logits_ready = m.counter("logits_ready")
        logit_copied = m.counter("logit_copied")
        top_ready = m.counter("top_ready", TB)
        topi_ready = m.counter("topi_ready", TB)
        gap_ready = m.counter("gap_ready", 2)
        eg_ready = m.counter("eg_ready")
        wt_steps = m.counter("wt_steps", 3)
        chosen = m.counter("chosen", 2 * TB)
        comb_ready = m.counter("comb_ready", 3)
        comb_turned = m.counter("comb_turned")
        split_steps = m.counter("split_steps", 4)
        h_ready = m.counter("h_ready", ET)
        g_ready = m.counter("g_ready", ET)
        cb_ready = m.counter("cb_ready", ET)
        silu_ready = m.counter("silu_ready", ET)
        prod_ready = m.counter("prod_ready", ET)
        hid_ready = m.counter("hid_ready", ET)
        hid_used = m.counter("hid_used", ET)
        res_ready = m.counter("res_ready")
        mean_ready = m.counter("mean_ready")
        cen_ready = m.counter("cen_ready")
        sq_ready = m.counter("sq_ready")
        var_ready = m.counter("var_ready")
        lv_ready = m.counter("lv_ready")
        rstd_ready = m.counter("rstd_ready")
        fin_ready = m.counter("fin_ready")
        stored = m.counter("stored")

        block = ctx.enter_context(nc.Block())
        N_LOADS = 7

        @block.sync
        def _(sp):
            for dst, name in ((wr, "wr"), (w1, "w1"), (w3, "w3"), (part, "part"), (iota, "iota")):
                sp.dma_start(dst[:, :], w[name]).then_inc(loaded.sem, 16)
            for dst, name in ((w2, "w2"), (owner, "owner")):
                sp.dma_start(dst[:, :, :], w[name]).then_inc(loaded.sem, 16)
            with sp.Fori(0, SEQS) as b:
                sp.wait_ge(fin_ready.sem, b + 1)
                sp.dma_start(out[:, bass.ds(b * T, T)], fin[:, :]).then_inc(stored.sem, 16)
            sp.wait_ge(loaded.sem, 16 * N_LOADS)
            sp.wait_ge(stored.sem, 16 * SEQS + 1)

        @block.tensor
        def _(pe):
            pe.wait_ge(loaded.sem, 16 * N_LOADS)
            with pe.Fori(0, SEQS) as b:
                pe.wait_ge(xm_ready.sem, b + 1)
                for t in range(TB):
                    mm = pe.matmul(bank[7][:, t * EXPERTS:(t + 1) * EXPERTS], xm[:, t * P:(t + 1) * P], wr[:, :],
                                   start=True, stop=True, skip_group_check=True)
                mm.then_inc(logits_ready.sem, 1)
                pe.wait_ge(comb_ready.sem, comb_ready.at(b, 3))
                for t in range(TB):
                    mm = pe.transpose(bank[7][0:96, t * P:(t + 1) * P], comb3[:, t, :], const["ident"][:, :])
                mm.then_inc(comb_turned.sem, 1)
                pe.wait_ge(split_steps.sem, split_steps.at(b, 4))

                def down(j):
                    pe.wait_ge(hid_ready.sem, hid_ready.at(b, j + 1))
                    pe.matmul(bank[6][:, :], w2[:, j, :], hid[:, j % 2, :],
                              start=(j == 0), stop=(j == ET - 1)).then_inc(hid_used.sem, 1)

                for j in range(ET):
                    if j >= 2:
                        pe.wait_ge(hid_ready.sem, hid_ready.at(b, j - 1))
                    pe.matmul(bank[j % 2][:, :], w1[:, j * P:(j + 1) * P], xm[:, :],
                              start=True, stop=True).then_inc(h_ready.sem, 1)
                    pe.matmul(bank[2 + j % 2][:, :], w3[:, j * P:(j + 1) * P], xm[:, :],
                              start=True, stop=True).then_inc(g_ready.sem, 1)
                    pe.matmul(bank[4 + j % 2][:, :], owner[:, j, :], combT[:, :],
                              start=True, stop=True).then_inc(cb_ready.sem, 1)
                    if j >= 1:
                        down(j - 1)
                down(ET - 1)
                pe.wait_ge(res_ready.sem, b + 1)
                pe.matmul(bank[0][:, :], const["mean"][:, :], res[:, :], start=True, stop=True).then_inc(mean_ready.sem, 1)
                pe.wait_ge(sq_ready.sem, b + 1)
                pe.matmul(bank[1][:, :], const["mean"][:, :], sq[:, :], start=True, stop=True).then_inc(var_ready.sem, 1)

        @block.scalar
        def _(act):
            with act.Fori(0, SEQS) as b:
                act.preload_act_table_set(EXP_LN_SET)
                act.wait_ge(gap_ready.sem, gap_ready.at(b, 1))
                act.activation(eg[:, :], gap[:, :], ACT.Exp).then_inc(eg_ready.sem, 1)
                act.wait_ge(comb_turned.sem, b + 1)
                act.activation(part_a[:, :], bank[7][0:72, :], ACT.Copy).then_inc(split_steps.sem, 1)
                for j in range(ET):
                    act.wait_ge(h_ready.sem, h_ready.at(b, j + 1))
                    if j >= 2:
                        act.wait_ge(prod_ready.sem, prod_ready.at(b, j - 1))
                    act.activation(act_h[:, j % 2, :], bank[j % 2][:, :], ACT.Silu).then_inc(silu_ready.sem, 1)
                act.preload_act_table_set(EXP_LN_SET)
                act.wait_ge(cen_ready.sem, b + 1)
                act.activation(sq[:, :], cen[:, :], ACT.Square).then_inc(sq_ready.sem, 1)
                act.wait_ge(var_ready.sem, b + 1)
                act.activation(lv[:, :], bank[1][:, :], ACT.Ln, bias=const["eps"][:, 0:1]).then_inc(lv_ready.sem, 1)
                act.wait_ge(lv_ready.sem, b + 1)
                act.activation(rstd[:, :], lv[:, :], ACT.Exp, scale=-0.5).then_inc(rstd_ready.sem, 1)

        @block.vector
        def _(ve):
            ve.memset(comb3[:, :, :], 0.0).then_inc(comb_zeroed.sem, 1)
            ve.wait_ge(loaded.sem, 16 * N_LOADS)
            ve.wait_ge(comb_zeroed.sem, 1)
            ve.sem_inc(stored.sem, 1)
            with ve.Fori(0, SEQS) as b:
                ve.tensor_copy(xm[:, :], xT[:, bass.ds(b * T, T)]).then_inc(xm_ready.sem, 1)
                ve.wait_ge(logits_ready.sem, b + 1)
                ve.tensor_copy(logit[:, :, :], bank[7][:, 0:TB * EXPERTS].rearrange("p (t e) -> p t e", e=EXPERTS))\
                  .then_inc(logit_copied.sem, 1)
                ve.wait_ge(logit_copied.sem, b + 1)
                ve.nop(nofuse=True)
                for t in range(TB):
                    ve.max(top[:, t, :], logit[:, t, :]).then_inc(top_ready.sem, 1)
                ve.wait_ge(top_ready.sem, top_ready.at(b, TB))
                ve.nop(nofuse=True)
                for t in range(TB):
                    ve.max_index(topi[:, t, :], top[:, t, :], logit[:, t, :]).then_inc(topi_ready.sem, 1)
                ve.tensor_tensor(gap[:, :], top[:, :, 1], top[:, :, 0], ALU.subtract).then_inc(gap_ready.sem, 1)
                ve.wait_ge(topi_ready.sem, topi_ready.at(b, TB))
                ve.tensor_copy(topf[:, :, :], topi[:, :, :]).then_inc(gap_ready.sem, 1)
                ve.wait_ge(eg_ready.sem, b + 1)
                ve.tensor_scalar(sg[:, :], eg[:, :], 1.0, None, ALU.add).then_inc(wt_steps.sem, 1)
                ve.wait_ge(wt_steps.sem, wt_steps.at(b, 1))
                ve.reciprocal(wt[:, 0, :], sg[:, :]).then_inc(wt_steps.sem, 1)
                ve.wait_ge(wt_steps.sem, wt_steps.at(b, 2))
                ve.tensor_tensor(wt[:, 1, :], wt[:, 0, :], eg[:, :], ALU.mult).then_inc(wt_steps.sem, 1)
                ve.wait_ge(wt_steps.sem, wt_steps.at(b, 3))
                ve.wait_ge(gap_ready.sem, gap_ready.at(b, 2))
                for k, dst in enumerate((first, second)):
                    for t in range(TB):
                        ve.tensor_scalar(dst[:, t, :], iota[:, :], topf[:, t, k:k + 1], wt[:, k, t:t + 1],
                                         ALU.is_equal, ALU.mult).then_inc(chosen.sem, 1)
                ve.wait_ge(chosen.sem, chosen.at(b, 2 * TB))
                for r in range(3):
                    ve.tensor_tensor(comb3[:, :, 32 * r:32 * r + EXPERTS], first[:, :, :], second[:, :, :],
                                     ALU.add).then_inc(comb_ready.sem, 1)
                ve.wait_ge(split_steps.sem, split_steps.at(b, 1))
                ve.scalar_tensor_tensor(out=rest_a[:, :], in0=part_a[:, :], scalar=part[0:72, 0:1],
                                        in1=bank[7][0:72, :], op0=ALU.mult, op1=ALU.add).then_inc(split_steps.sem, 1)
                ve.wait_ge(split_steps.sem, split_steps.at(b, 2))
                ve.tensor_copy(part_b[:, :], rest_a[:, :]).then_inc(split_steps.sem, 1)
                ve.wait_ge(split_steps.sem, split_steps.at(b, 3))
                ve.scalar_tensor_tensor(out=combT[:, :], in0=part_b[:, :], scalar=part[0:72, 1:2],
                                        in1=rest_a[:, :], op0=ALU.mult, op1=ALU.add).then_inc(split_steps.sem, 1)
                for j in range(ET):
                    ve.wait_ge(silu_ready.sem, silu_ready.at(b, j + 1))
                    ve.wait_ge(g_ready.sem, g_ready.at(b, j + 1))
                    ve.tensor_tensor(prod[:, j % 2, :], act_h[:, j % 2, :], bank[2 + j % 2][:, :],
                                     ALU.mult).then_inc(prod_ready.sem, 1)
                    ve.wait_ge(prod_ready.sem, prod_ready.at(b, j + 1))
                    ve.wait_ge(cb_ready.sem, cb_ready.at(b, j + 1))
                    if j >= 2:
                        ve.wait_ge(hid_used.sem, hid_used.at(b, j - 1))
                    ve.tensor_tensor(hid[:, j % 2, :], prod[:, j % 2, :], bank[4 + j % 2][:, :],
                                     ALU.mult).then_inc(hid_ready.sem, 1)
                ve.wait_ge(hid_used.sem, hid_used.at(b, ET))
                ve.tensor_tensor(res[:, :], bank[6][:, :], xm[:, :], ALU.add).then_inc(res_ready.sem, 1)
                ve.wait_ge(mean_ready.sem, b + 1)
                ve.wait_ge(res_ready.sem, b + 1)
                ve.tensor_tensor(cen[:, :], res[:, :], bank[0][:, :], ALU.subtract).then_inc(cen_ready.sem, 1)
                ve.wait_ge(rstd_ready.sem, b + 1)
                ve.wait_ge(stored.sem, b * 16 + 1)
                ve.tensor_tensor(fin[:, :], cen[:, :], rstd[:, :], ALU.mult).then_inc(fin_ready.sem, 1)



def build_program(nc, d, out):
    with ExitStack() as ctx:
        def sb(name, shape):
            return ctx.enter_context(nc.sbuf_tensor(name, shape, F32))

        xT = sb("xT", [P, SEQS * T])
        x0T = sb("x0T", [P, SEQS * T])
        const = {"ident": sb("ident", [P, P]), "mean": sb("mean", [P, P]),
                 "heads": sb("heads", [P, P]),
                 "one": sb("one", [P, 1]), "eps": sb("eps", [P, 1]), "unshift": sb("unshift", [P, 1])}
        with ExitStack() as c2:
            const_loaded = c2.enter_context(nc.semaphore("const_loaded"))
            const_set = c2.enter_context(nc.semaphore("const_set"))
            block = c2.enter_context(nc.Block())

            @block.sync
            def _(sp):
                sp.dma_start(const["ident"][:, :], d["c_ident"]).then_inc(const_loaded, 16)
                sp.dma_start(const["heads"][:, :], d["c_heads"]).then_inc(const_loaded, 16)
                sp.wait_ge(const_loaded, 32)
                sp.wait_ge(const_set, 4)

            @block.vector
            def _(ve):
                ve.memset(const["mean"][:, :], 1.0 / P).then_inc(const_set, 1)
                ve.memset(const["one"][:, :], 1.0).then_inc(const_set, 1)
                ve.memset(const["eps"][:, :], EPS).then_inc(const_set, 1)
                ve.memset(const["unshift"][:, :], 15 * math.log(2.0)).then_inc(const_set, 1)

        def ssm_weights(k):
            return {"pick": d["c_pick"],
                    **{n: d[f"{k}_{n}"] for n in ("w_in", "w_bc", "w_dlt", "w_dt", "w_out", "chan", "a_log")}}

        held = {}

        def signals(name, per=1):
            if name not in held:
                held[name] = Counter(ctx, nc, "ssm_" + name, per)
            return held[name]

        state_space_phase(nc, "s0_", signals, 0, xT, d["x"], const, ssm_weights("s0"))
        local_attention_phase(nc, "at_", xT, x0T, const,
                              {n: d["at_" + n] for n in ("w_qkv", "w_o", "w1", "w2", "chan_a", "chan", "tables", "mask")})
        layer_norm_phase(nc, "ln_", xT, x0T, const)
        state_space_phase(nc, "s1_", signals, 1, xT, None, const, ssm_weights("s1"))
        expert_phase(nc, "ex_", xT, const,
                     {n: d["ex_" + n] for n in ("wr", "w1", "w3", "w2", "owner", "part", "iota")}, out)


def kernel(**inputs):
    import numpy as np
    import concourse.bacc as _bacc
    from concourse.bass_utils import run_bass_kernel_spmd as _run

    i = {k: np.asarray(v) for k, v in inputs.items()}
    f = np.float32
    arrays = {"x": i["L0_attn_x"].transpose(2, 0, 1).reshape(P, SEQS * T)}
    pick = np.zeros((32, 32, P), f)
    pick[np.arange(32), np.arange(32), :] = 1
    arrays["c_ident"], arrays["c_pick"] = np.eye(P, dtype=f), pick

    def halves(a):
        return a.reshape(2, P, -1).transpose(1, 0, 2)

    def ssm(k, w_in, w_x, rank, w_dt, taps, conv_b, b_dt, skip, a_log, w_out):
        arrays[k + "w_in"] = w_in
        arrays[k + "w_bc"], arrays[k + "w_dlt"] = halves(w_x[:, rank:]), halves(w_x[:, :rank])
        arrays[k + "w_dt"], arrays[k + "w_out"] = w_dt, halves(w_out)
        arrays[k + "chan"] = np.concatenate([halves(taps), halves(conv_b), halves(b_dt), halves(skip)], 2)
        arrays[k + "a_log"] = halves(a_log)

    ssm("s0_", i["L0_attn_W_in"].T, i["L0_attn_W_xproj"].T, 8, i["L0_attn_W_dt"].T, i["L0_attn_W_conv"][:, 0, :],
        np.zeros(256, f), i["L0_attn_b_dt"], i["L0_attn_D"], i["L0_attn_A_log"], i["L0_attn_W_out"].T)
    ssm("s1_", i["L1_attn_W_in"], i["L1_attn_W_x"], 64, i["L1_attn_W_delta"], i["L1_attn_conv_w"][:, 0, :].T,
        i["L1_attn_conv_b"], i["L1_attn_b_delta"], i["L1_attn_D"], i["L1_attn_A_log"], i["L1_attn_W_out"])

    half = np.arange(0, 64, 2, dtype=f)
    t = np.arange(T, dtype=f)
    freqs = t[:, None] * (1.0 / 10000.0 ** (half / 64)).astype(f)[None, :]
    scale = (((half + 0.4 * 64) / (1.4 * 64)).astype(f)[None, :] ** ((t - T // 2) / 16)[:, None]).astype(f)
    cos, sin = np.cos(freqs), np.sin(freqs)

    def both_heads(a, sign):
        return np.concatenate([sign * a, a, sign * a, a], 1).T.astype(f)

    arrays["at_tables"] = np.stack([both_heads(cos * scale, 1), both_heads(sin * scale, -1),
                                    both_heads(cos / scale, 1), both_heads(sin / scale, -1)], 1)
    qi, kc = np.arange(P)[:, None] % 64, np.arange(96)[None, :]
    band = np.where((kc >= qi) & (kc <= qi + 32), f(0), f(-1e30))
    first = np.where(kc >= 32, band, f(-1e30))
    arrays["at_mask"] = np.concatenate([first] + [band] * 7, 1).reshape(P, 2, 4 * 96).astype(f)
    arrays["c_heads"] = np.kron(np.eye(2, dtype=f), np.ones((64, 64), f))
    arrays["at_w_qkv"] = i["L0_ffn_Wqkv"]
    arrays["at_w_o"] = i["L0_ffn_Wo"].reshape(6, 8, P, P).transpose(0, 2, 1, 3)
    arrays["at_w1"] = i["L0_ffn_W1"]
    hid = 114

    def hidden(a):
        a = np.concatenate([a, a[:, :1]], 1)
        return a.reshape(6, 3, hid, -1).transpose(0, 2, 1, 3)

    def per_channel(a):
        return np.stack([np.tile(a, 2), np.tile(np.roll(a, 32, 1), 2)], 2)

    arrays["at_w2"] = hidden(i["L0_ffn_W2"])
    b1 = i["L0_ffn_b1"][:, :, None]
    b1 = np.concatenate([hidden(b1[:, :341])[..., 0], hidden(b1[:, 341:])[..., 0]], 2)
    b1 = np.concatenate([b1, b1[:, :P - hid]], 1)
    arrays["at_chan_a"] = np.concatenate([per_channel(i["L0_ffn_q_scale"]), per_channel(i["L0_ffn_k_scale"])], 2)
    arrays["at_chan"] = np.concatenate(
        [np.stack([i["L0_ffn_ln_g"], i["L0_ffn_ln_b"], i["L0_ffn_b2"]], 2), b1], 2)

    import ml_dtypes
    arrays["ex_wr"] = i["L1_ffn_Wr"]
    arrays["ex_w1"] = i["L1_ffn_W1"].transpose(1, 0, 2).reshape(P, -1)
    arrays["ex_w3"] = i["L1_ffn_W3"].transpose(1, 0, 2).reshape(P, -1)
    arrays["ex_w2"] = i["L1_ffn_W2"].reshape(12, P, P).transpose(1, 0, 2)
    owner = np.zeros((72, 12 * P), ml_dtypes.bfloat16)
    for r in range(3):
        for e in range(8):
            owner[32 * r + e, 192 * e:192 * (e + 1)] = 1
    arrays["ex_owner"] = owner.reshape(72, 12, P)
    rows = np.arange(P)
    arrays["ex_part"] = np.stack([np.where(rows >= 32, f(-1), f(0)), np.where(rows >= 64, f(-1), f(0))], 1)
    arrays["ex_iota"] = np.tile(np.arange(8, dtype=f), (P, 1))

    nc = _bacc.Bacc("TRN2", target_bir_lowering=False, num_devices=1)
    arrays = {k: np.ascontiguousarray(v) for k, v in arrays.items()}
    d = {k: nc.dram_tensor("in_" + k, v.shape, mybir.dt.from_np(v.dtype), kind="ExternalInput").ap()
         for k, v in arrays.items()}
    out = nc.dram_tensor("out", (P, SEQS * T), F32, kind="ExternalOutput").ap()
    build_program(nc, d, out)
    r = _run(nc, [{"in_" + k: v for k, v in arrays.items()}], core_ids=[0])
    return np.ascontiguousarray(r.results[0]["out"].reshape(P, SEQS, T).transpose(1, 2, 0))
```

```python
import math
from contextlib import ExitStack

import concourse.bass as bass
from concourse import mybir

F32 = mybir.dt.float32
BF16 = mybir.dt.bfloat16
U32 = mybir.dt.uint32
ALU = mybir.AluOpType
ACT = mybir.ActivationFunctionType
AX = mybir.AxisListType
EXP_LN_SET = "natural_log_exp_and_others"
GELU_SET = "gelu_and_others"
SILU_SET = "silu_and_others"

P = 128
SEQS = 8
T = 512
EPS = 1e-5


class Counter:

    def __init__(self, ctx, nc, name, per):
        self.sem = ctx.enter_context(nc.semaphore(name))
        self.per = per

    def at(self, it, k):
        return it * self.per + k


class Memory:

    def __init__(self, ctx, nc, prefix):
        self.ctx, self.nc, self.prefix = ctx, nc, prefix

    def sb(self, name, shape, dt=F32):
        return self.ctx.enter_context(self.nc.sbuf_tensor(self.prefix + name, shape, dt))

    def bank(self, name):
        return self.ctx.enter_context(self.nc.psum_tensor(self.prefix + name, [P, 512], F32))

    def counter(self, name, per=1):
        return Counter(self.ctx, self.nc, self.prefix + name, per)


def state_space_phase(nc, prefix, signals, turn, xT, x_dram, const, w):
    NSTATE = 16
    HALVES = 2
    TAPS = 4
    R = w["w_dt"].shape[0]
    BCR = 96
    RING = 4
    LAG = RING - 1
    with ExitStack() as ctx:
        m = Memory(ctx, nc, prefix)
        w_in = m.sb("w_in", [P, 4 * P])
        pick = m.sb("pick", [BCR, 2 * NSTATE, P], BF16)
        part = m.sb("part", [P, 2])
        w_bc = m.sb("w_bc", [P, HALVES, BCR])
        w_dlt = m.sb("w_dlt", [P, HALVES, R])
        w_dt = m.sb("w_dt", [R, HALVES * P])
        w_out = m.sb("w_out", [P, HALVES, P])
        chan = m.sb("chan", [P, HALVES, TAPS + 3])
        a_log = m.sb("a_log", [P, HALVES, NSTATE])
        a_exp = m.sb("a_exp", [P, HALVES, NSTATE])
        decay = m.sb("decay", [P, HALVES, NSTATE])
        xpad = m.sb("xpad", [P, HALVES, TAPS - 1 + T])
        conv = m.sb("conv", [P, HALVES, T])
        xc = m.sb("xc", [P, 2, HALVES, T])
        zs = m.sb("zs", [P, 2, HALVES, T])
        part_a = m.sb("part_a", [BCR, T], BF16)
        rest_a = m.sb("rest_a", [BCR, T])
        part_b = m.sb("part_b", [BCR, T], BF16)
        bc = m.sb("bc", [BCR, 2, T], BF16)
        dlt = m.sb("dlt", [R, T])
        mag = m.sb("mag", [P, HALVES, T])
        em = m.sb("em", [P, HALVES, T])
        lg = mag
        onep = m.sb("onep", [P, HALVES, T])
        dm = m.sb("dm", [P, HALVES, T])
        pos = m.sb("pos", [P, HALVES, T])
        delta = m.sb("delta", [P, 2, HALVES, T])
        u = m.sb("u", [P, 2, HALVES, T])
        csb = m.sb("csb", [P, RING, T])
        dA = m.sb("dA", [P, RING, HALVES, T])
        dBx = m.sb("dBx", [P, RING, HALVES, T])
        h = m.sb("h", [P, RING, HALVES, T])
        hc = m.sb("hc", [P, RING, HALVES, T])
        y = m.sb("y", [P, HALVES, T])
        yz = m.sb("yz", [P, HALVES, T])
        res = m.sb("res", [P, T])
        cen = m.sb("cen", [P, T])
        sq = m.sb("sq", [P, T])
        lv = m.sb("lv", [P, T])
        rstd = m.sb("rstd", [P, T])
        bank_b = [m.bank("bank_b0"), m.bank("bank_b1")]
        bank_c = [m.bank("bank_c0"), m.bank("bank_c1")]
        bank_y = [m.bank("bank_y0"), m.bank("bank_y1")]
        bank_w = [m.bank("bank_w0"), m.bank("bank_w1")]

        loaded = signals("loaded")
        x_loaded = signals("x_loaded")
        zero_pad = signals("zero_pad")
        a_ready = signals("a_ready")
        x_ps = signals("x_ps", 2)
        z_ps = signals("z_ps", 2)
        xpad_ready = signals("xpad_ready", 2)
        tap_done = signals("tap_done", TAPS * HALVES)
        zs_ready = signals("zs_ready", 2)
        xc_ready = signals("xc_ready", 2)
        bc_ps = signals("bc_ps")
        dlt_ps = signals("dlt_ps")
        split_steps = signals("split_steps", 4)
        dlt_ready = signals("dlt_ready")
        dt_ready = signals("dt_ready", 2)
        mag_ready = signals("mag_ready", 2)
        em_ready = signals("em_ready", 2)
        lg_ready = signals("lg_ready", 2)
        dm_steps = signals("dm_steps", 5 * HALVES)
        pos_ready = signals("pos_ready", 2)
        delta_ready = signals("delta_ready", 2)
        u_ready = signals("u_ready", 2)
        b_ready = signals("b_ready", NSTATE)
        c_ready = signals("c_ready", NSTATE)
        c_copied = signals("c_copied", NSTATE)
        dA_ready = signals("dA_ready", NSTATE * HALVES)
        dBx_ready = signals("dBx_ready", NSTATE * HALVES)
        h_ready = signals("h_ready", NSTATE * HALVES)
        hc_ready = signals("hc_ready", NSTATE * HALVES)
        hc_used = signals("hc_used", NSTATE * HALVES)
        y_ready = signals("y_ready", 2)
        yz_ready = signals("yz_ready", 2)
        out_ps = signals("out_ps")
        res_ready = signals("res_ready")
        mean_ready = signals("mean_ready")
        cen_ready = signals("cen_ready")
        sq_ready = signals("sq_ready")
        var_ready = signals("var_ready")
        lv_ready = signals("lv_ready")
        rstd_ready = signals("rstd_ready")
        x_written = signals("x_written")

        block = ctx.enter_context(nc.Block())
        N_LOADS = 9
        BASE = turn * SEQS
        LAST = SEQS - 1

        def tokens(q):
            return bass.ds(q * T, T)

        def passes(eng, body):
            body(BASE, 0, 0)
            body(BASE + 1, 1, 1)
            with eng.Fori(1, SEQS // 2 - 1) as k:
                body(BASE + 2 * k, 2 * k, 2)
                body(BASE + 2 * k + 1, 2 * k + 1, 3)
            body(BASE + 6, 6, 6)
            body(BASE + 7, 7, 7)

        @block.sync
        def _(sp):
            if x_dram is not None:
                sp.dma_start(xT[:, :], x_dram).then_inc(x_loaded.sem, 16)
            sp.dma_start(w_in[:, :], w["w_in"]).then_inc(loaded.sem, 16)
            sp.dma_start(chan[:, :, :], w["chan"]).then_inc(loaded.sem, 16)
            sp.dma_start(w_bc[:, :, :], w["w_bc"]).then_inc(loaded.sem, 16)
            sp.dma_start(w_dlt[:, :, :], w["w_dlt"]).then_inc(loaded.sem, 16)
            sp.dma_start(w_dt[:, :], w["w_dt"]).then_inc(loaded.sem, 16)
            sp.dma_start(pick[:, :, :], w["pick"]).then_inc(loaded.sem, 16)
            sp.dma_start(part[:, :], w["part"]).then_inc(loaded.sem, 16)
            sp.dma_start(a_log[:, :, :], w["a_log"]).then_inc(loaded.sem, 16)
            sp.dma_start(w_out[:, :, :], w["w_out"]).then_inc(loaded.sem, 16)
            sp.wait_ge(loaded.sem, 16 * N_LOADS * (turn + 1))

        @block.tensor
        def _(pe):
            def project_x(it, q, n):
                for c in range(HALVES):
                    if n >= 1:
                        pe.wait_ge(pos_ready.sem, pos_ready.at(it - 1, c + 1))
                    if n >= 3 and c == 1:
                        pe.wait_ge(cen_ready.sem, cen_ready.at(it - 3, 1))
                    if n >= 3 and c == 0:
                        pe.wait_ge(lv_ready.sem, lv_ready.at(it - 3, 1))
                    pe.matmul(bank_w[c][:, :], w_in[:, c * P:(c + 1) * P], xT[:, tokens(q)],
                              start=True, stop=True).then_inc(x_ps.sem, 1)

            def project_z(it, q):
                for c in range(HALVES):
                    pe.wait_ge(xpad_ready.sem, xpad_ready.at(it, c + 1))
                    pe.matmul(bank_w[c][:, :], w_in[:, (2 + c) * P:(3 + c) * P], xT[:, tokens(q)],
                              start=True, stop=True).then_inc(z_ps.sem, 1)

            def project_bc(it, par):
                pe.wait_ge(zs_ready.sem, zs_ready.at(it, 2))
                pe.wait_ge(xc_ready.sem, xc_ready.at(it, 2))
                for c in range(HALVES):
                    mm = pe.matmul(bank_w[0][0:BCR, :], w_bc[:, c, :], xc[:, par, c, :],
                                   start=(c == 0), stop=(c == 1))
                mm.then_inc(bc_ps.sem, 1)
                for c in range(HALVES):
                    mm = pe.matmul(bank_w[1][0:R, :], w_dlt[:, c, :], xc[:, par, c, :],
                                   start=(c == 0), stop=(c == 1))
                mm.then_inc(dlt_ps.sem, 1)

            def project_dt(it):
                pe.wait_ge(dlt_ready.sem, dlt_ready.at(it, 1))
                pe.wait_ge(split_steps.sem, split_steps.at(it, 2))
                for c in range(HALVES):
                    pe.matmul(bank_w[c][:, :], w_dt[:, c * P:(c + 1) * P], dlt[:, :],
                              start=True, stop=True).then_inc(dt_ready.sem, 1)

            def accumulate(it, n, n0):
                for c in range(HALVES):
                    k = n * HALVES + c
                    if n == 0 and n0 >= 1:
                        pe.wait_ge(y_ready.sem, y_ready.at(it - 1, c + 1))
                    pe.wait_ge(hc_ready.sem, hc_ready.at(it, k + 1))
                    pe.matmul(bank_y[c][:, :], const["ident"][:, :], hc[:, n % RING, c, :],
                              start=(n == 0), stop=(n == NSTATE - 1)).then_inc(hc_used.sem, 1)

            def project_out(it, next_too):
                pe.wait_ge(yz_ready.sem, yz_ready.at(it, 2))
                if next_too:
                    pe.wait_ge(pos_ready.sem, pos_ready.at(it + 2, 1))
                else:
                    pe.wait_ge(pos_ready.sem, 2 * (BASE + SEQS))
                for c in range(HALVES):
                    mm = pe.matmul(bank_w[0][:, :], w_out[:, c, :], yz[:, c, :],
                                   start=(c == 0), stop=(c == 1))
                mm.then_inc(out_ps.sem, 1)

            def mean(it, next_too):
                pe.wait_ge(res_ready.sem, res_ready.at(it, 1))
                if next_too:
                    pe.wait_ge(pos_ready.sem, pos_ready.at(it + 2, 2))
                pe.matmul(bank_w[1][:, :], const["mean"][:, :], res[:, :],
                          start=True, stop=True).then_inc(mean_ready.sem, 1)

            def variance(it):
                pe.wait_ge(sq_ready.sem, sq_ready.at(it, 1))
                pe.matmul(bank_w[0][:, :], const["mean"][:, :], sq[:, :],
                          start=True, stop=True).then_inc(var_ready.sem, 1)

            def body(it, q, n0):
                par = n0 % 2
                more = n0 < LAST
                pe.wait_ge(split_steps.sem, split_steps.at(it, 4))
                for n in range(NSTATE):
                    if n0 >= 1 or n >= 2:
                        pe.wait_ge(dBx_ready.sem, dBx_ready.at(it, (n - 1) * HALVES))
                    pe.matmul(bank_b[n % 2][:, :], pick[:, n, :], bc[:, par, :],
                              start=True, stop=True).then_inc(b_ready.sem, 1)
                    if n0 >= 1 or n >= 2:
                        pe.wait_ge(c_copied.sem, c_copied.at(it, n - 1))
                    pe.matmul(bank_c[n % 2][:, :], pick[:, NSTATE + n, :], bc[:, par, :],
                              start=True, stop=True).then_inc(c_ready.sem, 1)
                    if n >= LAG:
                        accumulate(it, n - LAG, n0)
                    elif n0 >= 1:
                        accumulate(it - 1, NSTATE + n - LAG, n0 - 1)
                    if more:
                        if n == 1:
                            project_x(it + 1, q + 1, n0 + 1)
                        if n == 2:
                            project_z(it + 1, q + 1)
                        if n == 5:
                            project_bc(it + 1, 1 - par)
                        if n == 7:
                            project_dt(it + 1)
                    if n0 >= 1:
                        if n == 10:
                            project_out(it - 1, more)
                        if n == 12:
                            mean(it - 1, more)
                        if n == 14:
                            variance(it - 1)

            pe.wait_ge(loaded.sem, 16 * N_LOADS * (turn + 1))
            if x_dram is not None:
                pe.wait_ge(x_loaded.sem, 16)
            project_x(BASE, 0, 0)
            project_z(BASE, 0)
            project_bc(BASE, 0)
            project_dt(BASE)
            passes(pe, body)
            for n in range(NSTATE - LAG, NSTATE):
                accumulate(BASE + LAST, n, LAST)
            pe.wait_ge(lv_ready.sem, BASE + LAST)
            project_out(BASE + LAST, False)
            mean(BASE + LAST, False)
            variance(BASE + LAST)

        @block.scalar
        def _(act):
            def copy_x(it):
                for c in range(HALVES):
                    act.wait_ge(x_ps.sem, x_ps.at(it, c + 1))
                    act.activation(xpad[:, c, TAPS - 1:], bank_w[c][:, :], ACT.Copy).then_inc(xpad_ready.sem, 1)

            def silu(it, par, n):
                act.preload_act_table_set(SILU_SET)
                if n >= 2:
                    act.wait_ge(yz_ready.sem, yz_ready.at(it - 2, 2))
                for c in range(HALVES):
                    act.wait_ge(z_ps.sem, z_ps.at(it, c + 1))
                    act.activation(zs[:, par, c, :], bank_w[c][:, :], ACT.Silu).then_inc(zs_ready.sem, 1)
                for c in range(HALVES):
                    act.wait_ge(tap_done.sem, tap_done.at(it, HALVES * (TAPS - 1) + c + 1))
                    act.activation(xc[:, par, c, :], conv[:, c, :], ACT.Silu).then_inc(xc_ready.sem, 1)
                act.preload_act_table_set(EXP_LN_SET)

            def copy_rows(it):
                act.wait_ge(bc_ps.sem, bc_ps.at(it, 1))
                act.activation(part_a[:, :], bank_w[0][0:BCR, :], ACT.Copy).then_inc(split_steps.sem, 1)
                act.wait_ge(dlt_ps.sem, dlt_ps.at(it, 1))
                act.activation(dlt[:, :], bank_w[1][0:R, :], ACT.Copy).then_inc(dlt_ready.sem, 1)

            def magnitude(it):
                for c in range(HALVES):
                    act.wait_ge(dt_ready.sem, dt_ready.at(it, c + 1))
                    act.activation(mag[:, c, :], bank_w[c][:, :], ACT.Abs,
                                   bias=chan[:, c, TAPS + 1:TAPS + 2]).then_inc(mag_ready.sem, 1)
                for c in range(HALVES):
                    act.wait_ge(mag_ready.sem, mag_ready.at(it, c + 1))
                    act.activation(em[:, c, :], mag[:, c, :], ACT.Exp, scale=-1.0).then_inc(em_ready.sem, 1)

            def logarithm(it):
                for c in range(HALVES):
                    act.wait_ge(dm_steps.sem, dm_steps.at(it, c + 1))
                    act.activation(lg[:, c, :], onep[:, c, :], ACT.Ln).then_inc(lg_ready.sem, 1)

            def square(it):
                act.wait_ge(cen_ready.sem, cen_ready.at(it, 1))
                act.activation(sq[:, :], cen[:, :], ACT.Square).then_inc(sq_ready.sem, 1)

            def inverse_deviation(it):
                act.wait_ge(var_ready.sem, var_ready.at(it, 1))
                act.activation(lv[:, :], bank_w[0][:, :], ACT.Ln, bias=const["eps"][:, 0:1]).then_inc(lv_ready.sem, 1)
                act.wait_ge(lv_ready.sem, lv_ready.at(it, 1))
                act.activation(rstd[:, :], lv[:, :], ACT.Exp, scale=-0.5).then_inc(rstd_ready.sem, 1)

            def body(it, q, n0):
                par = n0 % 2
                act.preload_act_table_set(EXP_LN_SET)
                act.wait_ge(delta_ready.sem, delta_ready.at(it, 2))
                for n in range(NSTATE):
                    act.wait_ge(c_ready.sem, c_ready.at(it, n + 1))
                    if n0 >= 1 or n >= RING:
                        act.wait_ge(hc_ready.sem, hc_ready.at(it, (n - RING + 1) * HALVES))
                    act.activation(csb[:, n % RING, :], bank_c[n % 2][:, :], ACT.Copy).then_inc(c_copied.sem, 1)
                    for c in range(HALVES):
                        if n0 >= 1 or n >= RING:
                            act.wait_ge(h_ready.sem, h_ready.at(it, (n - RING) * HALVES + c + 1))
                        act.activation(dA[:, n % RING, c, :], delta[:, par, c, :], ACT.Exp,
                                       scale=decay[:, c, n:n + 1]).then_inc(dA_ready.sem, 1)
                    if n0 < LAST:
                        if n == 1:
                            copy_x(it + 1)
                        if n == 4:
                            silu(it + 1, 1 - par, n0 + 1)
                        if n == 5:
                            copy_rows(it + 1)
                        if n == 7:
                            magnitude(it + 1)
                        if n == 8:
                            logarithm(it + 1)
                    if n0 >= 1:
                        if n == 12:
                            square(it - 1)
                        if n == 14:
                            inverse_deviation(it - 1)

            act.preload_act_table_set(EXP_LN_SET)
            act.wait_ge(loaded.sem, 16 * N_LOADS * (turn + 1))
            act.activation(a_exp[:, :, :], a_log[:, :, :], ACT.Exp).then_inc(a_ready.sem, 1)
            copy_x(BASE)
            silu(BASE, 0, 0)
            copy_rows(BASE)
            magnitude(BASE)
            logarithm(BASE)
            act.wait_ge(a_ready.sem, 2 * turn + 2)
            passes(act, body)
            act.preload_act_table_set(EXP_LN_SET)
            square(BASE + LAST)
            inverse_deviation(BASE + LAST)

        @block.vector
        def _(ve):
            def convolve(it, j):
                for c in range(HALVES):
                    src, tap = xpad[:, c, j:j + T], chan[:, c, j:j + 1]
                    if j == 0:
                        ve.wait_ge(xpad_ready.sem, xpad_ready.at(it, c + 1))
                        ve.tensor_scalar(conv[:, c, :], src, tap, chan[:, c, TAPS:TAPS + 1],
                                         ALU.mult, ALU.add).then_inc(tap_done.sem, 1)
                    else:
                        ve.wait_ge(tap_done.sem, tap_done.at(it, HALVES * (j - 1) + c + 1))
                        ve.scalar_tensor_tensor(out=conv[:, c, :], in0=src, scalar=tap, in1=conv[:, c, :],
                                                op0=ALU.mult, op1=ALU.add).then_inc(tap_done.sem, 1)

            def split_rows(it, par):
                ve.wait_ge(split_steps.sem, split_steps.at(it, 1))
                ve.scalar_tensor_tensor(out=rest_a[:, :], in0=part_a[:, :], scalar=part[0:BCR, 0:1],
                                        in1=bank_w[0][0:BCR, :], op0=ALU.mult, op1=ALU.add).then_inc(split_steps.sem, 1)
                ve.wait_ge(split_steps.sem, split_steps.at(it, 2))
                ve.tensor_copy(part_b[:, :], rest_a[:, :]).then_inc(split_steps.sem, 1)
                ve.wait_ge(split_steps.sem, split_steps.at(it, 3))
                ve.scalar_tensor_tensor(out=bc[:, par, :], in0=part_b[:, :], scalar=part[0:BCR, 1:2],
                                        in1=rest_a[:, :], op0=ALU.mult, op1=ALU.add).then_inc(split_steps.sem, 1)

            def softplus_start(it):
                for c in range(HALVES):
                    ve.wait_ge(mag_ready.sem, mag_ready.at(it, c + 1))
                    ve.tensor_scalar(pos[:, c, :], bank_w[c][:, :], chan[:, c, TAPS + 1:TAPS + 2], 0.0,
                                     ALU.add, ALU.max).then_inc(pos_ready.sem, 1)
                for c in range(HALVES):
                    ve.wait_ge(em_ready.sem, em_ready.at(it, c + 1))
                    ve.tensor_scalar(onep[:, c, :], em[:, c, :], 1.0, None, ALU.add).then_inc(dm_steps.sem, 1)

            def softplus_quotient(it):
                for c in range(HALVES):
                    ve.wait_ge(dm_steps.sem, dm_steps.at(it, c + 1))
                    ve.tensor_scalar(dm[:, c, :], onep[:, c, :], 1.0, 1e-30,
                                     ALU.subtract, ALU.max).then_inc(dm_steps.sem, 1)
                for c in range(HALVES):
                    ve.wait_ge(dm_steps.sem, dm_steps.at(it, 3 + c))
                    ve.reciprocal(dm[:, c, :], dm[:, c, :]).then_inc(dm_steps.sem, 1)

            def softplus_end(it, par):
                for c in range(HALVES):
                    ve.wait_ge(dm_steps.sem, dm_steps.at(it, 5 + c))
                    ve.wait_ge(lg_ready.sem, lg_ready.at(it, c + 1))
                    ve.scalar_tensor_tensor(out=dm[:, c, :], in0=lg[:, c, :], scalar=1e-30, in1=dm[:, c, :],
                                            op0=ALU.max, op1=ALU.mult).then_inc(dm_steps.sem, 1)
                for c in range(HALVES):
                    ve.wait_ge(dm_steps.sem, dm_steps.at(it, 7 + c))
                    ve.scalar_tensor_tensor(out=dm[:, c, :], in0=dm[:, c, :], scalar=1.0, in1=em[:, c, :],
                                            op0=ALU.min, op1=ALU.mult).then_inc(dm_steps.sem, 1)
                for c in range(HALVES):
                    ve.wait_ge(dm_steps.sem, dm_steps.at(it, 9 + c))
                    ve.wait_ge(pos_ready.sem, pos_ready.at(it, c + 1))
                    ve.tensor_tensor(delta[:, par, c, :], dm[:, c, :], pos[:, c, :], ALU.add)\
                      .then_inc(delta_ready.sem, 1)

            def skip_sum(it, par, n):
                for c in range(HALVES):
                    ve.wait_ge(hc_used.sem, hc_used.at(it, NSTATE * HALVES))
                    if n >= 1:
                        ve.wait_ge(yz_ready.sem, yz_ready.at(it - 1, c + 1))
                    ve.scalar_tensor_tensor(out=y[:, c, :], in0=xc[:, par, c, :],
                                            scalar=chan[:, c, TAPS + 2:TAPS + 3],
                                            in1=bank_y[c][:, :], op0=ALU.mult, op1=ALU.add)\
                      .then_inc(y_ready.sem, 1)

            def residual(it, q):
                ve.wait_ge(out_ps.sem, out_ps.at(it, 1))
                ve.tensor_tensor(res[:, :], bank_w[0][:, :], xT[:, tokens(q)], ALU.add).then_inc(res_ready.sem, 1)

            def center(it):
                ve.wait_ge(res_ready.sem, res_ready.at(it, 1))
                ve.wait_ge(mean_ready.sem, mean_ready.at(it, 1))
                ve.tensor_tensor(cen[:, :], res[:, :], bank_w[1][:, :], ALU.subtract).then_inc(cen_ready.sem, 1)

            def write_x(it, q):
                ve.wait_ge(rstd_ready.sem, rstd_ready.at(it, 1))
                ve.tensor_tensor(xT[:, tokens(q)], cen[:, :], rstd[:, :], ALU.mult).then_inc(x_written.sem, 1)

            def body(it, q, n0):
                par = n0 % 2
                ve.wait_ge(u_ready.sem, u_ready.at(it, 2))
                for n in range(NSTATE):
                    ve.wait_ge(b_ready.sem, b_ready.at(it, n + 1))
                    for c in range(HALVES):
                        if n0 >= 1 or n >= RING:
                            ve.wait_ge(h_ready.sem, h_ready.at(it, (n - RING) * HALVES + c + 1))
                        ve.tensor_tensor(dBx[:, n % RING, c, :], u[:, par, c, :], bank_b[n % 2][:, :],
                                         ALU.mult).then_inc(dBx_ready.sem, 1)
                    for c in range(HALVES):
                        k = n * HALVES + c
                        ve.wait_ge(dBx_ready.sem, dBx_ready.at(it, k + 1))
                        ve.wait_ge(dA_ready.sem, dA_ready.at(it, k + 1))
                        if n0 >= 1 or n >= RING:
                            ve.wait_ge(hc_ready.sem, hc_ready.at(it, (n - RING) * HALVES + c + 1))
                        ve.tensor_tensor_scan(h[:, n % RING, c, :], dA[:, n % RING, c, :], dBx[:, n % RING, c, :], 0.0,
                                              ALU.mult, ALU.add).then_inc(h_ready.sem, 1)
                    if n0 >= 1 and n == LAG - 1:
                        skip_sum(it - 1, 1 - par, n0 - 1)
                    if n0 < LAST:
                        if n == 2:
                            convolve(it + 1, 0)
                            convolve(it + 1, 1)
                        if n == 3:
                            convolve(it + 1, 2)
                            convolve(it + 1, 3)
                        if n == 5:
                            split_rows(it + 1, 1 - par)
                        if n == 7:
                            softplus_start(it + 1)
                        if n == 8:
                            softplus_quotient(it + 1)
                        if n == 9:
                            softplus_end(it + 1, 1 - par)
                    if n0 >= 1:
                        if n == 11:
                            residual(it - 1, q - 1)
                        if n == 12:
                            center(it - 1)
                        if n == 15:
                            write_x(it - 1, q - 1)

            ve.memset(xpad[:, :, 0:TAPS - 1], 0.0).then_inc(zero_pad.sem, 1)
            ve.wait_ge(a_ready.sem, 2 * turn + 1)
            ve.tensor_scalar(decay[:, :, :], a_exp[:, :, :], -1.0, None, ALU.mult).then_inc(a_ready.sem, 1)
            ve.wait_ge(zero_pad.sem, turn + 1)
            for j in range(TAPS):
                convolve(BASE, j)
            split_rows(BASE, 0)
            softplus_start(BASE)
            softplus_quotient(BASE)
            softplus_end(BASE, 0)
            passes(ve, body)
            skip_sum(BASE + LAST, LAST % 2, LAST)
            residual(BASE + LAST, LAST)
            center(BASE + LAST)
            write_x(BASE + LAST, LAST)

        @block.gpsimd
        def _(pool):
            def input_step(it, par):
                for c in range(HALVES):
                    pool.wait_ge(delta_ready.sem, delta_ready.at(it, c + 1))
                    pool.tensor_tensor(u[:, par, c, :], delta[:, par, c, :], xc[:, par, c, :],
                                       ALU.mult).then_inc(u_ready.sem, 1)

            def gate(it, par, n):
                for c in range(HALVES):
                    pool.wait_ge(y_ready.sem, y_ready.at(it, c + 1))
                    if n >= 1:
                        pool.wait_ge(out_ps.sem, out_ps.at(it - 1, 1))
                    pool.tensor_tensor(yz[:, c, :], y[:, c, :], zs[:, par, c, :], ALU.mult).then_inc(yz_ready.sem, 1)

            def body(it, q, n0):
                par = n0 % 2
                for n in range(NSTATE):
                    pool.wait_ge(c_copied.sem, c_copied.at(it, n + 1))
                    for c in range(HALVES):
                        pool.wait_ge(h_ready.sem, h_ready.at(it, n * HALVES + c + 1))
                        if n0 >= 1 or n >= RING:
                            pool.wait_ge(hc_used.sem, hc_used.at(it, (n - RING) * HALVES + c + 1))
                        pool.tensor_tensor(hc[:, n % RING, c, :], h[:, n % RING, c, :], csb[:, n % RING, :],
                                           ALU.mult).then_inc(hc_ready.sem, 1)
                    if n == LAG and n0 >= 1:
                        gate(it - 1, 1 - par, n0 - 1)
                    if n == 10 and n0 < LAST:
                        input_step(it + 1, 1 - par)

            input_step(BASE, 0)
            passes(pool, body)
            gate(BASE + LAST, LAST % 2, LAST)


def local_attention_phase(nc, prefix, xT, x0T, const, w):
    DEPTH = 6
    PAIRS = 8
    HD = 64
    QB = 64
    KB = 96
    LOOK = KB - QB
    NB = T // QB
    HALF = NB // 2
    TILES = 2 * PAIRS
    INNER = PAIRS * P
    HID = w["w2"].shape[1]
    HT = 3
    HR = [HID, HID, 341 - 2 * HID]
    QK_SCALE = 8.0
    NORM_SHIFT = 2.0 ** 30
    with ExitStack() as ctx:
        m = Memory(ctx, nc, prefix)
        w_qkv = m.sb("w_qkv", [P, 3 * INNER])
        w_rot = m.sb("w_rot", [P, 2 * INNER])
        w_o = m.sb("w_o", [P, PAIRS, P])
        w_1 = m.sb("w_1", [P, 2 * 341])
        w_2 = m.sb("w_2", [HID, HT, P])
        chan_a = m.sb("chan_a", [P, 4])
        chan = m.sb("chan", [P, 9])
        base = m.sb("base", [P, 4, T])
        mask = m.sb("mask", [P, 2, HALF * KB])
        xs = m.sb("xs", [P, LOOK + T])
        vals = m.sb("vals", [KB, NB, INNER])
        sq = m.sb("sq", [P, 2, T])
        t1 = m.sb("t1", [P, 2, T])
        t2 = m.sb("t2", [P, 2, T])
        nrm = m.sb("nrm", [P, 2, T])
        lnn = m.sb("lnn", [P, 2, T])
        rn = m.sb("rn", [P, 2, T])
        qT = m.sb("qT", [P, 2, T])
        kT = m.sb("kT", [P, 2, LOOK + T])
        sc = m.sb("sc", [P, 2, HALF * KB])
        mx = m.sb("mx", [P, 2, HALF])
        pr = m.sb("pr", [P, 2, HALF * KB])
        den = m.sb("den", [P, 2, HALF])
        rden = m.sb("rden", [P, 2, HALF])
        pn = m.sb("pn", [P, 2, HALF * KB])
        pT = m.sb("pT", [KB, 2, HALF * P])
        oT = m.sb("oT", [P, PAIRS, T])
        fs = m.sb("fs", [P, T])
        cen = m.sb("cen", [P, T])
        csq = m.sb("csq", [P, T])
        lv = m.sb("lv", [P, T])
        rstd = m.sb("rstd", [P, T])
        xn = m.sb("xn", [P, T])
        hid = m.sb("hid", [HID, HT, T])
        bank = [m.bank(f"bank{i}") for i in range(8)]

        fixed_loaded = m.counter("fixed_loaded")
        zeroed = m.counter("zeroed")
        low_loaded = m.counter("low_loaded", 16 * 3)
        high_loaded = m.counter("high_loaded", 16 * 2)
        scales_loaded = m.counter("scales_loaded", 16)
        ffn_loaded = m.counter("ffn_loaded", 16 * 4)
        shifted = m.counter("shifted", 2)
        v_ready = m.counter("v_ready", 2 * NB)
        v_copied = m.counter("v_copied", 2 * NB)
        rt_ready = m.counter("rt_ready", TILES)
        sq_ready = m.counter("sq_ready", TILES)
        t_ready = m.counter("t_ready", 2 * TILES)
        n_ready = m.counter("n_ready", TILES)
        guarded = m.counter("guarded", TILES)
        ln_ready = m.counter("ln_ready", TILES)
        rn_ready = m.counter("rn_ready", TILES)
        added = m.counter("added", TILES)
        rotated = m.counter("rotated", TILES)
        s_ready = m.counter("s_ready", TILES)
        masked = m.counter("masked", TILES)
        mx_ready = m.counter("mx_ready", TILES)
        sub_ready = m.counter("sub_ready", TILES)
        exp_ready = m.counter("exp_ready", TILES)
        den_ready = m.counter("den_ready", TILES)
        rden_ready = m.counter("rden_ready", TILES)
        p_ready = m.counter("p_ready", TILES)
        pt_ready = m.counter("pt_ready", TILES)
        pt_copied = m.counter("pt_copied", TILES)
        pv_done = m.counter("pv_done", TILES)
        o_copied = m.counter("o_copied", PAIRS)
        wo_done = m.counter("wo_done")
        x1_ready = m.counter("x1_ready")
        fs_ready = m.counter("fs_ready", 2)
        mean_ready = m.counter("mean_ready")
        cen_ready = m.counter("cen_ready")
        csq_ready = m.counter("csq_ready")
        var_ready = m.counter("var_ready")
        lv_ready = m.counter("lv_ready")
        rstd_ready = m.counter("rstd_ready")
        xh_ready = m.counter("xh_ready")
        xn_ready = m.counter("xn_ready")
        gate_up_ready = m.counter("gate_up_ready", HT)
        up_ready = m.counter("up_ready", HT)
        gate_ready = m.counter("gate_ready", HT)
        hid_ready = m.counter("hid_ready", HT)
        down_ready = m.counter("down_ready")
        x_done = m.counter("x_done")

        block = ctx.enter_context(nc.Block())
        PASSES = DEPTH * SEQS
        LEAD = SEQS
        V_STEPS = {0: (0, 0), 1: (0, 4), 3: (1, 0), 4: (1, 4)}

        def tokens(b):
            return bass.ds(b * T, T)

        def layer_loads(counter, it):
            return counter.at(it // SEQS + 1, 0)

        @block.sync
        def _(sp):
            def pairs_half(tensor, h):
                return tensor.rearrange("p (j h n) -> p j h n", j=2, h=2)[:, :, h, :]

            def layer(name, l, columns):
                return w[name][bass.ds(l, 1), :, columns].rearrange("a p n -> p (a n)")

            def load_projection(l, h, loaded):
                qk = slice(0, 2 * INNER)
                sp.dma_start(pairs_half(w_qkv[:, qk], h), pairs_half(layer("w_qkv", l, qk), h)).then_inc(loaded.sem, 16)
                sp.dma_start(pairs_half(w_rot[:, :], h), pairs_half(layer("w_rot", l, qk), h)).then_inc(loaded.sem, 16)

            def load_values(l):
                v = slice(2 * INNER, 3 * INNER)
                sp.dma_start(w_qkv[:, v], layer("w_qkv", l, v)).then_inc(low_loaded.sem, 16)

            def load_scales(l):
                sp.dma_start(chan_a[:, :], layer("chan_a", l, slice(0, 4))).then_inc(scales_loaded.sem, 16)

            def load_ffn(l):
                sp.dma_start(w_o[:, :, :], w["w_o"][bass.ds(l, 1), :, :, :].rearrange("a p k n -> p (a k) n"))\
                  .then_inc(ffn_loaded.sem, 16)
                sp.dma_start(w_1[:, :], layer("w1", l, slice(0, 2 * 341))).then_inc(ffn_loaded.sem, 16)
                sp.dma_start(w_2[:, :, :], w["w2"][bass.ds(l, 1), :, :, :].rearrange("a p k n -> p (a k) n"))\
                  .then_inc(ffn_loaded.sem, 16)
                sp.dma_start(chan[:, :], layer("chan", l, slice(0, 9))).then_inc(ffn_loaded.sem, 16)

            load_values(0)
            load_projection(0, 0, low_loaded)
            load_scales(0)
            sp.dma_start(base[:, :, :], w["tables"]).then_inc(fixed_loaded.sem, 16)
            sp.dma_start(mask[:, :, :], w["mask"]).then_inc(fixed_loaded.sem, 16)
            load_projection(0, 1, high_loaded)
            load_ffn(0)
            with sp.Fori(1, DEPTH) as l:
                last = l * SEQS - 1
                sp.wait_ge(rt_ready.sem, rt_ready.at(last, TILES // 2 + 1))
                load_values(l)
                load_projection(l, 0, low_loaded)
                sp.wait_ge(rt_ready.sem, rt_ready.at(last, TILES))
                load_projection(l, 1, high_loaded)
                sp.wait_ge(t_ready.sem, t_ready.at(last, 2 * TILES))
                load_scales(l)
                sp.wait_ge(x_done.sem, last + 1 + LEAD)
                load_ffn(l)
            sp.wait_ge(low_loaded.sem, low_loaded.at(DEPTH, 0))
            sp.wait_ge(high_loaded.sem, high_loaded.at(DEPTH, 0))
            sp.wait_ge(scales_loaded.sem, scales_loaded.at(DEPTH, 0))
            sp.wait_ge(ffn_loaded.sem, ffn_loaded.at(DEPTH, 0))

        @block.tensor
        def _(pe):
            def values(it, p):
                f, t0 = V_STEPS[p]
                for i in range(4):
                    k = 4 * sorted(V_STEPS).index(p) + i
                    mm = pe.matmul(bank[i][0:KB, :], xs[:, (t0 + i) * QB:(t0 + i) * QB + KB],
                                   w_qkv[:, 2 * INNER + f * 512:2 * INNER + (f + 1) * 512],
                                   start=True, stop=True)
                    mm.then_inc(v_ready.sem, 1)

            def project(it, p, j, first):
                k = 2 * p + j
                if p in V_STEPS:
                    pe.wait_ge(v_copied.sem, v_copied.at(it, 4 * sorted(V_STEPS).index(p) + 2 * (j + 1)))
                elif not first or p >= 1:
                    pe.wait_ge(t_ready.sem, t_ready.at(it, 2 * (k - 1)))
                col = j * INNER + p * P
                pe.matmul(bank[2 * j][:, :], w_qkv[:, col:col + P], xs[:, LOOK:], start=True, stop=True)
                pe.matmul(bank[2 * j + 1][:, :], w_rot[:, col:col + P], xs[:, LOOK:],
                          start=True, stop=True).then_inc(rt_ready.sem, 1)

            def norm(it, p, j, first):
                k = 2 * p + j
                pe.wait_ge(sq_ready.sem, sq_ready.at(it, k + 1))
                if not first or k >= 1:
                    pe.wait_ge(guarded.sem, guarded.at(it, k))
                pe.matmul(bank[4][:, :], const["heads"][:, :], sq[:, j, :],
                          start=True, stop=True).then_inc(n_ready.sem, 1)

            def scores(it, p, f, first):
                g = 2 * p + f
                if f == 0:
                    pe.wait_ge(rotated.sem, rotated.at(it, 2 * p + 2))
                if not first or g >= 1:
                    pe.wait_ge(masked.sem, masked.at(it, g))
                pe.nop(nofuse=True)
                for i in range(HALF):
                    t = HALF * f + i
                    for a in range(2):
                        r = slice(a * HD, (a + 1) * HD)
                        mm = pe.matmul(bank[5][r, i * KB:(i + 1) * KB], qT[r, p % 2, t * QB:(t + 1) * QB],
                                       kT[r, p % 2, t * QB:t * QB + KB], start=True, stop=True,
                                       skip_group_check=True)
                mm.then_inc(s_ready.sem, 1)

            def turn(it, p, f, first):
                g = 2 * p + f
                pe.wait_ge(p_ready.sem, p_ready.at(it, g + 1))
                if not first or g >= 1:
                    pe.wait_ge(pt_copied.sem, pt_copied.at(it, g))
                for i in range(HALF):
                    mm = pe.transpose(bank[6][0:KB, i * P:(i + 1) * P], pn[:, f, i * KB:(i + 1) * KB],
                                      const["ident"][:, :])
                mm.then_inc(pt_ready.sem, 1)

            def mix(it, p, f, first):
                g = 2 * p + f
                if f == 0 and p in (0, 4):
                    pe.wait_ge(v_copied.sem, v_copied.at(it, 8 + 8 * (p // 4)))
                pe.wait_ge(pt_copied.sem, pt_copied.at(it, g + 1))
                if f == 0 and (not first or p >= 1):
                    pe.wait_ge(o_copied.sem, o_copied.at(it, p))
                pe.nop(nofuse=True)
                for i in range(HALF):
                    t = HALF * f + i
                    for a in range(2):
                        mm = pe.matmul(bank[7][a * HD:(a + 1) * HD, t * QB:(t + 1) * QB],
                                       vals[:, t, ((2 * p + a) * HD) % INNER:((2 * p + a) * HD) % INNER + HD],
                                       pT[:, f, i * P + a * QB:i * P + (a + 1) * QB],
                                       start=True, stop=True, skip_group_check=True)
                mm.then_inc(pv_done.sem, 1)

            def attention_out(it, ft):
                pe.wait_ge(ffn_loaded.sem, layer_loads(ffn_loaded, ft))
                pe.wait_ge(o_copied.sem, o_copied.at(ft, PAIRS))
                pe.wait_ge(guarded.sem, guarded.at(it, 4) if it is not ft else guarded.at(ft, TILES))
                for p in range(PAIRS):
                    mm = pe.matmul(bank[4][:, :], w_o[:, p, :], oT[:, p, :], start=(p == 0), stop=(p == PAIRS - 1))
                mm.then_inc(wo_done.sem, 1)

            def mean(ft):
                pe.wait_ge(fs_ready.sem, fs_ready.at(ft, 2))
                pe.matmul(bank[4][:, :], const["mean"][:, :], fs[:, :], start=True, stop=True)\
                  .then_inc(mean_ready.sem, 1)

            def variance(ft):
                pe.wait_ge(csq_ready.sem, csq_ready.at(ft, 1))
                pe.matmul(bank[4][:, :], const["mean"][:, :], csq[:, :], start=True, stop=True)\
                  .then_inc(var_ready.sem, 1)

            def gate_up(ft, i):
                pe.wait_ge(xn_ready.sem, xn_ready.at(ft, 1))
                if i >= 1:
                    pe.wait_ge(gate_ready.sem, gate_ready.at(ft, i))
                c = 341 + i * HID
                pe.matmul(bank[4][0:HR[i], :], w_1[:, c:c + HR[i]], xn[:, :],
                          start=True, stop=True).then_inc(gate_up_ready.sem, 1)

            def linear_up(ft, i):
                if i == 0:
                    pe.wait_ge(gate_ready.sem, gate_ready.at(ft, HT))
                else:
                    pe.wait_ge(hid_ready.sem, hid_ready.at(ft, i))
                c = i * HID
                pe.matmul(bank[4][0:HR[i], :], w_1[:, c:c + HR[i]], xn[:, :],
                          start=True, stop=True).then_inc(up_ready.sem, 1)

            def down(ft):
                pe.wait_ge(hid_ready.sem, hid_ready.at(ft, HT))
                for i in range(HT):
                    mm = pe.matmul(bank[4][:, :], w_2[0:HR[i], i, :], hid[0:HR[i], i, :],
                                   start=(i == 0), stop=(i == HT - 1))
                mm.then_inc(down_ready.sem, 1)

            def body(it, first):
                ft = it - 1
                for p in range(PAIRS):
                    if p == 0:
                        pe.wait_ge(low_loaded.sem, layer_loads(low_loaded, it))
                    if p == 4:
                        pe.wait_ge(high_loaded.sem, layer_loads(high_loaded, it))
                    if p in V_STEPS:
                        if not first or p > 0:
                            pe.wait_ge(t_ready.sem, t_ready.at(it, 4 * p))
                        if p == 0:
                            pe.wait_ge(shifted.sem, shifted.at(it, 2))
                        values(it, p)
                    if p in V_STEPS and (not first or p >= 2):
                        turn(it, p - 2, 0, first)
                    if p in (3, 4) and not first:
                        pe.wait_ge(guarded.sem, guarded.at(it, 2 * p))
                        if p == 3:
                            mean(ft)
                        else:
                            variance(ft)
                    project(it, p, 0, first)
                    if p not in V_STEPS and (not first or p >= 2):
                        turn(it, p - 2, 0, first)
                    if not first:
                        if p == 2:
                            attention_out(it, ft)
                        if p >= 5:
                            pe.wait_ge(guarded.sem, guarded.at(it, 2 * p))
                        if p == 5:
                            gate_up(ft, 0)
                        if p == 6:
                            linear_up(ft, 0)
                    project(it, p, 1, first)
                    if not first:
                        if p == 5:
                            gate_up(ft, 1)
                        if p == 6:
                            linear_up(ft, 1)
                        if p == 7:
                            down(ft)
                    if not first or p >= 2:
                        mix(it, p - 2, 0, first)
                        turn(it, p - 2, 1, first)
                    if not first:
                        if p == 5:
                            gate_up(ft, 2)
                        if p == 6:
                            linear_up(ft, 2)
                    if not first or p >= 1:
                        scores(it, p - 1, 0, first)
                    if not first:
                        if p == 2:
                            pe.wait_ge(x1_ready.sem, x1_ready.at(ft, 1))
                        if p == 3:
                            pe.wait_ge(cen_ready.sem, cen_ready.at(ft, 1))
                        if p == 4:
                            pe.wait_ge(lv_ready.sem, lv_ready.at(ft, 1))
                        if p == 5:
                            pe.wait_ge(gate_ready.sem, gate_ready.at(ft, HT))
                        if p == 6:
                            pe.wait_ge(hid_ready.sem, hid_ready.at(ft, HT))
                        if p == 7:
                            pe.wait_ge(x_done.sem, ft + LEAD + 1)
                    norm(it, p, 0, first)
                    if not first or p >= 2:
                        mix(it, p - 2, 1, first)
                    if not first or p >= 1:
                        scores(it, p - 1, 1, first)
                    norm(it, p, 1, first)

            def rest(it):
                ft = it - 1
                turn(it, -2, 0, False)
                mix(it, -2, 0, False)
                turn(it, -2, 1, False)
                mix(it, -2, 1, False)
                scores(it, -1, 0, False)
                scores(it, -1, 1, False)
                turn(it, -1, 0, False)
                mix(it, -1, 0, False)
                turn(it, -1, 1, False)
                mix(it, -1, 1, False)
                attention_out(ft, ft)
                mean(ft)
                variance(ft)
                for i in range(HT):
                    gate_up(ft, i)
                for i in range(HT):
                    linear_up(ft, i)
                down(ft)

            body(0, True)
            with pe.Fori(1, PASSES) as it:
                body(it, False)
            rest(PASSES)

        @block.scalar
        def _(act):
            def square(it, p, j, first):
                k = 2 * p + j
                act.wait_ge(rt_ready.sem, rt_ready.at(it, k + 1))
                if not first or p >= 1:
                    act.wait_ge(n_ready.sem, n_ready.at(it, k - 1))
                act.activation(sq[:, j, :], bank[2 * j][:, :], ACT.Square).then_inc(sq_ready.sem, 1)

            def inverse_norm(it, p, j, first):
                k = 2 * p + j
                act.wait_ge(guarded.sem, guarded.at(it, k + 1))
                act.activation(lnn[:, j, :], nrm[:, j, :], ACT.Ln, scale=NORM_SHIFT).then_inc(ln_ready.sem, 1)
                act.wait_ge(ln_ready.sem, ln_ready.at(it, k + 1))
                if not first or p >= 1:
                    act.wait_ge(rotated.sem, rotated.at(it, k - 1))
                act.activation(rn[:, j, :], lnn[:, j, :], ACT.Exp, scale=-0.5,
                               bias=const["unshift"][:, 0:1]).then_inc(rn_ready.sem, 1)

            def exponential(it, p, f, first):
                g = 2 * p + f
                act.wait_ge(sub_ready.sem, sub_ready.at(it, g + 1))
                if not first or p >= 1:
                    act.wait_ge(p_ready.sem, p_ready.at(it, g - 1))
                act.activation(pr[:, f, :], sc[:, f, :], ACT.Exp, scale=QK_SCALE).then_inc(exp_ready.sem, 1)

            def copy_turned(it, p, f, first):
                g = 2 * p + f
                act.wait_ge(pt_ready.sem, pt_ready.at(it, g + 1))
                if not first or p >= 1:
                    act.wait_ge(pv_done.sem, pv_done.at(it, g - 1))
                act.activation(pT[:, f, :], bank[6][0:KB, :], ACT.Copy).then_inc(pt_copied.sem, 1)

            def copy_mixed(it, p, first):
                act.wait_ge(pv_done.sem, pv_done.at(it, 2 * p + 2))
                if p == 0 and not first:
                    act.wait_ge(wo_done.sem, wo_done.at(it, 0))
                act.activation(oT[:, p % PAIRS, :], bank[7][:, :], ACT.Copy).then_inc(o_copied.sem, 1)

            def copy_values(it, p):
                f, t0 = V_STEPS[p]
                for i in range(4):
                    act.wait_ge(v_ready.sem, v_ready.at(it, 4 * sorted(V_STEPS).index(p) + i + 1))
                    act.activation(vals[:, t0 + i, f * 512:(f + 1) * 512], bank[i][0:KB, :],
                                   ACT.Copy).then_inc(v_copied.sem, 1)

            def center_square(ft):
                act.wait_ge(cen_ready.sem, cen_ready.at(ft, 1))
                act.activation(csq[:, :], cen[:, :], ACT.Square).then_inc(csq_ready.sem, 1)

            def inverse_deviation(ft):
                act.wait_ge(var_ready.sem, var_ready.at(ft, 1))
                act.activation(lv[:, :], bank[4][:, :], ACT.Ln, bias=const["eps"][:, 0:1]).then_inc(lv_ready.sem, 1)
                act.wait_ge(lv_ready.sem, lv_ready.at(ft, 1))
                act.activation(rstd[:, :], lv[:, :], ACT.Exp, scale=-0.5).then_inc(rstd_ready.sem, 1)

            def gelu(ft, i):
                r = slice(0, HR[i])
                act.wait_ge(gate_up_ready.sem, gate_up_ready.at(ft, i + 1))
                act.activation(hid[r, i, :], bank[4][r, :], ACT.Gelu,
                               bias=chan[r, 6 + i:7 + i]).then_inc(gate_ready.sem, 1)

            def body(it, first):
                ft = it - 1
                if not first:
                    act.wait_ge(ffn_loaded.sem, layer_loads(ffn_loaded, ft))
                    act.nop(nofuse=True)
                for p in range(PAIRS):
                    if p == 5 and not first:
                        act.preload_act_table_set(GELU_SET)
                    if p in V_STEPS:
                        copy_values(it, p)
                    if p == 4 and not first:
                        inverse_deviation(ft)
                    square(it, p, 0, first)
                    if p == 5 and not first:
                        gelu(ft, 0)
                    if not first or p >= 2:
                        copy_turned(it, p - 2, 0, first)
                    square(it, p, 1, first)
                    if p == 5 and not first:
                        gelu(ft, 1)
                    if not first or p >= 2:
                        copy_turned(it, p - 2, 1, first)
                    if not first:
                        if p == 5:
                            gelu(ft, 2)
                            act.preload_act_table_set(EXP_LN_SET)
                    if p == 0:
                        act.preload_act_table_set(EXP_LN_SET)
                    if not first or p >= 1:
                        exponential(it, p - 1, 0, first)
                    inverse_norm(it, p, 0, first)
                    if not first or p >= 2:
                        copy_mixed(it, p - 2, first)
                    if not first or p >= 1:
                        exponential(it, p - 1, 1, first)
                    inverse_norm(it, p, 1, first)
                    if p == 3 and not first:
                        center_square(ft)

            def rest(it):
                ft = it - 1
                act.preload_act_table_set(EXP_LN_SET)
                copy_turned(it, -2, 0, False)
                copy_turned(it, -2, 1, False)
                copy_mixed(it, -2, False)
                exponential(it, -1, 0, False)
                exponential(it, -1, 1, False)
                copy_turned(it, -1, 0, False)
                copy_turned(it, -1, 1, False)
                copy_mixed(it, -1, False)
                center_square(ft)
                inverse_deviation(ft)
                act.preload_act_table_set(GELU_SET)
                for i in range(HT):
                    gelu(ft, i)

            act.wait_ge(zeroed.sem, 5)
            body(0, True)
            with act.Fori(1, PASSES) as it:
                body(it, False)
            rest(PASSES)

        @block.vector
        def _(ve):
            def rotate(it, p, j, first):
                k = 2 * p + j
                ve.wait_ge(rt_ready.sem, rt_ready.at(it, k + 1))
                if not first or p >= 1:
                    ve.wait_ge(rotated.sem, rotated.at(it, k - 1))
                c = 2 * j + 1
                ve.scalar_tensor_tensor(out=t2[:, j, :], in0=bank[c][:, :], scalar=chan_a[:, c:c + 1],
                                        in1=base[:, c, :], op0=ALU.mult, op1=ALU.mult).then_inc(t_ready.sem, 1)
                ve.wait_ge(sq_ready.sem, sq_ready.at(it, k + 1))
                c = 2 * j
                ve.scalar_tensor_tensor(out=t1[:, j, :], in0=bank[c][:, :], scalar=chan_a[:, c:c + 1],
                                        in1=base[:, c, :], op0=ALU.mult, op1=ALU.mult).then_inc(t_ready.sem, 1)

            def guard(it, p, j, first):
                k = 2 * p + j
                ve.wait_ge(n_ready.sem, n_ready.at(it, k + 1))
                if not first or p >= 1:
                    ve.wait_ge(ln_ready.sem, ln_ready.at(it, k - 1))
                ve.tensor_scalar(nrm[:, j, :], bank[4][:, :], 1e-24, None, ALU.max).then_inc(guarded.sem, 1)

            def center(it, p, f, first):
                g = 2 * p + f
                sc3 = sc[:, f, :].rearrange("p (i k) -> p i k", k=KB)
                ve.wait_ge(s_ready.sem, s_ready.at(it, g + 1))
                if not first or p >= 1:
                    ve.wait_ge(exp_ready.sem, exp_ready.at(it, g - 1))
                ve.tensor_tensor(sc[:, f, :], bank[5][:, 0:HALF * KB], mask[:, f, :], ALU.add).then_inc(masked.sem, 1)
                ve.wait_ge(masked.sem, masked.at(it, g + 1))
                ve.tensor_reduce(mx[:, f, :], sc3, AX.X, ALU.max).then_inc(mx_ready.sem, 1)
                ve.wait_ge(mx_ready.sem, mx_ready.at(it, g + 1))
                ve.tensor_tensor(sc3, sc3, mx[:, f, :].unsqueeze(2).to_broadcast([P, HALF, KB]),
                                 ALU.subtract).then_inc(sub_ready.sem, 1)

            def denominator(it, p, f, first):
                g = 2 * p + f
                ve.wait_ge(exp_ready.sem, exp_ready.at(it, g + 1))
                ve.tensor_reduce(den[:, f, :], pr[:, f, :].rearrange("p (i k) -> p i k", k=KB), AX.X,
                                 ALU.add).then_inc(den_ready.sem, 1)
                ve.wait_ge(den_ready.sem, den_ready.at(it, g + 1))
                if not first or p >= 1:
                    ve.wait_ge(p_ready.sem, p_ready.at(it, g - 1))
                ve.reciprocal(rden[:, f, :], den[:, f, :]).then_inc(rden_ready.sem, 1)

            def residual(ft, b):
                ve.wait_ge(wo_done.sem, wo_done.at(ft, 1))
                ve.tensor_tensor(xT[:, tokens(b)], bank[4][:, :], xT[:, tokens(b)], ALU.add).then_inc(x1_ready.sem, 1)
                ve.wait_ge(x1_ready.sem, x1_ready.at(ft, 1))
                ve.nop(nofuse=True)
                ve.tensor_copy(fs[0:HD, :], xT[0:HD, tokens(b)]).then_inc(fs_ready.sem, 1)
                ve.tensor_copy(fs[HD:P, 1:], xT[HD:P, bass.ds(b * T, T - 1)]).then_inc(fs_ready.sem, 1)

            def subtract_mean(ft):
                ve.wait_ge(fs_ready.sem, fs_ready.at(ft, 2))
                ve.wait_ge(mean_ready.sem, mean_ready.at(ft, 1))
                ve.tensor_tensor(cen[:, :], fs[:, :], bank[4][:, :], ALU.subtract).then_inc(cen_ready.sem, 1)

            def scale_normed(ft):
                ve.wait_ge(rstd_ready.sem, rstd_ready.at(ft, 1))
                ve.tensor_tensor(xn[:, :], cen[:, :], rstd[:, :], ALU.mult).then_inc(xh_ready.sem, 1)
                ve.wait_ge(xh_ready.sem, xh_ready.at(ft, 1))
                ve.tensor_scalar(xn[:, :], xn[:, :], chan[:, 0:1], chan[:, 1:2], ALU.mult, ALU.add)\
                  .then_inc(xn_ready.sem, 1)

            def gated(ft, i):
                r = slice(0, HR[i])
                ve.wait_ge(gate_ready.sem, gate_ready.at(ft, i + 1))
                ve.wait_ge(up_ready.sem, up_ready.at(ft, i + 1))
                ve.scalar_tensor_tensor(out=hid[r, i, :], in0=bank[4][r, :], scalar=chan[r, 3 + i:4 + i],
                                        in1=hid[r, i, :], op0=ALU.add, op1=ALU.mult)\
                  .then_inc(hid_ready.sem, 1)

            def finish(ft, b):
                ve.wait_ge(down_ready.sem, down_ready.at(ft, 1))
                ve.scalar_tensor_tensor(out=xT[:, tokens(b)], in0=bank[4][:, :], scalar=chan[:, 2:3],
                                        in1=xT[:, tokens(b)], op0=ALU.add, op1=ALU.add).then_inc(x_done.sem, 1)

            def shift(b):
                ve.tensor_copy(xs[0:HD, LOOK:], xT[0:HD, tokens(b)]).then_inc(shifted.sem, 1)
                ve.tensor_copy(xs[HD:P, LOOK + 1:], xT[HD:P, bass.ds(b * T, T - 1)]).then_inc(shifted.sem, 1)

            def body(it, first):
                ft = it - 1
                ve.wait_ge(scales_loaded.sem, layer_loads(scales_loaded, it))
                ve.nop(nofuse=True)
                for p in range(PAIRS):
                    if p == 3 and not first:
                        subtract_mean(ft)
                    rotate(it, p, 0, first)
                    if p == 2 and not first:
                        residual(ft, (it + SEQS - 1) % SEQS)
                    if p == 6 and not first:
                        gated(ft, 0)
                    rotate(it, p, 1, first)
                    if not first:
                        if p == 4:
                            scale_normed(ft)
                        if p == 6:
                            gated(ft, 1)
                            gated(ft, 2)
                        if p == 7:
                            finish(ft, (it + SEQS - 1) % SEQS)
                    if p == 7:
                        ve.wait_ge(x_done.sem, it + 2)
                        ve.wait_ge(rt_ready.sem, rt_ready.at(it, TILES))
                        ve.nop(nofuse=True)
                        shift((it + 1) % SEQS)
                    if not first or p >= 1:
                        center(it, p - 1, 0, first)
                    guard(it, p, 0, first)
                    if not first or p >= 1:
                        denominator(it, p - 1, 0, first)
                        center(it, p - 1, 1, first)
                    guard(it, p, 1, first)
                    if not first or p >= 1:
                        denominator(it, p - 1, 1, first)

            def rest(it):
                ft = it - 1
                center(it, -1, 0, False)
                center(it, -1, 1, False)
                denominator(it, -1, 0, False)
                denominator(it, -1, 1, False)
                residual(ft, SEQS - 1)
                subtract_mean(ft)
                scale_normed(ft)
                for i in range(HT):
                    gated(ft, i)
                finish(ft, SEQS - 1)

            ve.memset(xs[:, 0:LOOK], 0.0).then_inc(zeroed.sem, 1)
            ve.memset(xs[HD:P, LOOK:LOOK + 1], 0.0).then_inc(zeroed.sem, 1)
            ve.memset(fs[HD:P, 0:1], 0.0).then_inc(zeroed.sem, 1)
            ve.memset(kT[:, :, 0:LOOK], 0.0).then_inc(zeroed.sem, 1)
            ve.tensor_copy(x0T[:, :], xT[:, :]).then_inc(zeroed.sem, 1)
            ve.wait_ge(zeroed.sem, 5)
            ve.sem_inc(x_done.sem, LEAD)
            shift(0)
            ve.wait_ge(fixed_loaded.sem, 16 * 2)
            ve.nop(nofuse=True)
            body(0, True)
            with ve.Fori(1, PASSES) as it:
                ve.wait_ge(ffn_loaded.sem, layer_loads(ffn_loaded, it - 1))
                ve.nop(nofuse=True)
                body(it, False)
            rest(PASSES)

        @block.gpsimd
        def _(pool):
            def join(it, p, j):
                k = 2 * p + j
                pool.wait_ge(t_ready.sem, t_ready.at(it, 2 * k + 2))
                pool.tensor_tensor(t1[:, j, :], t1[:, j, :], t2[:, j, :], ALU.add).then_inc(added.sem, 1)

            def normalise(it, p, j, first):
                k = 2 * p + j
                pool.wait_ge(rn_ready.sem, rn_ready.at(it, k + 1))
                pool.wait_ge(added.sem, added.at(it, k + 1))
                if not first or p >= 2:
                    pool.wait_ge(s_ready.sem, s_ready.at(it, 2 * (p - 2) + 2))
                dst = kT[:, p % 2, LOOK:] if j else qT[:, p % 2, :]
                pool.tensor_tensor(dst, t1[:, j, :], rn[:, j, :], ALU.mult).then_inc(rotated.sem, 1)

            def probabilities(it, p, f, first):
                g = 2 * p + f
                pool.wait_ge(rden_ready.sem, rden_ready.at(it, g + 1))
                if not first or p >= 1:
                    pool.wait_ge(pt_ready.sem, pt_ready.at(it, g - 1))
                pool.tensor_tensor(pn[:, f, :].rearrange("p (i k) -> p i k", k=KB),
                                   pr[:, f, :].rearrange("p (i k) -> p i k", k=KB),
                                   rden[:, f, :].unsqueeze(2).to_broadcast([P, HALF, KB]),
                                   ALU.mult).then_inc(p_ready.sem, 1)

            def body(it, first):
                for p in range(PAIRS):
                    join(it, p, 0)
                    join(it, p, 1)
                    if not first or p >= 1:
                        probabilities(it, p - 1, 0, first)
                    normalise(it, p, 0, first)
                    normalise(it, p, 1, first)
                    if not first or p >= 1:
                        probabilities(it, p - 1, 1, first)

            pool.wait_ge(zeroed.sem, 5)
            body(0, True)
            with pool.Fori(1, PASSES) as it:
                body(it, False)
            probabilities(PASSES, -1, 0, False)
            probabilities(PASSES, -1, 1, False)


def layer_norm_phase(nc, prefix, xT, x0T, const):
    with ExitStack() as ctx:
        m = Memory(ctx, nc, prefix)
        res = m.sb("res", [P, T])
        cen = m.sb("cen", [P, T])
        sq = m.sb("sq", [P, T])
        lv = m.sb("lv", [P, T])
        rstd = m.sb("rstd", [P, T])
        bank = [m.bank(f"bank{i}") for i in range(2)]
        res_ready, mean_ready, cen_ready = m.counter("res_ready"), m.counter("mean_ready"), m.counter("cen_ready")
        sq_ready, var_ready, lv_ready = m.counter("sq_ready"), m.counter("var_ready"), m.counter("lv_ready")
        rstd_ready, x_written = m.counter("rstd_ready"), m.counter("x_written")
        block = ctx.enter_context(nc.Block())

        @block.tensor
        def _(pe):
            with pe.Fori(0, SEQS) as b:
                pe.wait_ge(res_ready.sem, b + 1)
                pe.matmul(bank[0][:, :], const["mean"][:, :], res[:, :], start=True, stop=True).then_inc(mean_ready.sem, 1)
                pe.wait_ge(sq_ready.sem, b + 1)
                pe.matmul(bank[1][:, :], const["mean"][:, :], sq[:, :], start=True, stop=True).then_inc(var_ready.sem, 1)

        @block.scalar
        def _(act):
            with act.Fori(0, SEQS) as b:
                act.preload_act_table_set(EXP_LN_SET)
                act.wait_ge(cen_ready.sem, b + 1)
                act.activation(sq[:, :], cen[:, :], ACT.Square).then_inc(sq_ready.sem, 1)
                act.wait_ge(var_ready.sem, b + 1)
                act.activation(lv[:, :], bank[1][:, :], ACT.Ln, bias=const["eps"][:, 0:1]).then_inc(lv_ready.sem, 1)
                act.wait_ge(lv_ready.sem, b + 1)
                act.activation(rstd[:, :], lv[:, :], ACT.Exp, scale=-0.5).then_inc(rstd_ready.sem, 1)

        @block.vector
        def _(ve):
            with ve.Fori(0, SEQS) as b:
                x = xT[:, bass.ds(b * T, T)]
                ve.tensor_tensor(res[:, :], x, x0T[:, bass.ds(b * T, T)], ALU.add).then_inc(res_ready.sem, 1)
                ve.wait_ge(res_ready.sem, b + 1)
                ve.wait_ge(mean_ready.sem, b + 1)
                ve.tensor_tensor(cen[:, :], res[:, :], bank[0][:, :], ALU.subtract).then_inc(cen_ready.sem, 1)
                ve.wait_ge(cen_ready.sem, b + 1)
                ve.wait_ge(rstd_ready.sem, b + 1)
                ve.tensor_tensor(x, cen[:, :], rstd[:, :], ALU.mult).then_inc(x_written.sem, 1)



def expert_phase(nc, prefix, xT, const, w, out):
    EXPERTS = 8
    ET = 12
    TB = T // P
    with ExitStack() as ctx:
        m = Memory(ctx, nc, prefix)
        wr = m.sb("wr", [P, EXPERTS])
        w1 = m.sb("w1", [P, ET * P])
        w3 = m.sb("w3", [P, ET * P])
        w2 = m.sb("w2", [P, ET, P])
        owner = m.sb("owner", [72, ET, P], BF16)
        part = m.sb("part", [P, 2])
        iota = m.sb("iota", [P, EXPERTS])
        xm = m.sb("xm", [P, T])
        logit = m.sb("logit", [P, TB, EXPERTS])
        top = m.sb("top", [P, TB, 8])
        topi = m.sb("topi", [P, TB, 8], U32)
        topf = m.sb("topf", [P, TB, 8])
        gap = m.sb("gap", [P, TB])
        eg = m.sb("eg", [P, TB])
        sg = m.sb("sg", [P, TB])
        wt = m.sb("wt", [P, 2, TB])
        first_choice = m.sb("first_choice", [P, TB, EXPERTS])
        second_choice = m.sb("second_choice", [P, TB, EXPERTS])
        comb3 = m.sb("comb3", [P, TB, 96])
        part_a = m.sb("part_a", [72, T], BF16)
        rest_a = m.sb("rest_a", [72, T])
        part_b = m.sb("part_b", [72, T], BF16)
        combT = m.sb("combT", [72, T], BF16)
        act_h = m.sb("act_h", [P, 2, T])
        prod = m.sb("prod", [P, 2, T])
        hid = m.sb("hid", [P, 2, T])
        res = m.sb("res", [P, T])
        cen = m.sb("cen", [P, T])
        sq = m.sb("sq", [P, T])
        lv = m.sb("lv", [P, T])
        rstd = m.sb("rstd", [P, T])
        fin = m.sb("fin", [P, T])
        bank = [m.bank(f"bank{i}") for i in range(8)]

        loaded = m.counter("loaded")
        comb_zeroed = m.counter("comb_zeroed")
        xm_ready = m.counter("xm_ready")
        logits_ready = m.counter("logits_ready")
        logit_copied = m.counter("logit_copied")
        top_ready = m.counter("top_ready", TB)
        topi_ready = m.counter("topi_ready", TB)
        gap_ready = m.counter("gap_ready", 2)
        eg_ready = m.counter("eg_ready")
        wt_steps = m.counter("wt_steps", 3)
        chosen = m.counter("chosen", 2 * TB)
        comb_ready = m.counter("comb_ready", 3)
        comb_turned = m.counter("comb_turned")
        split_steps = m.counter("split_steps", 4)
        h_ready = m.counter("h_ready", ET)
        g_ready = m.counter("g_ready", ET)
        cb_ready = m.counter("cb_ready", ET)
        silu_ready = m.counter("silu_ready", ET)
        prod_ready = m.counter("prod_ready", ET)
        hid_ready = m.counter("hid_ready", ET)
        hid_used = m.counter("hid_used", ET)
        res_ready = m.counter("res_ready")
        mean_ready = m.counter("mean_ready")
        cen_ready = m.counter("cen_ready")
        sq_ready = m.counter("sq_ready")
        var_ready = m.counter("var_ready")
        lv_ready = m.counter("lv_ready")
        rstd_ready = m.counter("rstd_ready")
        fin_ready = m.counter("fin_ready")
        stored = m.counter("stored")

        block = ctx.enter_context(nc.Block())
        N_LOADS = 7

        def tokens(b):
            return bass.ds(b * T, T)

        @block.sync
        def _(sp):
            for dst, name in ((wr, "wr"), (w1, "w1"), (w3, "w3"), (part, "part"), (iota, "iota")):
                sp.dma_start(dst[:, :], w[name]).then_inc(loaded.sem, 16)
            for dst, name in ((w2, "w2"), (owner, "owner")):
                sp.dma_start(dst[:, :, :], w[name]).then_inc(loaded.sem, 16)
            with sp.Fori(0, SEQS) as b:
                sp.wait_ge(fin_ready.sem, b + 1)
                sp.dma_start(out[:, bass.ds(b * T, T)], fin[:, :]).then_inc(stored.sem, 16)
            sp.wait_ge(loaded.sem, 16 * N_LOADS)
            sp.wait_ge(stored.sem, 16 * SEQS + 1)

        @block.tensor
        def _(pe):
            def route(r):
                pe.wait_ge(xm_ready.sem, xm_ready.at(r, 1))
                for t in range(TB):
                    mm = pe.matmul(bank[7][:, t * EXPERTS:(t + 1) * EXPERTS], xm[:, t * P:(t + 1) * P], wr[:, :],
                                   start=True, stop=True, skip_group_check=True)
                mm.then_inc(logits_ready.sem, 1)

            def turn(r):
                pe.wait_ge(comb_ready.sem, comb_ready.at(r, 3))
                for t in range(TB):
                    mm = pe.transpose(bank[7][0:96, t * P:(t + 1) * P], comb3[:, t, :], const["ident"][:, :])
                mm.then_inc(comb_turned.sem, 1)

            def up(b, j, first):
                if not first or j >= 2:
                    pe.wait_ge(hid_ready.sem, hid_ready.at(b, j - 1))
                pe.matmul(bank[j % 2][:, :], w1[:, j * P:(j + 1) * P], xT[:, tokens(b)],
                          start=True, stop=True).then_inc(h_ready.sem, 1)
                pe.matmul(bank[2 + j % 2][:, :], w3[:, j * P:(j + 1) * P], xT[:, tokens(b)],
                          start=True, stop=True).then_inc(g_ready.sem, 1)
                if j == 0:
                    pe.wait_ge(split_steps.sem, split_steps.at(b, 4))
                pe.matmul(bank[4 + j % 2][:, :], owner[:, j, :], combT[:, :],
                          start=True, stop=True).then_inc(cb_ready.sem, 1)

            def down(b, j, first):
                if j == 0 and not first:
                    pe.wait_ge(res_ready.sem, res_ready.at(b, 0))
                pe.wait_ge(hid_ready.sem, hid_ready.at(b, j + 1))
                pe.matmul(bank[6][:, :], w2[:, j, :], hid[:, j % 2, :],
                          start=(j == 0), stop=(j == ET - 1)).then_inc(hid_used.sem, 1)

            def mean(b):
                pe.wait_ge(res_ready.sem, res_ready.at(b, 1))
                pe.matmul(bank[7][:, :], const["mean"][:, :], res[:, :], start=True, stop=True).then_inc(mean_ready.sem, 1)

            def variance(b):
                pe.wait_ge(sq_ready.sem, sq_ready.at(b, 1))
                pe.matmul(bank[7][:, :], const["mean"][:, :], sq[:, :], start=True, stop=True).then_inc(var_ready.sem, 1)

            def body(b, first):
                for j in range(ET):
                    up(b, j, first)
                    if j >= 1:
                        down(b, j - 1, first)
                    elif not first:
                        down(b - 1, ET - 1, False)
                    if j == 1:
                        pe.wait_ge(split_steps.sem, split_steps.at(b, 4))
                        route(b + 1)
                    if j == 2 and not first:
                        pe.wait_ge(logit_copied.sem, logit_copied.at(b + 1, 1))
                        mean(b - 1)
                    if j == 4 and not first:
                        variance(b - 1)
                    if j == 8:
                        pe.wait_ge(logit_copied.sem, logit_copied.at(b + 1, 1))
                        if not first:
                            pe.wait_ge(lv_ready.sem, lv_ready.at(b, 0))
                        turn(b + 1)

            pe.wait_ge(loaded.sem, 16 * N_LOADS)
            route(0)
            pe.wait_ge(logit_copied.sem, 1)
            turn(0)
            body(0, True)
            with pe.Fori(1, SEQS) as b:
                body(b, False)
            down(SEQS - 1, ET - 1, False)
            pe.wait_ge(split_steps.sem, split_steps.at(SEQS, 2))
            mean(SEQS - 1)
            variance(SEQS - 1)

        @block.scalar
        def _(act):
            def weight(r):
                act.wait_ge(gap_ready.sem, gap_ready.at(r, 1))
                act.activation(eg[:, :], gap[:, :], ACT.Exp).then_inc(eg_ready.sem, 1)

            def first_part(r):
                act.wait_ge(comb_turned.sem, comb_turned.at(r, 1))
                act.activation(part_a[:, :], bank[7][0:72, :], ACT.Copy).then_inc(split_steps.sem, 1)

            def square(b):
                act.wait_ge(cen_ready.sem, cen_ready.at(b, 1))
                act.activation(sq[:, :], cen[:, :], ACT.Square).then_inc(sq_ready.sem, 1)

            def inverse_deviation(b):
                act.wait_ge(var_ready.sem, var_ready.at(b, 1))
                act.activation(lv[:, :], bank[7][:, :], ACT.Ln, bias=const["eps"][:, 0:1]).then_inc(lv_ready.sem, 1)
                act.wait_ge(lv_ready.sem, lv_ready.at(b, 1))
                act.activation(rstd[:, :], lv[:, :], ACT.Exp, scale=-0.5).then_inc(rstd_ready.sem, 1)

            def body(b, first):
                act.preload_act_table_set(SILU_SET)
                for j in range(ET):
                    act.wait_ge(h_ready.sem, h_ready.at(b, j + 1))
                    if not first or j >= 2:
                        act.wait_ge(prod_ready.sem, prod_ready.at(b, j - 1))
                    act.activation(act_h[:, j % 2, :], bank[j % 2][:, :], ACT.Silu).then_inc(silu_ready.sem, 1)
                    if j == 3 and not first:
                        square(b - 1)
                    if j == 5:
                        act.preload_act_table_set(EXP_LN_SET)
                        weight(b + 1)
                        if not first:
                            inverse_deviation(b - 1)
                        act.preload_act_table_set(SILU_SET)
                    if j == 9:
                        first_part(b + 1)

            act.preload_act_table_set(EXP_LN_SET)
            weight(0)
            first_part(0)
            body(0, True)
            with act.Fori(1, SEQS) as b:
                body(b, False)
            act.preload_act_table_set(EXP_LN_SET)
            square(SEQS - 1)
            inverse_deviation(SEQS - 1)

        @block.vector
        def _(ve):
            def load_x(r, q):
                ve.wait_ge(logits_ready.sem, logits_ready.at(r, 0))
                ve.nop(nofuse=True)
                ve.tensor_copy(xm[:, :], xT[:, tokens(q)]).then_inc(xm_ready.sem, 1)

            def find_two(r):
                ve.wait_ge(logits_ready.sem, logits_ready.at(r, 1))
                ve.tensor_copy(logit[:, :, :], bank[7][:, 0:TB * EXPERTS].rearrange("p (t e) -> p t e", e=EXPERTS))\
                  .then_inc(logit_copied.sem, 1)
                ve.wait_ge(logit_copied.sem, logit_copied.at(r, 1))
                ve.nop(nofuse=True)
                for t in range(TB):
                    ve.max(top[:, t, :], logit[:, t, :]).then_inc(top_ready.sem, 1)
                ve.wait_ge(top_ready.sem, top_ready.at(r, TB))
                ve.nop(nofuse=True)
                for t in range(TB):
                    ve.max_index(topi[:, t, :], top[:, t, :], logit[:, t, :]).then_inc(topi_ready.sem, 1)
                ve.tensor_tensor(gap[:, :], top[:, :, 1], top[:, :, 0], ALU.subtract).then_inc(gap_ready.sem, 1)
                ve.wait_ge(topi_ready.sem, topi_ready.at(r, TB))
                ve.tensor_copy(topf[:, :, :], topi[:, :, :]).then_inc(gap_ready.sem, 1)

            def combine(r, start=False):
                ve.wait_ge(eg_ready.sem, eg_ready.at(r, 1))
                ve.tensor_scalar(sg[:, :], eg[:, :], 1.0, None, ALU.add).then_inc(wt_steps.sem, 1)
                ve.wait_ge(wt_steps.sem, wt_steps.at(r, 1))
                ve.reciprocal(wt[:, 0, :], sg[:, :]).then_inc(wt_steps.sem, 1)
                ve.wait_ge(wt_steps.sem, wt_steps.at(r, 2))
                ve.tensor_tensor(wt[:, 1, :], wt[:, 0, :], eg[:, :], ALU.mult).then_inc(wt_steps.sem, 1)
                ve.wait_ge(wt_steps.sem, wt_steps.at(r, 3))
                ve.wait_ge(gap_ready.sem, gap_ready.at(r, 2))
                for k, dst in enumerate((first_choice, second_choice)):
                    for t in range(TB):
                        ve.tensor_scalar(dst[:, t, :], iota[:, :], topf[:, t, k:k + 1], wt[:, k, t:t + 1],
                                         ALU.is_equal, ALU.mult).then_inc(chosen.sem, 1)
                ve.wait_ge(chosen.sem, chosen.at(r, 2 * TB))
                if not start:
                    ve.wait_ge(comb_turned.sem, comb_turned.at(r, 0))
                for c in range(3):
                    ve.tensor_tensor(comb3[:, :, 32 * c:32 * c + EXPERTS], first_choice[:, :, :],
                                     second_choice[:, :, :], ALU.add).then_inc(comb_ready.sem, 1)

            def split(r):
                ve.wait_ge(split_steps.sem, split_steps.at(r, 1))
                ve.scalar_tensor_tensor(out=rest_a[:, :], in0=part_a[:, :], scalar=part[0:72, 0:1],
                                        in1=bank[7][0:72, :], op0=ALU.mult, op1=ALU.add).then_inc(split_steps.sem, 1)
                ve.wait_ge(split_steps.sem, split_steps.at(r, 2))
                ve.tensor_copy(part_b[:, :], rest_a[:, :]).then_inc(split_steps.sem, 1)

            def join_parts(r, start=False):
                ve.wait_ge(split_steps.sem, split_steps.at(r, 3))
                if not start:
                    ve.wait_ge(cb_ready.sem, cb_ready.at(r, 0))
                ve.scalar_tensor_tensor(out=combT[:, :], in0=part_b[:, :], scalar=part[0:72, 1:2],
                                        in1=rest_a[:, :], op0=ALU.mult, op1=ALU.add).then_inc(split_steps.sem, 1)

            def hidden(b, j, first):
                ve.wait_ge(silu_ready.sem, silu_ready.at(b, j + 1))
                ve.wait_ge(g_ready.sem, g_ready.at(b, j + 1))
                ve.tensor_tensor(prod[:, j % 2, :], act_h[:, j % 2, :], bank[2 + j % 2][:, :],
                                 ALU.mult).then_inc(prod_ready.sem, 1)
                ve.wait_ge(prod_ready.sem, prod_ready.at(b, j + 1))
                ve.wait_ge(cb_ready.sem, cb_ready.at(b, j + 1))
                if not first or j >= 2:
                    ve.wait_ge(hid_used.sem, hid_used.at(b, j - 1))
                ve.tensor_tensor(hid[:, j % 2, :], prod[:, j % 2, :], bank[4 + j % 2][:, :],
                                 ALU.mult).then_inc(hid_ready.sem, 1)

            def residual(b, q):
                ve.wait_ge(hid_used.sem, hid_used.at(b, ET))
                ve.tensor_tensor(res[:, :], bank[6][:, :], xT[:, tokens(q)], ALU.add).then_inc(res_ready.sem, 1)

            def center(b):
                ve.wait_ge(mean_ready.sem, mean_ready.at(b, 1))
                ve.wait_ge(res_ready.sem, res_ready.at(b, 1))
                ve.tensor_tensor(cen[:, :], res[:, :], bank[7][:, :], ALU.subtract).then_inc(cen_ready.sem, 1)

            def finish(b):
                ve.wait_ge(rstd_ready.sem, rstd_ready.at(b, 1))
                ve.wait_ge(stored.sem, b * 16 + 1)
                ve.tensor_tensor(fin[:, :], cen[:, :], rstd[:, :], ALU.mult).then_inc(fin_ready.sem, 1)

            def body(b, first):
                for j in range(ET):
                    if j == 1:
                        load_x(b + 1, (b + 1) % SEQS)
                    hidden(b, j, first)
                    if j == 0 and not first:
                        residual(b - 1, b - 1)
                    if j == 1:
                        find_two(b + 1)
                    if j == 2 and not first:
                        center(b - 1)
                    if j == 6:
                        combine(b + 1)
                        if not first:
                            finish(b - 1)
                    if j == 9:
                        split(b + 1)
                join_parts(b + 1)

            ve.memset(comb3[:, :, :], 0.0).then_inc(comb_zeroed.sem, 1)
            ve.wait_ge(loaded.sem, 16 * N_LOADS)
            ve.wait_ge(comb_zeroed.sem, 1)
            ve.sem_inc(stored.sem, 1)
            ve.tensor_copy(xm[:, :], xT[:, tokens(0)]).then_inc(xm_ready.sem, 1)
            find_two(0)
            combine(0, True)
            split(0)
            join_parts(0, True)
            body(0, True)
            with ve.Fori(1, SEQS) as b:
                body(b, False)
            residual(SEQS - 1, SEQS - 1)
            center(SEQS - 1)
            finish(SEQS - 1)


def build_program(nc, d, out):
    with ExitStack() as ctx:
        def sb(name, shape):
            return ctx.enter_context(nc.sbuf_tensor(name, shape, F32))

        xT = sb("xT", [P, SEQS * T])
        x0T = sb("x0T", [P, SEQS * T])
        const = {"ident": sb("ident", [P, P]), "mean": sb("mean", [P, P]),
                 "heads": sb("heads", [P, P]),
                 "one": sb("one", [P, 1]), "eps": sb("eps", [P, 1]), "unshift": sb("unshift", [P, 1])}
        with ExitStack() as c2:
            const_loaded = c2.enter_context(nc.semaphore("const_loaded"))
            const_set = c2.enter_context(nc.semaphore("const_set"))
            block = c2.enter_context(nc.Block())

            @block.sync
            def _(sp):
                sp.dma_start(const["ident"][:, :], d["c_ident"]).then_inc(const_loaded, 16)
                sp.dma_start(const["heads"][:, :], d["c_heads"]).then_inc(const_loaded, 16)
                sp.wait_ge(const_loaded, 32)
                sp.wait_ge(const_set, 4)

            @block.vector
            def _(ve):
                ve.memset(const["mean"][:, :], 1.0 / P).then_inc(const_set, 1)
                ve.memset(const["one"][:, :], 1.0).then_inc(const_set, 1)
                ve.memset(const["eps"][:, :], EPS).then_inc(const_set, 1)
                ve.memset(const["unshift"][:, :], 15 * math.log(2.0)).then_inc(const_set, 1)

        def ssm_weights(k):
            return {"pick": d["c_pick"], "part": d["c_part"],
                    **{n: d[f"{k}_{n}"] for n in ("w_in", "w_bc", "w_dlt", "w_dt", "w_out", "chan", "a_log")}}

        held = {}

        def signals(name, per=1):
            if name not in held:
                held[name] = Counter(ctx, nc, "ssm_" + name, per)
            return held[name]

        state_space_phase(nc, "s0_", signals, 0, xT, d["x"], const, ssm_weights("s0"))
        local_attention_phase(nc, "at_", xT, x0T, const,
                              {n: d["at_" + n] for n in ("w_qkv", "w_rot", "w_o", "w1", "w2", "chan_a", "chan", "tables", "mask")})
        layer_norm_phase(nc, "ln_", xT, x0T, const)
        state_space_phase(nc, "s1_", signals, 1, xT, None, const, ssm_weights("s1"))
        expert_phase(nc, "ex_", xT, const,
                     {n: d["ex_" + n] for n in ("wr", "w1", "w3", "w2", "owner", "part", "iota")}, out)


def kernel(**inputs):
    import ml_dtypes
    import numpy as np
    import concourse.bacc as _bacc
    from concourse.bass_utils import run_bass_kernel_spmd as _run

    i = {k: np.asarray(v) for k, v in inputs.items()}
    f = np.float32
    arrays = {"x": i["L0_attn_x"].transpose(2, 0, 1).reshape(P, SEQS * T)}
    pick = np.zeros((96, 32, P), ml_dtypes.bfloat16)
    pick[np.arange(96), np.arange(96) % 32, :] = 1
    rows = np.arange(P)
    arrays["c_part"] = np.stack([np.where(rows >= 32, f(-1), f(0)), np.where(rows >= 64, f(-1), f(0))], 1)
    arrays["c_ident"], arrays["c_pick"] = np.eye(P, dtype=f), pick

    def halves(a):
        return a.reshape(2, P, -1).transpose(1, 0, 2)

    def ssm(k, w_in, w_x, rank, w_dt, taps, conv_b, b_dt, skip, a_log, w_out):
        arrays[k + "w_in"] = w_in
        arrays[k + "w_bc"] = halves(np.tile(w_x[:, rank:], (1, 3)))
        arrays[k + "w_dlt"] = halves(w_x[:, :rank])
        arrays[k + "w_dt"], arrays[k + "w_out"] = w_dt, halves(w_out)
        arrays[k + "chan"] = np.concatenate([halves(taps), halves(conv_b), halves(b_dt), halves(skip)], 2)
        arrays[k + "a_log"] = halves(a_log)

    ssm("s0_", i["L0_attn_W_in"].T, i["L0_attn_W_xproj"].T, 8, i["L0_attn_W_dt"].T, i["L0_attn_W_conv"][:, 0, :],
        np.zeros(256, f), i["L0_attn_b_dt"], i["L0_attn_D"], i["L0_attn_A_log"], i["L0_attn_W_out"].T)
    ssm("s1_", i["L1_attn_W_in"], i["L1_attn_W_x"], 64, i["L1_attn_W_delta"], i["L1_attn_conv_w"][:, 0, :].T,
        i["L1_attn_conv_b"], i["L1_attn_b_delta"], i["L1_attn_D"], i["L1_attn_A_log"], i["L1_attn_W_out"])

    half = np.arange(0, 64, 2, dtype=f)
    t = np.arange(T, dtype=f)
    freqs = t[:, None] * (1.0 / 10000.0 ** (half / 64)).astype(f)[None, :]
    scale = (((half + 0.4 * 64) / (1.4 * 64)).astype(f)[None, :] ** ((t - T // 2) / 16)[:, None]).astype(f)
    cos, sin = np.cos(freqs), np.sin(freqs)

    def both_heads(a, sign):
        return np.concatenate([sign * a, a, sign * a, a], 1).T.astype(f)

    arrays["at_tables"] = np.stack([both_heads(cos * scale, 1), both_heads(sin * scale, -1),
                                    both_heads(cos / scale, 1), both_heads(sin / scale, -1)], 1)
    qi, kc = np.arange(P)[:, None] % 64, np.arange(96)[None, :]
    band = np.where((kc >= qi) & (kc <= qi + 32), f(0), f(-1e30))
    first = np.where(kc >= 32, band, f(-1e30))
    arrays["at_mask"] = np.concatenate([first] + [band] * 7, 1).reshape(P, 2, 4 * 96).astype(f)
    arrays["c_heads"] = np.kron(np.eye(2, dtype=f), np.ones((64, 64), f))
    arrays["at_w_qkv"] = i["L0_ffn_Wqkv"]
    arrays["at_w_rot"] = i["L0_ffn_Wqkv"][:, :, :2048].reshape(6, P, 32, 2, 32)[:, :, :, ::-1].reshape(6, P, 2048)
    arrays["at_w_o"] = i["L0_ffn_Wo"].reshape(6, 8, P, P).transpose(0, 2, 1, 3)
    arrays["at_w1"] = i["L0_ffn_W1"]
    hid = 114

    def hidden(a):
        a = np.concatenate([a, a[:, :1]], 1)
        return a.reshape(6, 3, hid, -1).transpose(0, 2, 1, 3)

    def per_channel(a):
        return np.stack([np.tile(a, 2), np.tile(np.roll(a, 32, 1), 2)], 2)

    arrays["at_w2"] = hidden(i["L0_ffn_W2"])
    b1 = i["L0_ffn_b1"][:, :, None]
    b1 = np.concatenate([hidden(b1[:, :341])[..., 0], hidden(b1[:, 341:])[..., 0]], 2)
    b1 = np.concatenate([b1, b1[:, :P - hid]], 1)
    arrays["at_chan_a"] = np.concatenate([per_channel(i["L0_ffn_q_scale"]), per_channel(i["L0_ffn_k_scale"])], 2)
    arrays["at_chan"] = np.concatenate(
        [np.stack([i["L0_ffn_ln_g"], i["L0_ffn_ln_b"], i["L0_ffn_b2"]], 2), b1], 2)

    arrays["ex_wr"] = i["L1_ffn_Wr"]
    arrays["ex_w1"] = i["L1_ffn_W1"].transpose(1, 0, 2).reshape(P, -1)
    arrays["ex_w3"] = i["L1_ffn_W3"].transpose(1, 0, 2).reshape(P, -1)
    arrays["ex_w2"] = i["L1_ffn_W2"].reshape(12, P, P).transpose(1, 0, 2)
    owner = np.zeros((72, 12 * P), ml_dtypes.bfloat16)
    for r in range(3):
        for e in range(8):
            owner[32 * r + e, 192 * e:192 * (e + 1)] = 1
    arrays["ex_owner"] = owner.reshape(72, 12, P)
    arrays["ex_part"] = arrays["c_part"]
    arrays["ex_iota"] = np.tile(np.arange(8, dtype=f), (P, 1))

    nc = _bacc.Bacc("TRN2", target_bir_lowering=False, num_devices=1)
    arrays = {k: np.ascontiguousarray(v) for k, v in arrays.items()}
    d = {k: nc.dram_tensor("in_" + k, v.shape, mybir.dt.from_np(v.dtype), kind="ExternalInput").ap()
         for k, v in arrays.items()}
    out = nc.dram_tensor("out", (P, SEQS * T), F32, kind="ExternalOutput").ap()
    build_program(nc, d, out)
    r = _run(nc, [{"in_" + k: v for k, v in arrays.items()}], core_ids=[0])
    return np.ascontiguousarray(r.results[0]["out"].reshape(P, SEQS, T).transpose(1, 2, 0))
```
